# Optimizing a Trainium2 kernel written in Bass

```python
import numpy as np
import jax
import jax.numpy as jnp

def _softmax(x, axis=-1):
    return jax.nn.softmax(x, axis=axis)

def _gelu(x):
    return jax.nn.gelu(x, approximate=True)

def _silu(x):
    return jax.nn.silu(x)

def _sigmoid(x):
    return jax.nn.sigmoid(x)

def _layernorm(x, axis=-1, eps=1e-05):
    m = jnp.mean(x, axis=axis, keepdims=True)
    v = jnp.var(x, axis=axis, keepdims=True)
    return (x - m) / jnp.sqrt(v + eps)

def _scatter_add(tgt, idx, src, axis=0):
    return tgt.at[idx].add(src)

def _segment_sum(src, seg, n):
    return jax.ops.segment_sum(src, seg, n)
kernel_name = 'mk_perceiver_d2_seqx_r8_9fe096'

def setup_inputs(seed: int=0):
    np.random.seed(seed)
    _w = jnp.asarray

    def _rec_inputs():
        import jax
        import jax.numpy as jnp
        _rk = jax.random.key(seed)
        x = -0.0005207 + 1.001 * jax.random.normal(jax.random.fold_in(_rk, 1), (32, 64, 512), jnp.float32)
        _lenS = 64 - jax.random.randint(jax.random.fold_in(_rk, 7), (32,), 0, max(1, 64 // 4) + 1, jnp.int32)
        _lenS2 = 128 - jax.random.randint(jax.random.fold_in(_rk, 8), (32,), 0, max(1, 128 // 4) + 1, jnp.int32)
        _ctx_4096P = jax.random.normal(jax.random.fold_in(_rk, 11), (32, 16, 512), jnp.float32)
        _ctx_4096c = jax.random.dirichlet(jax.random.fold_in(_rk, 511), 0.3 * jnp.ones((16,), jnp.float32), (32, 128))
        _ctx_4096t = jnp.einsum('bsk,bkd->bsd', _ctx_4096c, _ctx_4096P)
        _ctx_4096t = _ctx_4096t * jax.lax.rsqrt(jnp.mean(jnp.square(_ctx_4096t)) + 1e-12) * 0.953939
        ctx_4096 = -0.00010331 + 0.999899 * (_ctx_4096t + 0.3 * jax.random.normal(jax.random.fold_in(_rk, 611), (32, 128, 512), jnp.float32))
        return (x, ctx_4096)
    x, ctx_4096 = _rec_inputs()

    def _L0_xattn_setup():
        import jax, jax.numpy as jnp
        import numpy as np
        B, Q, D = (8, 64, 512)
        CTX = 512
        H, KV, HD = (16, 4, 96)
        G = H // KV
        key = jax.random.key(seed)
        ks = jax.random.split(key, 6)
        s = 0.02
        return {'latents': jax.random.normal(ks[0], (B, Q, D), jnp.float32), 'context': jax.random.normal(ks[1], (B, CTX, D), jnp.float32), 'Wq': jax.random.normal(ks[2], (H * HD, D), jnp.float32) * s, 'Wk': jax.random.normal(ks[3], (KV * HD, D), jnp.float32) * s, 'Wv': jax.random.normal(ks[4], (KV * HD, D), jnp.float32) * s, 'Wo': jax.random.normal(ks[5], (D, H * HD), jnp.float32) * s}
    _L0_xattn_all = _L0_xattn_setup()
    _L0_xattn_in = {k: v for k, v in _L0_xattn_all.items() if k in ('Wq', 'Wk', 'Wv', 'Wo')}
    del _L0_xattn_all

    def _L0_attn_setup():
        import jax, jax.numpy as jnp
        import numpy as np
        import math
        B, L, D, H = (32, 64, 512, 32)
        HD = D // H
        key = jax.random.key(seed)
        ks = jax.random.split(key, 9)
        s = 1.0 / math.sqrt(D)
        return {'x': jax.random.normal(ks[0], (B, L, D), jnp.float32), 'Wq': jax.random.normal(ks[1], (D, D), jnp.float32) * s, 'bq': jax.random.normal(ks[2], (D,), jnp.float32) * s, 'Wk': jax.random.normal(ks[3], (D, D), jnp.float32) * s, 'bk': jax.random.normal(ks[4], (D,), jnp.float32) * s, 'Wv': jax.random.normal(ks[5], (D, D), jnp.float32) * s, 'bv': jax.random.normal(ks[6], (D,), jnp.float32) * s, 'Wo': jax.random.normal(ks[7], (D, D), jnp.float32) * s, 'bo': jax.random.normal(ks[8], (D,), jnp.float32) * s}
    _L0_attn_all = _L0_attn_setup()
    _L0_attn_in = {k: v for k, v in _L0_attn_all.items() if k in ('Wq', 'bq', 'Wk', 'bk', 'Wv', 'bv', 'Wo', 'bo')}
    del _L0_attn_all

    def _L0_ffn_setup():
        import jax, jax.numpy as jnp
        import numpy as np
        HID, INT, LAT, NE, K = (512, 1024, 256, 8, 2)
        LN_EPS = 1e-05

        def _layernorm(x, gamma, beta):
            mu = jnp.mean(x, axis=-1, keepdims=True)
            var = jnp.var(x, axis=-1, keepdims=True)
            return (x - mu) * jax.lax.rsqrt(var + LN_EPS) * gamma + beta
        key = jax.random.key(seed)
        ks = jax.random.split(key, 8)
        s = lambda d: 1.0 / np.sqrt(d)
        return {'hidden_states': jax.random.normal(ks[0], (4, 256, HID), jnp.float32), 'gate_w': jax.random.normal(ks[1], (HID, NE), jnp.float32) * s(HID), 'up_w': jax.random.normal(ks[2], (HID, INT), jnp.float32) * s(HID), 'down_w': jax.random.normal(ks[3], (INT, HID), jnp.float32) * s(INT), 'fc1_w': jax.random.normal(ks[4], (HID, LAT), jnp.float32) * s(HID), 'fc2_w': jax.random.normal(ks[5], (LAT, HID), jnp.float32) * s(LAT), 'expert_w': jax.random.normal(ks[6], (LAT, LAT), jnp.float32), 'ln_gamma': jnp.ones((HID,), jnp.float32), 'ln_beta': jnp.zeros((HID,), jnp.float32)}
    _L0_ffn_all = _L0_ffn_setup()
    _L0_ffn_in = {k: v for k, v in _L0_ffn_all.items() if k in ('gate_w', 'up_w', 'down_w', 'fc1_w', 'fc2_w', 'expert_w', 'ln_gamma', 'ln_beta')}
    del _L0_ffn_all

    def _L1_xattn_setup():
        import jax, jax.numpy as jnp
        import numpy as np
        import math
        HIDDEN = 512
        N_HEADS = 32
        HEAD_DIM = 128
        N_KV_HEADS = 4
        N_GROUPS = N_HEADS // N_KV_HEADS
        key = jax.random.key(seed)
        ks = jax.random.split(key, 6)
        B, NL, S = (8, 64, 512)
        latents = jax.random.normal(ks[0], (B, NL, HIDDEN), dtype=jnp.float32)
        context = jax.random.normal(ks[1], (B, S, HIDDEN), dtype=jnp.float32)
        scale = 1.0 / math.sqrt(HIDDEN)
        Wq = jax.random.normal(ks[2], (HIDDEN, N_HEADS * HEAD_DIM), dtype=jnp.float32) * scale
        Wk = jax.random.normal(ks[3], (HIDDEN, N_KV_HEADS * HEAD_DIM), dtype=jnp.float32) * scale
        Wv = jax.random.normal(ks[4], (HIDDEN, N_KV_HEADS * HEAD_DIM), dtype=jnp.float32) * scale
        Wo = jax.random.normal(ks[5], (N_HEADS * HEAD_DIM, HIDDEN), dtype=jnp.float32) * scale
        return {'latents': latents, 'context': context, 'Wq': Wq, 'Wk': Wk, 'Wv': Wv, 'Wo': Wo}
    _L1_xattn_all = _L1_xattn_setup()
    _L1_xattn_in = {k: v for k, v in _L1_xattn_all.items() if k in ('Wq', 'Wk', 'Wv', 'Wo')}
    del _L1_xattn_all

    def _L1_attn_setup():
        import math
        import jax, jax.numpy as jnp
        import numpy as np
        D_MODEL = 512
        N_HEADS = 32
        N_KV_HEADS = 8
        D_HEAD = D_MODEL // N_HEADS
        GROUP = N_HEADS // N_KV_HEADS
        ROPE = dict(rope_theta=500000.0, factor=32.0, hi_freq_factor=4.0, lo_freq_factor=1.0, original_context_length=1024)

        def _rope_cos_sin(head_dim, pos, dtype):
            idx = jnp.arange(0, head_dim, 2, dtype=jnp.float32) / head_dim
            freq = 1.0 / (2.0 * math.pi) * ROPE['rope_theta'] ** (-idx)
            factor, lo, hi = (ROPE['factor'], ROPE['lo_freq_factor'], ROPE['hi_freq_factor'])
            L0 = ROPE['original_context_length']
            freq_low, freq_high = (lo / L0, hi / L0)
            freq_scaled = jnp.where(freq < freq_low, freq / factor, freq)
            smooth = jnp.clip((L0 * freq - lo) / (hi - lo), 0.0, 1.0)
            freq_smooth = (1.0 - smooth) * (freq / factor) + smooth * freq
            is_mid = (freq >= freq_low) & (freq <= freq_high)
            freq = jnp.where(is_mid, freq_smooth, freq_scaled)
            phase = 2.0 * math.pi * pos.astype(jnp.float32)[:, None] * freq[None, :]
            emb = jnp.concatenate([phase, phase], axis=-1)
            return (jnp.cos(emb).astype(dtype), jnp.sin(emb).astype(dtype))

        def _rotate_half(x):
            h = x.shape[-1] // 2
            return jnp.concatenate([-x[..., h:], x[..., :h]], axis=-1)
        key = jax.random.key(seed)
        ks = jax.random.split(key, 5)
        B, T = (1, 256)
        s = 0.02
        return {'resid': jax.random.normal(ks[0], (B, T, D_MODEL), jnp.float32), 'Wq': jax.random.normal(ks[1], (D_MODEL, D_MODEL), jnp.float32) * s, 'Wk': jax.random.normal(ks[2], (D_MODEL, N_KV_HEADS * D_HEAD), jnp.float32) * s, 'Wv': jax.random.normal(ks[3], (D_MODEL, N_KV_HEADS * D_HEAD), jnp.float32) * s, 'Wo': jax.random.normal(ks[4], (D_MODEL, D_MODEL), jnp.float32) * s}
    _L1_attn_all = _L1_attn_setup()
    _L1_attn_in = {k: v for k, v in _L1_attn_all.items() if k in ('Wq', 'Wk', 'Wv', 'Wo')}
    del _L1_attn_all

    def _L1_ffn_setup():
        import jax, jax.numpy as jnp
        import numpy as np
        EPS = 1e-05

        def rms_norm(x):
            return x * jax.lax.rsqrt(jnp.mean(x * x, axis=-1, keepdims=True) + EPS)

        def activation_quant(x):
            scale = 127.0 / jnp.clip(jnp.max(jnp.abs(x), axis=-1, keepdims=True), EPS, None)
            return jnp.clip(jnp.round(x * scale), -128.0, 127.0) / scale

        def weight_quant(w):
            scale = 1.0 / jnp.clip(jnp.mean(jnp.abs(w)), EPS, None)
            return jnp.clip(jnp.round(w * scale), -1.0, 1.0) / scale
        key = jax.random.key(seed)
        k1, k2, k3 = jax.random.split(key, 3)
        B, S, D = (4, 256, 512)
        x = jax.random.normal(k1, (B, S, D), dtype=jnp.float32)
        W = jax.random.normal(k2, (D, D), dtype=jnp.float32) * (1.0 / np.sqrt(D))
        b = jax.random.normal(k3, (D,), dtype=jnp.float32) * 0.02
        return {'x': x, 'W': W, 'b': b}
    _L1_ffn_all = _L1_ffn_setup()
    _L1_ffn_in = {k: v for k, v in _L1_ffn_all.items() if k in ('W', 'b')}
    del _L1_ffn_all
    return {'x': x, 'ctx_4096': ctx_4096, 'L0_xattn_Wq': _L0_xattn_in['Wq'], 'L0_xattn_Wk': _L0_xattn_in['Wk'], 'L0_xattn_Wv': _L0_xattn_in['Wv'], 'L0_xattn_Wo': _L0_xattn_in['Wo'], 'L0_attn_Wq': _L0_attn_in['Wq'], 'L0_attn_bq': _L0_attn_in['bq'], 'L0_attn_Wk': _L0_attn_in['Wk'], 'L0_attn_bk': _L0_attn_in['bk'], 'L0_attn_Wv': _L0_attn_in['Wv'], 'L0_attn_bv': _L0_attn_in['bv'], 'L0_attn_Wo': _L0_attn_in['Wo'], 'L0_attn_bo': _L0_attn_in['bo'], 'L0_ffn_gate_w': _L0_ffn_in['gate_w'], 'L0_ffn_up_w': _L0_ffn_in['up_w'], 'L0_ffn_down_w': _L0_ffn_in['down_w'], 'L0_ffn_fc1_w': _L0_ffn_in['fc1_w'], 'L0_ffn_fc2_w': _L0_ffn_in['fc2_w'], 'L0_ffn_expert_w': _L0_ffn_in['expert_w'], 'L0_ffn_ln_gamma': _L0_ffn_in['ln_gamma'], 'L0_ffn_ln_beta': _L0_ffn_in['ln_beta'], 'L1_xattn_Wq': _L1_xattn_in['Wq'], 'L1_xattn_Wk': _L1_xattn_in['Wk'], 'L1_xattn_Wv': _L1_xattn_in['Wv'], 'L1_xattn_Wo': _L1_xattn_in['Wo'], 'L1_attn_Wq': _L1_attn_in['Wq'], 'L1_attn_Wk': _L1_attn_in['Wk'], 'L1_attn_Wv': _L1_attn_in['Wv'], 'L1_attn_Wo': _L1_attn_in['Wo'], 'L1_ffn_W': _L1_ffn_in['W'], 'L1_ffn_b': _L1_ffn_in['b']}

def reference(x, ctx_4096, L0_xattn_Wq, L0_xattn_Wk, L0_xattn_Wv, L0_xattn_Wo, L0_attn_Wq, L0_attn_bq, L0_attn_Wk, L0_attn_bk, L0_attn_Wv, L0_attn_bv, L0_attn_Wo, L0_attn_bo, L0_ffn_gate_w, L0_ffn_up_w, L0_ffn_down_w, L0_ffn_fc1_w, L0_ffn_fc2_w, L0_ffn_expert_w, L0_ffn_ln_gamma, L0_ffn_ln_beta, L1_xattn_Wq, L1_xattn_Wk, L1_xattn_Wv, L1_xattn_Wo, L1_attn_Wq, L1_attn_Wk, L1_attn_Wv, L1_attn_Wo, L1_ffn_W, L1_ffn_b):
    import jax
    import jax.numpy as jnp

    def _L0_xattn_ref(latents, context, Wq, Wk, Wv, Wo):
        import jax, jax.numpy as jnp
        import numpy as np
        B, Q, D = (8, 64, 512)
        CTX = 512
        H, KV, HD = (16, 4, 96)
        G = H // KV
        b, q_len, _ = latents.shape
        hidden = jnp.concatenate([context, latents], axis=1)
        s_len = hidden.shape[1]
        q = (latents @ Wq.T).reshape(b, q_len, H, HD)
        k = (hidden @ Wk.T).reshape(b, s_len, KV, HD)
        v = (hidden @ Wv.T).reshape(b, s_len, KV, HD)
        q = q.transpose(0, 2, 1, 3).reshape(b, KV, G, q_len, HD)
        k = k.transpose(0, 2, 1, 3)
        v = v.transpose(0, 2, 1, 3)
        scale = 1.0 / jnp.sqrt(jnp.asarray(HD, q.dtype))
        scores = jnp.einsum('bkgqd,bksd->bkgqs', q, k) * scale
        attn = jax.nn.softmax(scores.astype(jnp.float32), axis=-1).astype(q.dtype)
        out = jnp.einsum('bkgqs,bksd->bkgqd', attn, v)
        out = out.reshape(b, H, q_len, HD).transpose(0, 2, 1, 3).reshape(b, q_len, H * HD)
        return out @ Wo.T

    def _L0_attn_ref(x, Wq, bq, Wk, bk, Wv, bv, Wo, bo):
        import jax, jax.numpy as jnp
        import numpy as np
        import math
        B, L, D, H = (32, 64, 512, 32)
        HD = D // H
        b, l, d = x.shape
        h, hd = (H, HD)
        q = (x @ Wq.T + bq).reshape(b, l, h, hd).transpose(0, 2, 1, 3)
        k = (x @ Wk.T + bk).reshape(b, l, h, hd).transpose(0, 2, 1, 3)
        v = (x @ Wv.T + bv).reshape(b, l, h, hd).transpose(0, 2, 1, 3)
        scores = jnp.einsum('bhqd,bhkd->bhqk', q, k) / math.sqrt(hd)
        causal = jnp.tril(jnp.ones((l, l), bool))
        scores = jnp.where(causal, scores, -jnp.inf)
        att = jax.nn.softmax(scores, axis=-1)
        out = jnp.einsum('bhqk,bhkd->bhqd', att, v)
        out = out.transpose(0, 2, 1, 3).reshape(b, l, d)
        return out @ Wo.T + bo

    def _L0_ffn_ref(hidden_states, gate_w, up_w, down_w, fc1_w, fc2_w, expert_w, ln_gamma, ln_beta):
        import jax, jax.numpy as jnp
        import numpy as np
        HID, INT, LAT, NE, K = (512, 1024, 256, 8, 2)
        LN_EPS = 1e-05

        def _layernorm(x, gamma, beta):
            mu = jnp.mean(x, axis=-1, keepdims=True)
            var = jnp.var(x, axis=-1, keepdims=True)
            return (x - mu) * jax.lax.rsqrt(var + LN_EPS) * gamma + beta
        logits = jnp.einsum('bsh,he->bse', hidden_states, gate_w)
        routing_weights, selected_experts = jax.lax.top_k(logits, K)
        h = jax.nn.relu(jnp.einsum('bsh,hi->bsi', hidden_states, up_w)) ** 2
        shared_out = jnp.einsum('bsi,ih->bsh', h, down_w)
        x_latent = jnp.einsum('bsh,hl->bsl', hidden_states, fc1_w)
        expert_out = jnp.einsum('bsl,lm->bsm', x_latent, expert_w)
        moe_out = expert_out * jnp.sum(routing_weights, axis=-1, keepdims=True)
        routed_out = jnp.einsum('bsl,lh->bsh', moe_out, fc2_w)
        return _layernorm(shared_out + routed_out, ln_gamma, ln_beta)

    def _L1_xattn_ref(latents, context, Wq, Wk, Wv, Wo):
        import jax, jax.numpy as jnp
        import numpy as np
        import math
        HIDDEN = 512
        N_HEADS = 32
        HEAD_DIM = 128
        N_KV_HEADS = 4
        N_GROUPS = N_HEADS // N_KV_HEADS
        b, q_len, _ = latents.shape
        kv_len = q_len + context.shape[1]
        hidden_states = jnp.concatenate([context, latents], axis=1)
        q = (latents @ Wq).reshape(b, q_len, N_KV_HEADS, N_GROUPS, HEAD_DIM)
        k = (hidden_states @ Wk).reshape(b, kv_len, N_KV_HEADS, HEAD_DIM)
        v = (hidden_states @ Wv).reshape(b, kv_len, N_KV_HEADS, HEAD_DIM)
        scale = 1.0 / math.sqrt(HEAD_DIM)
        scores = jnp.einsum('bqhgd,bkhd->bhgqk', q, k) * scale
        attn = jax.nn.softmax(scores.astype(jnp.float32), axis=-1).astype(q.dtype)
        out = jnp.einsum('bhgqk,bkhd->bqhgd', attn, v)
        out = out.reshape(b, q_len, N_HEADS * HEAD_DIM)
        return out @ Wo

    def _L1_attn_ref(resid, Wq, Wk, Wv, Wo):
        import math
        import jax, jax.numpy as jnp
        import numpy as np
        D_MODEL = 512
        N_HEADS = 32
        N_KV_HEADS = 8
        D_HEAD = D_MODEL // N_HEADS
        GROUP = N_HEADS // N_KV_HEADS
        ROPE = dict(rope_theta=500000.0, factor=32.0, hi_freq_factor=4.0, lo_freq_factor=1.0, original_context_length=1024)

        def _rope_cos_sin(head_dim, pos, dtype):
            idx = jnp.arange(0, head_dim, 2, dtype=jnp.float32) / head_dim
            freq = 1.0 / (2.0 * math.pi) * ROPE['rope_theta'] ** (-idx)
            factor, lo, hi = (ROPE['factor'], ROPE['lo_freq_factor'], ROPE['hi_freq_factor'])
            L0 = ROPE['original_context_length']
            freq_low, freq_high = (lo / L0, hi / L0)
            freq_scaled = jnp.where(freq < freq_low, freq / factor, freq)
            smooth = jnp.clip((L0 * freq - lo) / (hi - lo), 0.0, 1.0)
            freq_smooth = (1.0 - smooth) * (freq / factor) + smooth * freq
            is_mid = (freq >= freq_low) & (freq <= freq_high)
            freq = jnp.where(is_mid, freq_smooth, freq_scaled)
            phase = 2.0 * math.pi * pos.astype(jnp.float32)[:, None] * freq[None, :]
            emb = jnp.concatenate([phase, phase], axis=-1)
            return (jnp.cos(emb).astype(dtype), jnp.sin(emb).astype(dtype))

        def _rotate_half(x):
            h = x.shape[-1] // 2
            return jnp.concatenate([-x[..., h:], x[..., :h]], axis=-1)
        B, T, _ = resid.shape
        q = (resid @ Wq).reshape(B, T, N_HEADS, D_HEAD).transpose(0, 2, 1, 3)
        k = (resid @ Wk).reshape(B, T, N_KV_HEADS, D_HEAD).transpose(0, 2, 1, 3)
        v = (resid @ Wv).reshape(B, T, N_KV_HEADS, D_HEAD).transpose(0, 2, 1, 3)
        cos, sin = _rope_cos_sin(D_HEAD, jnp.arange(T), resid.dtype)
        cos = cos[None, None]
        sin = sin[None, None]
        q = q * cos + _rotate_half(q) * sin
        k = k * cos + _rotate_half(k) * sin
        qg = q.reshape(B, N_KV_HEADS, GROUP, T, D_HEAD)
        att = jnp.einsum('bhgqd,bhkd->bhgqk', qg.astype(jnp.float32), k.astype(jnp.float32)) / math.sqrt(D_HEAD)
        causal = jnp.tril(jnp.ones((T, T), dtype=bool))
        att = jnp.where(causal[None, None, None], att, -jnp.inf)
        probs = jax.nn.softmax(att, axis=-1).astype(resid.dtype)
        ctx = jnp.einsum('bhgqk,bhkd->bhgqd', probs, v)
        out = ctx.reshape(B, N_HEADS, T, D_HEAD).transpose(0, 2, 1, 3).reshape(B, T, D_MODEL)
        return out @ Wo

    def _L1_ffn_ref(x, W, b):
        import jax, jax.numpy as jnp
        import numpy as np
        EPS = 1e-05

        def rms_norm(x):
            return x * jax.lax.rsqrt(jnp.mean(x * x, axis=-1, keepdims=True) + EPS)

        def activation_quant(x):
            scale = 127.0 / jnp.clip(jnp.max(jnp.abs(x), axis=-1, keepdims=True), EPS, None)
            return jnp.clip(jnp.round(x * scale), -128.0, 127.0) / scale

        def weight_quant(w):
            scale = 1.0 / jnp.clip(jnp.mean(jnp.abs(w)), EPS, None)
            return jnp.clip(jnp.round(w * scale), -1.0, 1.0) / scale
        xn = rms_norm(x)
        xq = xn + jax.lax.stop_gradient(activation_quant(xn) - xn)
        wq = W + jax.lax.stop_gradient(weight_quant(W) - W)
        y = jnp.einsum('bsd,od->bso', xq, wq) + b
        return x + jax.nn.gelu(y, approximate=False)
    x = x + _L0_xattn_ref(_layernorm(x, axis=-1), ctx_4096, L0_xattn_Wq, L0_xattn_Wk, L0_xattn_Wv, L0_xattn_Wo)
    x = x + _L0_attn_ref(_layernorm(x, axis=-1), L0_attn_Wq, L0_attn_bq, L0_attn_Wk, L0_attn_bk, L0_attn_Wv, L0_attn_bv, L0_attn_Wo, L0_attn_bo)
    x = x + _L0_ffn_ref(_layernorm(x, axis=-1), L0_ffn_gate_w, L0_ffn_up_w, L0_ffn_down_w, L0_ffn_fc1_w, L0_ffn_fc2_w, L0_ffn_expert_w, L0_ffn_ln_gamma, L0_ffn_ln_beta)
    x = x + _L1_xattn_ref(_layernorm(x, axis=-1), ctx_4096, L1_xattn_Wq, L1_xattn_Wk, L1_xattn_Wv, L1_xattn_Wo)
    x = x + _L1_attn_ref(_layernorm(x, axis=-1), L1_attn_Wq, L1_attn_Wk, L1_attn_Wv, L1_attn_Wo)
    x = x + _L1_ffn_ref(_layernorm(x, axis=-1), L1_ffn_W, L1_ffn_b)
    return x

_drawn_inputs = setup_inputs


def setup_inputs(seed=0):
    import zlib

    import numpy as np

    out = dict(_drawn_inputs(seed))
    spreads = {'L0_ffn_ln_gamma': (1.0, 0.2), 'L0_ffn_ln_beta': (0.0, 0.1)}
    factors = {'L0_xattn_Wq': 4.202,
     'L0_xattn_Wk': 4.116,
     'L0_attn_bq': 5.308,
     'L0_attn_bk': 8.0,
     'L1_attn_Wq': 8.0,
     'L1_attn_Wk': 8.0,
     'L1_ffn_b': 8.0}
    for name, (base, spread) in spreads.items():
        noise = np.random.default_rng([zlib.crc32(name.encode()), seed]).standard_normal(out[name].shape)
        drawn = base * np.exp(spread * noise) if base else spread * noise
        out[name] = jnp.asarray(drawn.astype(out[name].dtype))
    for name, factor in factors.items():
        out[name] = (out[name] * factor).astype(out[name].dtype)
    return out
```

```python
from contextlib import ExitStack

import numpy as np

import concourse.bass as bass
from concourse import mybir

F32 = mybir.dt.float32
BF16 = mybir.dt.bfloat16
ALU = mybir.AluOpType
ACT = mybir.ActivationFunctionType
AX = mybir.AxisListType

P = 128
B, L, D = 32, 64, 512
S = 128
KC = D // P
NT = B * L // P
GB = 4
GT = GB * L // P
NG = B // GB
KV = 4
KEYS = S + L
EPS = 1e-5
HI, LO = 0, 1
PASSES = ((HI, HI), (HI, LO), (LO, HI))
PREP_T = 4


class Cross:

    def __init__(self, name, heads, hd):
        self.name, self.hd = name, hd
        self.nh = heads // KV
        self.pairs = self.nh // 2
        self.sbanks = self.pairs // 2
        self.scale = float(hd) ** -0.5
        self.fills = [("q", n) for n in range(self.nh // 2)] + [("kc", 0), ("kl", 0), ("vc", 0), ("vl", 0)]
        self.nf = len(self.fills)
        if self.nh * hd * KC > 2048:
            self.chunks = [("wq", 0, 2), ("wq", 2, 2), ("wk", 0, KC), ("wv", 0, KC),
                           ("wo", 0, self.nh // 2), ("wo", self.nh // 2, self.nh // 2)]
        else:
            self.chunks = [("wq", 0, KC), ("wk", 0, KC), ("wv", 0, KC), ("wo", 0, self.nh)]


class Self:

    def __init__(self, name, rope):
        self.name, self.rope = name, rope
        self.kvc = 1 if rope else KC
        if rope:
            self.fills = [("q", 0), ("r", 0), ("q", 1), ("r", 1), ("k", 0), ("r", 2), ("v", 0), ("v", 1)]
            self.chunks = [("wq", 0, KC), ("wk", 0, KC), ("wv", 0, KC), ("wo", 0, KC)]
        else:
            self.fills = [("q", 0), ("q", 1), ("k", 0), ("k", 1), ("v", 0), ("v", 1)]
            self.chunks = [("wq", 0, KC), ("wk", 0, KC), ("wv", 0, KC), ("wo", 0, KC), ("bv", 0, 1), ("bo", 0, 1)]
        self.nf = len(self.fills)
        self.nrope = 3 if rope else 0


class Ffn:
    hidden, lat, experts = 1024, 256, 8
    fills = [("f", 0), ("u", 0), ("u", 1), ("u", 2), ("u", 3), ("e", 0), ("g", 0), ("g", 1)]
    nf = len(fills)
    chunks = [("up", 0, 2), ("up", 2, 2), ("fc1", 0, KC), ("gate", 0, KC), ("expert", 0, 2),
              ("fc2", 0, 2), ("down", 0, 4), ("down", 4, 4)]


A0 = Self("L0_attn", False)
A1 = Self("L1_attn", True)
F0 = Ffn()
HPC = 8
HD = 16
UNITS = 2 * GB
ROUND = 1.5 * 2.0 ** 23
X0 = Cross("L0_xattn", 16, 96)
X1 = Cross("L1_xattn", 32, 128)


def build(nc, a, out, layers=6):
    ctx = ExitStack()
    with ctx:
        def sb(name, shape, dt):
            return ctx.enter_context(nc.sbuf_tensor(name, shape, dt))

        def sem(name):
            return ctx.enter_context(nc.semaphore(name))

        bank = [ctx.enter_context(nc.psum_tensor(f"bank{i}", [P, 512], F32)) for i in range(8)]
        proj_ps, score_ps, turn_ps, pv_ps, out_ps = bank[0:2], bank[2:4], bank[4:6], bank[6], bank[7]

        scratch = nc.dram_tensor("xn_scratch", (NT, P, 2, KC, P), BF16).ap()

        X = sb("X", [P, NT, D], F32)
        identf = sb("identf", [P, P], F32)
        neghalf = sb("neghalf", [P, PREP_T], F32)
        credit = sb("credit", [P, 8], F32)
        carrier = sb("carrier", [P, 8], F32)
        scales = sb("scales", [P, 4], F32)
        stats = sb("stats", [P, PREP_T, 6], F32)
        meanvar = sb("meanvar", [P, PREP_T, 2], F32)
        vareps = sb("vareps", [P, PREP_T], F32)
        rstd = sb("rstd", [P, PREP_T], F32)
        xn = sb("xn", [P, PREP_T, D], F32)
        xt = sb("xt", [P, 2, 2, KC, P], BF16)
        wstage = sb("wstage", [P, 2, 2048], F32)
        xg = sb("xg", [P, 2, GT, 2, KC, P], BF16)
        consts = sb("consts", [P, 8 + 64 + 128 + 64 + 64], F32)
        hmask, cmask, perm = consts[:, 0:8], consts[:, 8:72], consts[:, 72:200]
        cos, sin = consts[:, 200:264], consts[:, 264:328]
        row0 = sb("row0", [P, P], BF16)
        identb = sb("identb", [P, P], BF16)
        bqk = sb("bqk", [P, 2, KC], F32)

        ARENA = 70144
        arena = sb("arena", [P, ARENA], BF16)

        class Carve:
            def __init__(self):
                self.at = 0

            def __call__(self, shape, dt):
                n = int(np.prod(shape)) * (2 if dt == F32 else 1)
                ap = arena[:, self.at:self.at + n]
                self.at += n
                assert self.at <= ARENA, self.at
                if dt == F32:
                    ap = ap.bitcast(F32)
                if len(shape) > 1:
                    names = "abcdefg"[:len(shape)]
                    ap = ap.rearrange("p (" + " ".join(names) + ") -> p " + " ".join(names),
                                      **{k: v for k, v in zip(names[1:], shape[1:])})
                return ap

        cv = Carve()
        wq = cv([2, KC * 1024], BF16)
        wk = cv([2, KC * P], BF16)
        wv = cv([2, KC * P], BF16)
        wo = cv([2, 8 * D], BF16)
        cstage = cv([KC, GB * S], F32)
        cT = cv([2, 2, KC, GB * S], BF16)
        q = cv([2, 2, GB * 8 * L], BF16)
        kT = cv([2, 2, GB, KEYS], BF16)
        v = cv([2, 2, (GB + GT) * P], BF16)
        negmax = cv([4], F32)
        nbias = cv([4], F32)
        rowsum = cv([4], F32)
        rinv = cv([4], F32)
        probs = cv([4, KEYS], F32)
        pT1 = cv([2, 512], BF16)
        pT2 = cv([2, 2, 512], BF16)
        att = cv([2, 8 * P], BF16)

        cv = Carve()
        sw = {n: cv([2, KC, D], BF16) for n in ("wq", "wk", "wv", "wo")}
        sw.update({n: cv([2, 1, D], BF16) for n in ("bv", "bo")})
        vx_at = cv.at
        vx = cv([2, 2, 2, KC, 4, P], BF16)
        qm = cv([2, 2, KC, 2, HPC, L], BF16)
        sq = cv([2, 2, KC, GT * P], BF16)
        sk = cv([2, 2, KC, GT * P], BF16)
        sv = cv([2, GT, D], BF16)
        sc = cv([2, HPC, L], F32)
        spT = cv([2, 2, 512], BF16)
        satt = cv([2, KC, P], BF16)
        smax, ssum, sinv = cv([2, 8], F32), cv([2, 8], F32), cv([2, 8], F32)
        raw32, rt1 = cv([512], F32), cv([512], F32)
        rt2 = cv([512], F32)
        cv = Carve()
        fw = {"up": cv([2, KC, Ffn.hidden], BF16), "fc1": cv([2, KC, Ffn.lat], BF16),
              "gate": cv([2, KC, Ffn.experts], BF16), "expert": cv([2, 2, Ffn.lat], BF16),
              "fc2": cv([2, 2, D], BF16), "down": cv([2, Ffn.hidden // P, D], BF16)}
        hT = cv([2, 2, 8, GT * P], BF16)
        fT = cv([2, 2, GT * P], BF16)
        eT = cv([2, 2, 2, GT * P], BF16)
        relu32, sq32 = cv([512], F32), cv([512], F32)
        logits, top8 = cv([2, 8], F32), cv([2, 8], F32)
        gsum = cv([2, GT], F32)
        shared, y32, yn = cv([D], F32), cv([D], F32), cv([D], F32)
        ystats, ymv, yvar, yrstd = cv([6], F32), cv([2], F32), cv([1], F32), cv([1], F32)
        gamma, beta = cv([D], F32), cv([D], F32)
        cv = Carve()
        tw = cv([KC, D], BF16)
        tw32 = cv([KC * D], F32)
        ones = cv([P], F32)
        wabs, wmean, winv = cv([1], F32), cv([1], F32), cv([1], F32)
        brow = cv([D], F32)
        junk = cv([PREP_T, D], F32)
        sumsq, absmax, rms_in, rms = cv([PREP_T], F32), cv([PREP_T], F32), cv([PREP_T], F32), cv([PREP_T], F32)
        nmax_, ninv, nscale, nfac = cv([PREP_T], F32), cv([PREP_T], F32), cv([PREP_T], F32), cv([PREP_T], F32)
        q32 = cv([PREP_T, D], F32)
        xq = cv([PREP_T, D], BF16)
        xqT = cv([2, KC, P], BF16)
        yb, gl = cv([2, D], F32), cv([2, D], F32)

        names = ("x_in ident_set ident_ok const_ok x_out credits scratch_in "
                 "ln_stat ln_mv ln_var ln_rstd ln_xn "
                 "w_hi w_free ctx_in ctx_hi ctx_ok "
                 "proj_full proj_hi proj_free s_full s_free nmax nbias_ok exp_ok rinv_ok p_ok "
                 "t_full t_hi t_free pv_full pv_hi pv_free o_full o_free "
                 "bias_in masked summed qm_ok vx_ok rope_ok rope_lo zero_ok rot_ok "
                 "h_hi h_ok gate_max gate_ok sh_ok y_stat y_mv y_var y_rstd y_n y_g y_b x_ok gb_in "
                 "wt_in wsum wsum_ps wm wround wt_ok sumsq_ok rms_in rms_ok d1 v1 v2 xq_ok "
                 "q_turn q_evac y_full y_free gelu_ok xz_ok xo_ok").split()
        sm = {n: sem(n) for n in names}
        w_in = [sem("w_in0"), sem("w_in1")]
        xg_in = [sem("xg_in0"), sem("xg_in1")]
        xt_out = [sem("xt_out0"), sem("xt_out1")]

        START = 1
        once = "x_in ident_set ident_ok const_ok x_out bias_in wt_in gb_in ctx_in wsum wsum_ps wm wt_ok".split()
        done = {n: 0 if n in once else START for n in sm}
        done["xg"] = 0
        plan = []

        def block_of(kind, c, **raised):
            plan.append((kind, dict(done), c))
            for n, k in raised.items():
                done[n] += k

        for n in range(layers):
            if n < 5:
                block_of("prep", None, ln_stat=NT // PREP_T, ln_mv=NT // PREP_T, ln_var=NT // PREP_T,
                         ln_rstd=NT // PREP_T, ln_xn=NT, proj_full=NT, proj_hi=NT, proj_free=NT)
            if n in (0, 3):
                c = X0 if n == 0 else X1
                f, j, t = KV * NG * c.nf, KV * B, KV * NT
                block_of("cross", c, proj_full=f, proj_hi=f, proj_free=f, s_full=j * c.sbanks, nmax=j,
                         nbias_ok=j, exp_ok=j, rinv_ok=j, p_ok=j, t_full=j, t_hi=j, t_free=j,
                         pv_full=j, pv_hi=j, pv_free=j, o_full=t, o_free=t, w_hi=KV * len(c.chunks),
                         w_free=KV * len(c.chunks), ctx_ok=KV * NG, xg=KV * NG, zero_ok=2)
            if n in (1, 4):
                c = A0 if n == 1 else A1
                f, j = NG * c.nf, NG * UNITS
                block_of("self", c, proj_full=f, proj_hi=f, proj_free=f, s_full=j, masked=j, nmax=j, summed=j,
                         nbias_ok=j, exp_ok=j, rinv_ok=j, p_ok=j, t_full=j, t_hi=j, t_free=j,
                         pv_full=NT, pv_hi=NT, pv_free=NT, o_full=NT, o_free=NT, w_hi=len(c.chunks),
                         w_free=len(c.chunks), xg=NG, qm_ok=NT, vx_ok=NT,
                         rope_ok=NG * c.nrope, rot_ok=NG * c.nrope, rope_lo=NG * c.nrope, zero_ok=1)
            if n == 2:
                c = F0
                f = NG * c.nf
                block_of("ffn0", c, proj_full=f, proj_hi=f, proj_free=f, h_hi=NG * 4, h_ok=NG * 4, gate_ok=NT,
                         o_full=NT, pv_full=NT, pv_free=NT, sh_ok=NT, y_stat=NT, y_mv=NT, y_var=NT,
                         y_rstd=NT, y_n=NT, y_g=NT, y_b=NT, x_ok=NT, w_hi=len(c.chunks), w_free=len(c.chunks), xg=NG)
            if n == 5:
                block_of("ffn1", None)

        def wchunk(c, part, name, i, n):
            hd = c.hd
            if name == "wq":
                w = wq[:, part, 0:KC * c.nh * hd].rearrange("p (k m) -> p k m", k=KC)
                return w[:, i:i + n, :], P, c.nh * hd
            if name in ("wk", "wv"):
                w = (wk if name == "wk" else wv)[:, part, 0:KC * hd].rearrange("p (k m) -> p k m", k=KC)
                return w[:, i:i + n, :], P, hd
            w = wo[0:hd, part, 0:c.nh * D].rearrange("p (h m) -> p h m", h=c.nh)
            return w[:, i:i + n, :], hd, D

        def stage_of(slot, rows, n, m):
            return wstage[0:rows, slot, 0:n * m].rearrange("p (k m) -> p k m", k=n)

        def q_view(c, par, part):
            return q[0:c.hd, par, part, 0:GB * c.nh * L].rearrange("p (b h t) -> p b h t", b=GB, h=c.nh)

        def v_view(c, par, part):
            return v[:, par, part, 0:(GB + GT) * c.hd].rearrange("p (n m) -> p n m", m=c.hd)

        def fill_io(c, fill, par, part):
            def views(ps):
                kind, n = fill
                hd = c.hd
                if kind == "q":
                    return (ps[0:hd, :].rearrange("p (h b t) -> p h b t", h=2, b=GB),
                            q_view(c, par, part)[:, :, 2 * n:2 * n + 2, :].rearrange("p b h t -> p h b t"))
                if kind == "kc":
                    return ps[0:hd, :].rearrange("p (b t) -> p b t", b=GB), kT[0:hd, par, part, :, 0:S]
                if kind == "kl":
                    return (ps[0:hd, 0:GB * L].rearrange("p (b t) -> p b t", b=GB),
                            kT[0:hd, par, part, :, S:KEYS])
                if kind == "vc":
                    return (ps[:, 0:GB * hd].rearrange("p (b t) -> p b t", b=GB), v_view(c, par, part)[:, 0:GB, :])
                return (ps[:, 0:GT * hd].rearrange("p (b t) -> p b t", b=GT),
                        v_view(c, par, part)[:, GB:GB + GT, :])
            return views

        def slots(c, last):
            f = iter(range(c.nf)) if not last else iter(())
            per = [2, 2, 2, 2] if c.nf == 8 else [2, 2, 1, 1]
            order = []

            def fill():
                n = next(f, None)
                if n is not None:
                    order.append(("fill", n))
            for b in range(GB):
                order.append(("scores", b))
                fill()
                if b:
                    order.append(("pv", b - 1))
                    if b == 2:
                        order.append(("out", 0))
                if b < GB - 1:
                    if per[b] == 2:
                        fill()
                    order.append(("turn", b))
                else:
                    order.append(("turn", b))
                    if per[b] == 2:
                        fill()
                    order.append(("pv", b))
                    order.append(("out", 1))
            return order

        def cross_loop(eng, c, head, step):
            with eng.Fori(0, KV) as kvh:
                head(kvh)
                for n in range(c.nf):
                    step("fill", n, kvh * NG, 0)
                with eng.Fori(0, NG // 2 - 1) as i:
                    for par in (0, 1):
                        for what, n in slots(c, False):
                            if what == "fill":
                                step(what, n, kvh * NG + i * 2 + (par + 1), 1 - par)
                            else:
                                step(what, n, kvh * NG + i * 2 + par, par)
                for par in (0, 1):
                    for what, n in slots(c, par == 1):
                        if what == "fill":
                            step(what, n, kvh * NG + (NG - 2 + par + 1), 1 - par)
                        else:
                            step(what, n, kvh * NG + (NG - 2 + par), par)

        def swdst(c, part, name, i, n):
            m = D if name in ("wq", "wo", "bv", "bo") else c.kvc * P
            return sw[name][:, part, i:i + n, 0:m], P, m

        def fwdst(c, part, name, i, n):
            return fw[name][:, part, i:i + n, :], P, fw[name].shape[-1]

        def self_order(c, last):
            order = [("expand", 1, 0)]
            at = {0: [0], 1: [1, 2], 2: [3], 3: [4, 5], 4: [6], 5: [7]} if c.nf == 8 else {n: [n] for n in range(6)}
            for u in range(UNITS):
                if u < UNITS - 1:
                    order.append(("scores", u + 1, 0))
                elif not last:
                    order += [("expand", 0, 1), ("scores", 0, 1)]
                if not last:
                    order += [("fill", f, 1) for f in at.get(u, [])]
                order.append(("sum", u, 0))
                if u:
                    order.append(("pv", u - 1, 0))
                if u == UNITS // 2:
                    order += [("pve", 0, 0), ("out", 0, 0)]
                order.append(("turn", u, 0))
            return order + [("pv", UNITS - 1, 0), ("pve", 1, 0), ("out", 1, 0)]

        def ffn_order(c, last):
            order = [("fill", n, 1) for n in range(4) if not last] + [("down", 0, 0)]
            return order + [("fill", n, 1) for n in range(4, 8) if not last] + [("down", 1, 0)]

        def walk(eng, first, order, c, step):
            for what, n in first:
                step(what, n, 0, 0)
            with eng.Fori(0, NG // 2 - 1) as i:
                for par in (0, 1):
                    for what, n, ahead in order(c, False):
                        step(what, n, i * 2 + (par + ahead), (par + ahead) % 2)
            for par in (0, 1):
                for what, n, ahead in order(c, par == 1):
                    step(what, n, NG - 2 + par + ahead, (par + ahead) % 2)

        def self_first(c):
            return [("fill", n) for n in range(c.nf)] + [("expand", 0), ("scores", 0)]

        def ffn_first(c):
            return [("fill", n) for n in range(c.nf)]

        def rope_dst(m, par, part):
            return sk[:, par, part, 0:1, :] if m == 2 else sq[:, par, part, 2 * m:2 * m + 2, :]

        def unit(u):
            b, half = divmod(u, 2)
            return b, b // 2, b % 2, 2 * half

        def xtile(t):
            return X[:, bass.ds(t, 1), :].rearrange("p o d -> p (o d)")

        def carry(eng, col):
            if eng is nc.gpsimd:
                eng.tensor_tensor(carrier[:, col:col + 1], neghalf[:, 0:1], neghalf[:, 0:1], ALU.mult)
            else:
                eng.memset(carrier[:, col:col + 1], 0.0)

        block = ctx.enter_context(nc.Block())

        @block.sync
        def _(sp):
            for n in sm:
                if n not in once:
                    sp.sem_inc(sm[n], START)
            for slot in (0, 1):
                sp.sem_inc(xt_out[slot], 16)
            sp.dma_start(X[:, :, :], a["x"].rearrange("(t p) d -> p t d", p=P)).then_inc(sm["x_in"], 16)
            sp.dma_start(consts[:, :], a["consts"]).then_inc(sm["bias_in"], 16)
            sp.dma_start(bqk[:, :, :], a["L0_attn_bqk"]).then_inc(sm["bias_in"], 16)

            def prep(t0):
                with sp.Fori(0, NT // PREP_T) as i:
                    for t in range(PREP_T):
                        slot = t % 2
                        sp.wait_ge(sm["proj_free"], 2 + t0["proj_full"] + i * PREP_T + (t + 1))
                        sp.dma_start(scratch[bass.ds(i * PREP_T + t, 1), :, :, :, :].rearrange("o p s k t -> p (o s k t)"),
                                     xt[:, slot].rearrange("p s k t -> p (s k t)")).then_inc(xt_out[slot], 16)
                for slot in (0, 1):
                    sp.wait_ge(xt_out[slot], 16 + 16 * (t0["ln_var"] - START + NT // PREP_T) * PREP_T // 2)

            def cross(t0, c):
                nm = c.name
                qw, ow = c.nh * c.hd, c.nh * c.hd
                src = {
                    "wq": lambda h, i, n: a[nm + "_Wq"].rearrange("(k p) m -> p k m", p=P)[:, i:i + n, bass.ds(h * qw, qw)],
                    "wk": lambda h, i, n: a[nm + "_Wk"].rearrange("(k p) m -> p k m", p=P)[:, i:i + n, bass.ds(h * c.hd, c.hd)],
                    "wv": lambda h, i, n: a[nm + "_Wv"].rearrange("(k p) m -> p k m", p=P)[:, i:i + n, bass.ds(h * c.hd, c.hd)],
                    "wo": lambda h, i, n: a[nm + "_Wo"].rearrange("(v h p) m -> v p h m", p=c.hd, h=c.nh)[bass.ds(h, 1), :, i:i + n, :].rearrange("o p h m -> (o p) h m"),
                }

                def group_in(U, par, gi):
                    sp.wait_ge(sm["proj_full"], t0["proj_full"] - c.nf + U * c.nf)
                    for t in range(GT):
                        sp.dma_start(xg[:, par, t].rearrange("p s k t -> p (s k t)"),
                                     scratch[bass.ds(gi * GT + t, 1), :, :, :, :].rearrange("o p s k t -> p (o s k t)")
                                     ).then_inc(xg_in[par], 16)
                    sp.wait_ge(sm["ctx_ok"], t0["ctx_ok"] + U)
                    sp.dma_start(cstage[:, :, :], a["ctxT"].rearrange("(k p) t -> p k t", p=P)[:, :, bass.ds(gi * (GB * S), GB * S)]
                                 ).then_inc(sm["ctx_in"], 16)

                sp.wait_ge(sm["o_full"], t0["o_full"])
                sp.wait_ge(sm["x_ok"], t0["x_ok"])
                with sp.Fori(0, KV) as h:
                    for n, (name, i, k) in enumerate(c.chunks):
                        slot = n % 2
                        _, rows, m = wchunk(c, HI, name, i, k)
                        sp.wait_ge(sm["w_free"], t0["w_hi"] + h * len(c.chunks) + (n + 1))
                        sp.dma_start(stage_of(slot, rows, k, m), src[name](h, i, k)).then_inc(w_in[slot], 16)
                    with sp.Fori(0, NG // 2) as i:
                        for par in (0, 1):
                            group_in(h * NG + i * 2 + par, par, i * 2 + par)

            def simple(t0, c, src, dst):
                for n, (name, i, k) in enumerate(c.chunks):
                    _, rows, m = dst(c, HI, name, i, k)
                    sp.wait_ge(sm["w_free"], t0["w_hi"] + (n + 1))
                    sp.dma_start(stage_of(n % 2, rows, k, m), src(name, i, k)).then_inc(w_in[n % 2], 16)
                with sp.Fori(0, NG // 2) as i:
                    for par in (0, 1):
                        sp.wait_ge(sm["proj_full"], t0["proj_full"] - c.nf + (i * 2 + par) * c.nf)
                        for t in range(GT):
                            sp.dma_start(xg[:, par, t].rearrange("p s k t -> p (s k t)"),
                                         scratch[bass.ds((i * 2 + par) * GT + t, 1), :, :, :, :].rearrange("o p s k t -> p (o s k t)")
                                         ).then_inc(xg_in[par], 16)

            def rows_of(name):
                return lambda n, i, k: a[name(n)].rearrange("(k p) m -> p k m", p=P)[:, i:i + k, :]

            def self_(t0, c):
                def src(n, i, k):
                    if n in ("bv", "bo"):
                        return a[c.name + "_" + n].rearrange("(o k m) -> o k m", o=1, k=1).to_broadcast([P, 1, D])
                    return a[c.name + "_W" + n[1]].rearrange("(k p) m -> p k m", p=P)[:, i:i + k, :]
                simple(t0, c, src, swdst)

            def ffn0(t0, c):
                sp.wait_ge(sm["o_full"], t0["o_full"])
                for n, t in (("gamma", gamma), ("beta", beta)):
                    sp.dma_start(t, a["L0_ffn_ln_" + n].rearrange("(o m) -> o m", o=1).to_broadcast([P, D])).then_inc(sm["gb_in"], 16)
                simple(t0, c, lambda n, i, k: a["L0_ffn_" + n + "_w"].rearrange("(k p) m -> p k m", p=P)[:, i:i + k, :], fwdst)

            def ffn1(t0):
                sp.wait_ge(sm["w_free"], 2 + t0["w_hi"])
                sp.dma_start(wstage[:, :, :].rearrange("p (k s) m -> p k (s m)", k=1)[:, 0, 0:KC * D].rearrange("p (k m) -> p k m", k=KC),
                             a["L1_ffn_W"].rearrange("(k p) m -> p k m", p=P)).then_inc(sm["wt_in"], 16)
                sp.wait_ge(sm["o_full"], t0["o_full"])
                sp.dma_start(brow, a["L1_ffn_b"].rearrange("(o m) -> o m", o=1).to_broadcast([P, D])).then_inc(sm["wt_in"], 16)
                with sp.Fori(0, NT // PREP_T) as i:
                    for t in range(PREP_T):
                        sp.wait_ge(sm["xo_ok"], START + i * PREP_T + (t + 1))
                        sp.dma_start(out.rearrange("(t p) d -> t p d", p=P)[bass.ds(i * PREP_T + t, 1), :, :].rearrange("o p d -> p (o d)"),
                                     xtile(i * PREP_T + t)).then_inc(sm["x_out"], 16)
                sp.wait_ge(sm["x_out"], 16 * NT)

            for kind, t0, c in plan:
                if kind == "prep":
                    prep(t0)
                elif kind == "ffn1":
                    ffn1(t0)
                else:
                    {"cross": cross, "self": self_, "ffn0": ffn0}[kind](t0, c)
            if layers < 6:
                sp.wait_ge(sm["o_free"], 1 + done["o_free"])
                sp.wait_ge(sm["x_ok"], done["x_ok"])
                sp.dma_start(out.rearrange("(t p) d -> p t d", p=P), X[:, :, :]).then_inc(sm["x_out"], 16)
                sp.wait_ge(sm["x_out"], 16)

        @block.gpsimd
        def _(pool):
            pool.memset(neghalf[:, :], -0.5).then_inc(sm["ident_set"], 1)
            pool.memset(identf[:, :], 0.0).then_inc(sm["ident_set"], 1)
            pool.wait_ge(sm["ident_set"], 2)
            pool.affine_select(out=identf[:, :], in_=identf[:, :], compare_op=ALU.not_equal, fill=1.0,
                               base=0, pattern=[[-1, P]], channel_multiplier=1).then_inc(sm["ident_ok"], 1)
            pool.memset(row0[:, :], 0.0).then_inc(sm["ident_set"], 1)
            pool.wait_ge(sm["ident_set"], 3)
            pool.memset(row0[0:1, :], 1.0).then_inc(sm["ident_ok"], 1)
            pool.wait_ge(sm["ident_ok"], 1)
            pool.tensor_copy(identb[:, :], identf[:, :]).then_inc(sm["ident_ok"], 1)

            def prep(t0):
                with pool.Fori(0, NT // PREP_T) as i:
                    pool.wait_ge(sm["ln_var"], t0["ln_var"] + i + 1)
                    pool.tensor_tensor(rstd[:, :], vareps[:, :], neghalf[:, :], ALU.pow).then_inc(sm["ln_rstd"], 1)

            def cross(t0, c):
                def ctx_split(U, par):
                    pool.wait_ge(sm["ctx_in"], 16 * (t0["ctx_ok"] - START) + U * 16 + 16)
                    pool.wait_ge(sm["proj_full"], t0["proj_full"] - c.nf + U * c.nf)
                    carry(pool, 0)
                    pool.tensor_copy(cT[:, par, HI], cstage[:, :, :]).then_inc(sm["ctx_hi"], 1)
                    pool.wait_ge(sm["ctx_hi"], t0["ctx_ok"] + U + 1)
                    pool.tensor_tensor(cT[:, par, LO], cstage[:, :, :], cT[:, par, HI], ALU.subtract).then_inc(sm["ctx_ok"], 1)

                def step(what, n, U, par):
                    J = t0["exp_ok"] + U * GB + n
                    pool.wait_ge(sm["nmax"], J + 1)
                    pool.tensor_tensor(nbias[:, 0:c.pairs], negmax[:, 0:c.pairs], scales[:, 0:c.pairs], ALU.mult).then_inc(sm["nbias_ok"], 1)
                    pool.wait_ge(sm["rinv_ok"], J + 1)
                    pool.tensor_tensor(probs[:, 0:c.pairs, :], probs[:, 0:c.pairs, :],
                                       rinv[:, 0:c.pairs].unsqueeze(2).to_broadcast([P, c.pairs, KEYS]), ALU.mult).then_inc(sm["p_ok"], 1)

                pool.wait_ge(sm["o_full"], t0["o_full"])
                pool.wait_ge(sm["x_ok"], t0["x_ok"])
                pool.memset(pT2.bitcast(F32), 0.0).then_inc(sm["zero_ok"], 1)
                pool.memset(scales[:, :], c.scale).then_inc(sm["zero_ok"], 1)
                pool.wait_ge(sm["zero_ok"], t0["zero_ok"] + 2)
                with pool.Fori(0, KV) as kvh:
                    ctx_split(kvh * NG, 0)
                    with pool.Fori(0, NG // 2 - 1) as i:
                        for par in (0, 1):
                            ctx_split(kvh * NG + i * 2 + (par + 1), 1 - par)
                            for n in range(GB):
                                step("scores", n, kvh * NG + i * 2 + par, par)
                    for par in (0, 1):
                        if par == 0:
                            ctx_split(kvh * NG + (NG - 1), 1)
                        for n in range(GB):
                            step("scores", n, kvh * NG + (NG - 2 + par), par)

            def self_(t0, c):
                pool.wait_ge(sm["o_full"], t0["o_full"])
                pool.memset(vx.bitcast(F32), 0.0).then_inc(sm["zero_ok"], 1)
                pool.wait_ge(sm["bias_in"], 32)

                def step(what, n, U, par):
                    if what == "fill" and c.fills[n][0] == "r":
                        m = c.fills[n][1]
                        N = t0["rope_ok"] + U * c.nrope + m
                        w = GT * P * (1 if m == 2 else 2)
                        pool.wait_ge(sm["rot_ok"], N + 1)
                        pool.tensor_tensor(rt1[:, 0:w], rt1[:, 0:w], rt2[:, 0:w], ALU.add).then_inc(sm["rope_ok"], 1)
                        pool.wait_ge(sm["proj_hi"], t0["proj_full"] + U * c.nf + (n + 1))
                        hi, lo = (rope_dst(m, par, x) for x in (HI, LO))
                        pool.tensor_tensor(lo, rt1[:, 0:w].rearrange("p (c t) -> p c t", t=GT * P), hi, ALU.subtract).then_inc(sm["rope_lo"], 1)
                    if what == "scores":
                        Q, s = t0["exp_ok"] + U * UNITS + n, n % 2
                        pool.wait_ge(sm["nmax"], Q + 1)
                        pool.tensor_tensor(sc[:, s], sc[:, s], smax[:, s].unsqueeze(2).to_broadcast([P, HPC, L]), ALU.add).then_inc(sm["nbias_ok"], 1)
                    if what == "sum":
                        Q, s = t0["exp_ok"] + U * UNITS + n, n % 2
                        pool.wait_ge(sm["rinv_ok"], Q + 1)
                        pool.tensor_tensor(sc[:, s], sc[:, s], sinv[:, s].unsqueeze(2).to_broadcast([P, HPC, L]), ALU.mult).then_inc(sm["p_ok"], 1)
                walk(pool, self_first(c), self_order, c, step)

            def ffn0(t0, c):
                pool.wait_ge(sm["gb_in"], 32)

                def step(what, n, U, par):
                    if what == "fill" and c.fills[n][0] == "u":
                        m = c.fills[n][1]
                        pool.wait_ge(sm["h_hi"], t0["h_hi"] + U * 4 + (m + 1))
                        pool.tensor_tensor(hT[:, par, LO, 2 * m:2 * m + 2, :], sq32.rearrange("p (c t) -> p c t", c=2),
                                           hT[:, par, HI, 2 * m:2 * m + 2, :], ALU.subtract).then_inc(sm["h_ok"], 1)
                    if what == "down":
                        N = t0["x_ok"] + U * GT + n
                        pool.wait_ge(sm["y_var"], N + 1)
                        pool.tensor_tensor(yrstd, yvar, neghalf[:, 0:1], ALU.pow).then_inc(sm["y_rstd"], 1)
                        pool.wait_ge(sm["y_n"], N + 1)
                        pool.tensor_tensor(yn, yn, gamma, ALU.mult).then_inc(sm["y_g"], 1)
                        pool.wait_ge(sm["y_g"], N + 1)
                        pool.tensor_tensor(yn, yn, beta, ALU.add).then_inc(sm["y_b"], 1)
                        pool.wait_ge(sm["y_b"], N + 1)
                        pool.tensor_tensor(xtile(U * GT + n), xtile(U * GT + n), yn, ALU.add).then_inc(sm["x_ok"], 1)
                walk(pool, ffn_first(c), ffn_order, c, step)

            def ffn1(t0):
                pool.wait_ge(sm["o_full"], t0["o_full"])
                pool.memset(ones, 1.0).then_inc(sm["zero_ok"], 1)
                with pool.Fori(0, NT // PREP_T) as i:
                    pool.wait_ge(sm["ln_var"], t0["ln_var"] + i + 1)
                    pool.tensor_tensor(rstd[:, :], vareps[:, :], neghalf[:, :], ALU.pow).then_inc(sm["ln_rstd"], 1)
                    pool.wait_ge(sm["rms_in"], START + i + 1)
                    pool.tensor_tensor(rms, rms_in, neghalf[:, :], ALU.pow).then_inc(sm["rms_ok"], 1)
                    for t in range(PREP_T):
                        pool.tensor_tensor(xtile(i * PREP_T + t), xtile(i * PREP_T + t), xn[:, t, :], ALU.add).then_inc(sm["xz_ok"], 1)

            for kind, t0, c in plan:
                if kind == "prep":
                    prep(t0)
                elif kind == "ffn1":
                    ffn1(t0)
                else:
                    {"cross": cross, "self": self_, "ffn0": ffn0}[kind](t0, c)

        @block.scalar
        def _(act):
            def prep(t0):
                with act.Fori(0, NT // PREP_T) as i:
                    for t in range(PREP_T):
                        f = i * PREP_T + t
                        slot = t % 2
                        act.wait_ge(sm["proj_full"], t0["proj_full"] + f + 1)
                        if t >= 2:
                            act.wait_ge(xt_out[slot], 16 + 8 * PREP_T * (t0["ln_var"] - START) + i * (8 * PREP_T) + 16 * ((t - 2) // 2 + 1))
                        else:
                            act.wait_ge(xt_out[slot], 16 + 8 * PREP_T * (t0["ln_var"] - START) + i * (8 * PREP_T))
                        act.activation(xt[:, slot, HI], bank[t % 2][:, :].rearrange("p (k t) -> p k t", k=KC), ACT.Copy).then_inc(sm["proj_hi"], 1)

            def cross(t0, c):
                def head(h):
                    act.wait_ge(sm["o_full"], t0["o_full"] + h * NT)
                    for n, (name, i, k) in enumerate(c.chunks):
                        slot = n % 2
                        dst, rows, m = wchunk(c, HI, name, i, k)
                        half = len(c.chunks) // 2
                        act.wait_ge(w_in[slot], 8 * (t0["w_hi"] - START) + h * (16 * half) + 16 * (n // 2 + 1))
                        act.activation(dst, stage_of(slot, rows, k, m), ACT.Copy).then_inc(sm["w_hi"], 1)

                def step(what, n, U, par):
                    J = U * GB + n + t0["exp_ok"]
                    if what == "fill":
                        src, dst = fill_io(c, c.fills[n], par, HI)(proj_ps[n % 2])
                        act.wait_ge(sm["proj_full"], t0["proj_full"] + U * c.nf + (n + 1))
                        act.activation(dst, src, ACT.Copy).then_inc(sm["proj_hi"], 1)
                    elif what == "scores":
                        act.wait_ge(sm["nbias_ok"], J + 1)
                        for j in range(c.pairs):
                            e = act.activation(probs[:, j, :], score_ps[j // 2][:, (j % 2) * KEYS:(j % 2 + 1) * KEYS],
                                               ACT.Exp, bias=nbias[:, j:j + 1], scale=c.scale,
                                               accum_out=rowsum[:, j:j + 1])
                        e.then_inc(sm["exp_ok"], 1)
                    elif what == "turn":
                        w = c.pairs * P
                        lo = 64 * (n % 2)
                        act.wait_ge(sm["t_full"], J + 1)
                        act.activation(pT1[:, HI, 0:w], turn_ps[0][:, 0:w], ACT.Copy)
                        act.activation(pT2[lo:lo + 64, n % 2, HI, 0:w], turn_ps[1][lo:lo + 64, 0:w], ACT.Copy).then_inc(sm["t_hi"], 1)
                    elif what == "pv":
                        act.wait_ge(sm["pv_full"], t0["pv_full"] + U * GB + (n + 1))
                        dst = att[0:c.hd, HI, 0:c.nh * P].rearrange("p (h t) -> p h t", h=c.nh)[:, :, 64 * (n % 2):64 * (n % 2) + 64]
                        act.activation(dst, pv_ps[0:c.hd, 0:c.nh * L].rearrange("p (h t) -> p h t", h=c.nh), ACT.Copy).then_inc(sm["pv_hi"], 1)

                act.wait_ge(sm["zero_ok"], t0["zero_ok"] + 2)
                cross_loop(act, c, head, step)

            def weights(t0, c, dst):
                act.wait_ge(sm["o_full"], t0["o_full"])
                act.wait_ge(sm["x_ok"], t0["x_ok"])
                for n, (name, i, k) in enumerate(c.chunks):
                    d, rows, m = dst(c, HI, name, i, k)
                    act.wait_ge(w_in[n % 2], 8 * (t0["w_hi"] - START) + 16 * (n // 2 + 1))
                    act.activation(d, stage_of(n % 2, rows, k, m), ACT.Copy).then_inc(sm["w_hi"], 1)

            def self_(t0, c):
                weights(t0, c, swdst)
                act.wait_ge(sm["zero_ok"], t0["zero_ok"] + 1)
                act.wait_ge(sm["bias_in"], 32)

                def step(what, n, U, par):
                    if what == "fill":
                        kind, m = c.fills[n]
                        ps = proj_ps[n % 2]
                        F = t0["proj_full"] + U * c.nf + (n + 1)
                        if kind in "qk" and not c.rope:
                            act.wait_ge(sm["proj_full"], F)
                            for j in range(2):
                                ch = 2 * m + j
                                e = act.activation((sq if kind == "q" else sk)[:, par, HI, ch, :], ps[:, j * GT * P:(j + 1) * GT * P],
                                                   ACT.Identity, bias=bqk[:, 0 if kind == "q" else 1, ch:ch + 1])
                            e.then_inc(sm["proj_hi"], 1)
                        elif kind in "qk":
                            w = GT * P * (2 if kind == "q" else 1)
                            act.wait_ge(sm["proj_full"], F)
                            act.activation(raw32[:, 0:w], ps[:, 0:w], ACT.Copy).then_inc(sm["proj_hi"], 1)
                        elif kind == "r":
                            w = GT * P * (1 if m == 2 else 2)
                            act.wait_ge(sm["rope_ok"], t0["rope_ok"] + U * c.nrope + (m + 1))
                            act.activation(rope_dst(m, par, HI), rt1[:, 0:w].rearrange("p (c t) -> p c t", t=GT * P),
                                           ACT.Copy).then_inc(sm["proj_hi"], 1)
                        else:
                            act.wait_ge(sm["proj_full"], F)
                            act.activation(sv[:, HI, m, 0:c.kvc * P], ps[:, 0:c.kvc * P], ACT.Copy).then_inc(sm["proj_hi"], 1)
                    elif what == "expand":
                        act.wait_ge(sm["proj_free"], 2 + t0["proj_full"] + U * c.nf + c.nf)
                        if n == 1:
                            act.wait_ge(sm["pv_full"], t0["pv_full"] + U * GT)
                        elif not (isinstance(U, int) and U == 0):
                            act.wait_ge(sm["pv_full"], t0["pv_full"] + U * GT - 1)
                        for b in range(2):
                            for j in range(2):
                                for part in (HI, LO):
                                    at = vx_at + ((n * 2 + part) * 2 + b) * KC * 4 * P + 64 * j
                                    dst = bass.AP(tensor=arena[:, :].tensor, offset=arena[64 * j:64 * j + 64, at:at + 1].offset,
                                                  ap=[[ARENA, 64], [4 * P, c.kvc], [P + HD, 4], [1, HD]])
                                    src = sv[64 * b:64 * b + 64, part, n, 0:c.kvc * P].rearrange("p (c j t d) -> p c j t d", j=2, t=4, d=HD)[:, :, j]
                                    e = act.activation(dst, src, ACT.Copy)
                        e.then_inc(sm["vx_ok"], 1)
                    elif what == "scores":
                        act.wait_ge(sm["nbias_ok"], t0["exp_ok"] + U * UNITS + (n + 1))
                        act.activation(sc[:, n % 2], sc[:, n % 2], ACT.Exp, scale=HD ** -0.5).then_inc(sm["exp_ok"], 1)
                    elif what == "turn":
                        act.wait_ge(sm["t_full"], t0["t_full"] + U * UNITS + (n + 1))
                        act.activation(spT[:, n % 2, HI], turn_ps[n % 2][:, :], ACT.Copy).then_inc(sm["t_hi"], 1)
                    elif what == "pve":
                        act.wait_ge(sm["pv_full"], t0["pv_full"] + U * GT + (n + 1))
                        act.activation(satt[:, HI], pv_ps[:, :].rearrange("p (c t) -> p c t", c=KC), ACT.Copy).then_inc(sm["pv_hi"], 1)
                walk(act, self_first(c), self_order, c, step)

            def ffn0(t0, c):
                weights(t0, c, fwdst)

                def step(what, n, U, par):
                    if what == "fill":
                        kind, m = c.fills[n]
                        ps = proj_ps[n % 2]
                        F = t0["proj_full"] + U * c.nf + (n + 1)
                        act.wait_ge(sm["proj_full"], F)
                        two = ps[:, :].rearrange("p (c t) -> p c t", c=2)
                        if kind == "u":
                            act.activation(relu32, ps[:, :], ACT.Relu).then_inc(sm["proj_hi"], 1)
                            act.wait_ge(sm["proj_free"], 2 + F)
                            act.activation(hT[:, par, HI, 2 * m:2 * m + 2, :], sq32.rearrange("p (c t) -> p c t", c=2),
                                           ACT.Copy).then_inc(sm["h_hi"], 1)
                        elif kind == "f":
                            act.activation(fT[:, HI], two, ACT.Copy).then_inc(sm["proj_hi"], 1)
                        elif kind == "e":
                            act.activation(eT[:, par, HI], two, ACT.Copy).then_inc(sm["proj_hi"], 1)
                        else:
                            act.activation(logits[:, m], ps[:, 0:8], ACT.Copy).then_inc(sm["proj_hi"], 1)
                    elif what == "down":
                        N = U * GT + n
                        act.wait_ge(sm["o_full"], t0["o_full"] + N + 1)
                        act.wait_ge(sm["pv_free"], 1 + t0["pv_full"] + N)
                        act.activation(shared, out_ps[:, :], ACT.Copy).then_inc(sm["sh_ok"], 1)
                walk(act, ffn_first(c), ffn_order, c, step)

            def ffn1(t0):
                act.wait_ge(sm["o_full"], t0["o_full"])
                with act.Fori(0, NT // PREP_T) as i:
                    for t in range(PREP_T):
                        act.wait_ge(sm["ln_xn"], t0["ln_xn"] + i * PREP_T + (t + 1))
                        e = act.activation(junk[:, t], xn[:, t, :], ACT.Square, accum_out=sumsq[:, t:t + 1])
                    e.then_inc(sm["sumsq_ok"], 1)
                    for t in range(PREP_T):
                        act.wait_ge(sm["q_turn"], START + i * PREP_T + (t + 1))
                        act.activation(xqT[:, t % 2], bank[t % 2][:, 0:KC * P // 2].bitcast(BF16).rearrange("p (k t) -> p k t", k=KC),
                                       ACT.Copy).then_inc(sm["q_evac"], 1)
                        if t:
                            gelu(act, i, t - 1)
                    gelu(act, i, PREP_T - 1)

            def gelu(act, i, t):
                act.wait_ge(sm["y_free"], START + i * PREP_T + (t + 1))
                act.activation(gl[:, t % 2], yb[:, t % 2], ACT.Gelu).then_inc(sm["gelu_ok"], 1)

            for kind, t0, c in plan:
                if kind == "prep":
                    prep(t0)
                elif kind == "ffn1":
                    ffn1(t0)
                else:
                    {"cross": cross, "self": self_, "ffn0": ffn0}[kind](t0, c)

        @block.vector
        def _(dve):
            dve.memset(credit[:, 0:1], 0.0).then_inc(sm["proj_free"], 2)
            dve.memset(credit[:, 1:2], 0.0).then_inc(sm["w_free"], 2)
            dve.memset(credit[:, 3:4], 0.0).then_inc(sm["t_free"], 1)
            dve.memset(credit[:, 4:5], 0.0).then_inc(sm["pv_free"], 1)
            dve.memset(credit[:, 5:6], 0.0).then_inc(sm["o_free"], 1)
            dve.memset(credit[:, 6:7], 0.0).then_inc(sm["const_ok"], 1)
            dve.wait_ge(sm["x_in"], 16)
            dve.wait_ge(sm["const_ok"], 1)

            def x_final(t0):
                dve.wait_ge(sm["o_free"], 1 + t0["o_free"])
                dve.wait_ge(sm["x_ok"], t0["x_ok"])

            def prep(t0):
                x_final(t0)
                with dve.Fori(0, NT // PREP_T) as i:
                    N = t0["ln_var"] + i
                    for t in range(PREP_T):
                        s = dve.bn_stats(stats[:, t, :], X[:, bass.ds(i * PREP_T + t, 1), :].rearrange("p o d -> p (o d)"))
                    s.then_inc(sm["ln_stat"], 1)
                    dve.wait_ge(sm["ln_stat"], N + 1)
                    carry(dve, 1)
                    for t in range(PREP_T):
                        s = dve.bn_aggr(meanvar[:, t, :], stats[:, t, :])
                    s.then_inc(sm["ln_mv"], 1)
                    dve.wait_ge(sm["ln_mv"], N + 1)
                    dve.tensor_scalar(vareps[:, :], meanvar[:, :, 1], EPS, None, ALU.add).then_inc(sm["ln_var"], 1)
                    dve.wait_ge(sm["ln_rstd"], N + 1)
                    for t in range(PREP_T):
                        dve.tensor_scalar(xn[:, t, :], X[:, bass.ds(i * PREP_T + t, 1), :].rearrange("p o d -> p (o d)"),
                                          meanvar[:, t, 0:1], rstd[:, t:t + 1], ALU.subtract, ALU.mult).then_inc(sm["ln_xn"], 1)
                    for t in range(PREP_T):
                        f = i * PREP_T + t
                        dve.wait_ge(sm["proj_hi"], t0["proj_full"] + f + 1)
                        dve.tensor_tensor(xt[:, t % 2, LO], bank[t % 2][:, :].rearrange("p (k t) -> p k t", k=KC),
                                          xt[:, t % 2, HI], ALU.subtract).then_inc(sm["proj_free"], 1)

            def cross(t0, c):
                def head(h):
                    for n, (name, i, k) in enumerate(c.chunks):
                        slot = n % 2
                        hi, rows, m = wchunk(c, HI, name, i, k)
                        lo, _, _ = wchunk(c, LO, name, i, k)
                        dve.wait_ge(sm["w_hi"], t0["w_hi"] + h * len(c.chunks) + (n + 1))
                        dve.tensor_tensor(lo, stage_of(slot, rows, k, m), hi, ALU.subtract).then_inc(sm["w_free"], 1)

                def step(what, n, U, par):
                    J = U * GB + n + t0["exp_ok"]
                    if what == "fill":
                        src, lo = fill_io(c, c.fills[n], par, LO)(proj_ps[n % 2])
                        _, hi = fill_io(c, c.fills[n], par, HI)(proj_ps[n % 2])
                        dve.wait_ge(sm["proj_hi"], t0["proj_full"] + U * c.nf + (n + 1))
                        dve.tensor_tensor(lo, src, hi, ALU.subtract).then_inc(sm["proj_free"], 1)
                    elif what == "scores":
                        for s in range(c.sbanks):
                            dve.wait_ge(sm["s_full"], t0["s_full"] + U * (GB * c.sbanks) + (n * c.sbanks + s + 1))
                            r = dve.tensor_reduce(negmax[:, 2 * s:2 * s + 2],
                                                  score_ps[s][:, 0:2 * KEYS].rearrange("p (j k) -> p j k", j=2),
                                                  AX.X, ALU.max, negate=True)
                        r.then_inc(sm["nmax"], 1)
                        dve.wait_ge(sm["exp_ok"], J + 1)
                        dve.reciprocal(rinv[:, 0:c.pairs], rowsum[:, 0:c.pairs]).then_inc(sm["rinv_ok"], 1)
                    elif what == "turn":
                        w = c.pairs * P
                        lo = 64 * (n % 2)
                        dve.wait_ge(sm["t_hi"], J + 1)
                        dve.tensor_tensor(pT1[:, LO, 0:w], turn_ps[0][:, 0:w], pT1[:, HI, 0:w], ALU.subtract)
                        dve.tensor_tensor(pT2[lo:lo + 64, n % 2, LO, 0:w], turn_ps[1][lo:lo + 64, 0:w],
                                          pT2[lo:lo + 64, n % 2, HI, 0:w], ALU.subtract).then_inc(sm["t_free"], 1)
                    elif what == "pv":
                        dve.wait_ge(sm["pv_hi"], t0["pv_hi"] + U * GB + (n + 1))
                        at = [att[0:c.hd, part, 0:c.nh * P].rearrange("p (h t) -> p h t", h=c.nh)[:, :, 64 * (n % 2):64 * (n % 2) + 64]
                              for part in (HI, LO)]
                        dve.tensor_tensor(at[LO], pv_ps[0:c.hd, 0:c.nh * L].rearrange("p (h t) -> p h t", h=c.nh),
                                          at[HI], ALU.subtract).then_inc(sm["pv_free"], 1)
                    elif what == "out":
                        dve.wait_ge(sm["o_full"], t0["o_full"] + U * GT + (n + 1))
                        xt_ = X[:, bass.ds(tile_of[0] * GT + n, 1), :].rearrange("p o d -> p (o d)")
                        dve.tensor_tensor(xt_, out_ps[:, :], xt_, ALU.add).then_inc(sm["o_free"], 1)

                tile_of = [0]

                with dve.Fori(0, KV) as kvh:
                    head(kvh)
                    for n in range(c.nf):
                        step("fill", n, kvh * NG, 0)
                    with dve.Fori(0, NG // 2 - 1) as i:
                        for par in (0, 1):
                            tile_of[0] = i * 2 + par
                            for what, n in slots(c, False):
                                if what == "fill":
                                    step(what, n, kvh * NG + i * 2 + (par + 1), 1 - par)
                                else:
                                    step(what, n, kvh * NG + i * 2 + par, par)
                    for par in (0, 1):
                        tile_of[0] = NG - 2 + par
                        for what, n in slots(c, par == 1):
                            if what == "fill":
                                step(what, n, kvh * NG + (NG - 2 + par + 1), 1 - par)
                            else:
                                step(what, n, kvh * NG + (NG - 2 + par), par)

            def weights(t0, c, dst):
                for n, (name, i, k) in enumerate(c.chunks):
                    hi, rows, m = dst(c, HI, name, i, k)
                    lo, _, _ = dst(c, LO, name, i, k)
                    dve.wait_ge(sm["w_hi"], t0["w_hi"] + (n + 1))
                    dve.tensor_tensor(lo, stage_of(n % 2, rows, k, m), hi, ALU.subtract).then_inc(sm["w_free"], 1)

            def self_(t0, c):
                weights(t0, c, swdst)
                dve.wait_ge(sm["bias_in"], 32)

                def step(what, n, U, par):
                    if what == "fill":
                        kind, m = c.fills[n]
                        ps = proj_ps[n % 2]
                        F = t0["proj_full"] + U * c.nf + (n + 1)
                        if kind in "qk" and not c.rope:
                            dve.wait_ge(sm["proj_hi"], F)
                            t = sq if kind == "q" else sk
                            for j in range(2):
                                ch = 2 * m + j
                                e = dve.scalar_tensor_tensor(out=t[:, par, LO, ch, :], in0=ps[:, j * GT * P:(j + 1) * GT * P],
                                                             scalar=bqk[:, 0 if kind == "q" else 1, ch:ch + 1],
                                                             in1=t[:, par, HI, ch, :], op0=ALU.add, op1=ALU.subtract)
                            e.then_inc(sm["proj_free"], 1)
                        elif kind in "qk":
                            g = GB * (2 if kind == "q" else 1)
                            dve.wait_ge(sm["proj_hi"], F)
                            r = {"q": m, "k": 2}[kind]
                            dve.wait_ge(sm["rope_lo"], t0["rope_lo"] + U * c.nrope + r)
                            dve.tensor_tensor(rt1[:, 0:g * L].rearrange("p (g t) -> p g t", g=g), ps[:, 0:g * L].rearrange("p (g t) -> p g t", g=g),
                                              cos.unsqueeze(1).to_broadcast([P, g, L]), ALU.mult).then_inc(sm["proj_free"], 1)
                        elif kind == "r":
                            g = GB * (1 if m == 2 else 2)
                            dve.wait_ge(sm["proj_full"], F)
                            dve.tensor_tensor(rt2[:, 0:g * L].rearrange("p (g t) -> p g t", g=g), ps[:, 0:g * L].rearrange("p (g t) -> p g t", g=g),
                                              sin.unsqueeze(1).to_broadcast([P, g, L]), ALU.mult).then_inc(sm["proj_free"], 1)
                            dve.wait_ge(sm["proj_free"], 2 + F)
                            dve.memset(credit[:, 7:8], 0.0).then_inc(sm["rot_ok"], 1)
                        else:
                            dve.wait_ge(sm["proj_hi"], F)
                            dve.tensor_tensor(sv[:, LO, m, 0:c.kvc * P], ps[:, 0:c.kvc * P], sv[:, HI, m, 0:c.kvc * P],
                                              ALU.subtract).then_inc(sm["proj_free"], 1)
                    elif what == "expand":
                        dve.wait_ge(sm["proj_free"], 2 + t0["proj_full"] + U * c.nf + c.nf)
                        if c.rope:
                            dve.wait_ge(sm["rope_lo"], t0["rope_lo"] + U * c.nrope + c.nrope)
                        if n == 1:
                            dve.wait_ge(sm["pv_full"], t0["pv_full"] + U * GT)
                        elif not (isinstance(U, int) and U == 0):
                            dve.wait_ge(sm["pv_full"], t0["pv_full"] + U * GT - 1)
                        for part in (HI, LO):
                            for h in range(HPC):
                                e = dve.tensor_scalar(qm[:, n, part, :, :, h, :],
                                                      sq[:, par, part, :, n * P:(n + 1) * P].rearrange("p c (b t) -> p c b t", b=2),
                                                      hmask[:, h:h + 1], None, ALU.mult)
                        e.then_inc(sm["qm_ok"], 1)
                    elif what == "scores":
                        Q, s = t0["exp_ok"] + U * UNITS + n, n % 2
                        dve.wait_ge(sm["s_full"], t0["s_full"] + U * UNITS + (n + 1))
                        dve.tensor_tensor(sc[:, s], score_ps[s][:, :].rearrange("p (g k) -> p g k", g=HPC),
                                          cmask.unsqueeze(1).to_broadcast([P, HPC, L]), ALU.add).then_inc(sm["masked"], 1)
                        dve.wait_ge(sm["masked"], t0["masked"] + U * UNITS + (n + 1))
                        dve.tensor_reduce(smax[:, s], sc[:, s], AX.X, ALU.max, negate=True).then_inc(sm["nmax"], 1)
                    elif what == "sum":
                        Q, s = t0["exp_ok"] + U * UNITS + n, n % 2
                        dve.wait_ge(sm["exp_ok"], Q + 1)
                        dve.tensor_reduce(ssum[:, s], sc[:, s], AX.X, ALU.add).then_inc(sm["summed"], 1)
                        dve.wait_ge(sm["summed"], t0["summed"] + U * UNITS + (n + 1))
                        dve.reciprocal(sinv[:, s], ssum[:, s]).then_inc(sm["rinv_ok"], 1)
                    elif what == "turn":
                        dve.wait_ge(sm["t_hi"], t0["t_hi"] + U * UNITS + (n + 1))
                        dve.tensor_tensor(spT[:, n % 2, LO], turn_ps[n % 2][:, :], spT[:, n % 2, HI], ALU.subtract).then_inc(sm["t_free"], 1)
                    elif what == "pve":
                        dve.wait_ge(sm["pv_hi"], t0["pv_hi"] + U * GT + (n + 1))
                        dve.tensor_tensor(satt[:, LO], pv_ps[:, :].rearrange("p (c t) -> p c t", c=KC), satt[:, HI],
                                          ALU.subtract).then_inc(sm["pv_free"], 1)
                    elif what == "out":
                        dve.wait_ge(sm["o_full"], t0["o_full"] + U * GT + (n + 1))
                        dve.tensor_tensor(xtile(U * GT + n), out_ps[:, :], xtile(U * GT + n), ALU.add).then_inc(sm["o_free"], 1)
                walk(dve, self_first(c), self_order, c, step)

            def ffn0(t0, c):
                weights(t0, c, fwdst)

                def step(what, n, U, par):
                    if what == "fill":
                        kind, m = c.fills[n]
                        ps = proj_ps[n % 2]
                        F = t0["proj_full"] + U * c.nf + (n + 1)
                        dve.wait_ge(sm["proj_hi"], F)
                        two = ps[:, :].rearrange("p (c t) -> p c t", c=2)
                        if kind == "u":
                            dve.wait_ge(sm["h_ok"], t0["h_ok"] + U * 4 + m)
                            dve.scalar_tensor_tensor(out=sq32, in0=ps[:, :], scalar=0.0, in1=relu32,
                                                     op0=ALU.max, op1=ALU.mult).then_inc(sm["proj_free"], 1)
                        elif kind == "f":
                            dve.tensor_tensor(fT[:, LO], two, fT[:, HI], ALU.subtract).then_inc(sm["proj_free"], 1)
                        elif kind == "e":
                            dve.tensor_tensor(eT[:, par, LO], two, eT[:, par, HI], ALU.subtract).then_inc(sm["proj_free"], 1)
                        else:
                            carry(dve, 1)
                            dve.max(top8[:, m], logits[:, m]).then_inc(sm["proj_free"], 1)
                            dve.wait_ge(sm["proj_free"], 2 + F)
                            dve.tensor_tensor(gsum[:, par, m:m + 1], top8[:, m, 0:1], top8[:, m, 1:2], ALU.add).then_inc(sm["gate_ok"], 1)
                    elif what == "down":
                        N = U * GT + n
                        dve.wait_ge(sm["gate_ok"], t0["gate_ok"] + U * GT + GT)
                        dve.wait_ge(sm["sh_ok"], t0["sh_ok"] + N + 1)
                        dve.wait_ge(sm["y_n"], t0["y_n"] + N)
                        dve.wait_ge(sm["pv_full"], t0["pv_full"] + N + 1)
                        dve.scalar_tensor_tensor(out=y32, in0=pv_ps[:, :], scalar=gsum[:, par, n:n + 1], in1=shared,
                                                 op0=ALU.mult, op1=ALU.add).then_inc(sm["pv_free"], 1)
                        dve.wait_ge(sm["pv_free"], 1 + t0["pv_full"] + N + 1)
                        dve.bn_stats(ystats, y32).then_inc(sm["y_stat"], 1)
                        dve.wait_ge(sm["y_stat"], t0["y_stat"] + N + 1)
                        carry(dve, 1)
                        dve.bn_aggr(ymv, ystats).then_inc(sm["y_mv"], 1)
                        dve.wait_ge(sm["y_mv"], t0["y_mv"] + N + 1)
                        dve.tensor_scalar(yvar, ymv[:, 1:2], EPS, None, ALU.add).then_inc(sm["y_var"], 1)
                        dve.wait_ge(sm["y_rstd"], t0["y_rstd"] + N + 1)
                        dve.wait_ge(sm["x_ok"], t0["x_ok"] + N)
                        dve.tensor_scalar(yn, y32, ymv[:, 0:1], yrstd, ALU.subtract, ALU.mult).then_inc(sm["y_n"], 1)
                walk(dve, ffn_first(c), ffn_order, c, step)

            def ffn1(t0):
                x_final(t0)
                W = wstage[:, 0, :]
                link = [0]

                def chain(ins):
                    link[0] += 1
                    ins.then_inc(sm["wm"], 1)
                    dve.wait_ge(sm["wm"], link[0])
                dve.wait_ge(sm["wt_in"], 32)
                dve.tensor_reduce(wabs, W, AX.X, ALU.add, apply_absolute_value=True).then_inc(sm["wsum"], 1)
                dve.wait_ge(sm["wsum_ps"], 1)
                chain(dve.tensor_scalar(wmean, out_ps[:, 0:1], 1.0 / (D * D), EPS, ALU.mult, ALU.max))
                chain(dve.reciprocal(winv, wmean))
                chain(dve.tensor_scalar(tw32, W, winv, ROUND, ALU.mult, ALU.add))
                chain(dve.tensor_scalar(tw32, tw32, ROUND, 1.0, ALU.subtract, ALU.min))
                dve.tensor_scalar(tw.rearrange("p k m -> p (k m)"), tw32, -1.0, None, ALU.max).then_inc(sm["wt_ok"], 1)
                LINKS = 7

                with dve.Fori(0, NT // PREP_T) as i:
                    N = t0["ln_stat"] + i
                    at = [0]

                    def link_(ins):
                        at[0] += 1
                        ins.then_inc(sm["d1"], 1)
                        dve.wait_ge(sm["d1"], START + i * LINKS + at[0])
                    dve.wait_ge(sm["xz_ok"], START + i * PREP_T)
                    for t in range(PREP_T):
                        s = dve.bn_stats(stats[:, t, :], xtile(i * PREP_T + t))
                    s.then_inc(sm["ln_stat"], 1)
                    dve.wait_ge(sm["ln_stat"], N + 1)
                    carry(dve, 1)
                    for t in range(PREP_T):
                        s = dve.bn_aggr(meanvar[:, t, :], stats[:, t, :])
                    s.then_inc(sm["ln_mv"], 1)
                    dve.wait_ge(sm["ln_mv"], t0["ln_mv"] + i + 1)
                    dve.tensor_scalar(vareps[:, :], meanvar[:, :, 1], EPS, None, ALU.add).then_inc(sm["ln_var"], 1)
                    dve.wait_ge(sm["ln_rstd"], t0["ln_rstd"] + i + 1)
                    for t in range(PREP_T):
                        dve.tensor_scalar(xn[:, t, :], xtile(i * PREP_T + t), meanvar[:, t, 0:1], rstd[:, t:t + 1],
                                          ALU.subtract, ALU.mult).then_inc(sm["ln_xn"], 1)
                    dve.wait_ge(sm["ln_xn"], t0["ln_xn"] + i * PREP_T + PREP_T)
                    dve.tensor_reduce(absmax, xn[:, :, :], AX.X, ALU.max, apply_absolute_value=True)
                    dve.wait_ge(sm["sumsq_ok"], START + i + 1)
                    dve.tensor_scalar(rms_in, sumsq, 1.0 / D, EPS, ALU.mult, ALU.add).then_inc(sm["rms_in"], 1)
                    dve.wait_ge(sm["rms_ok"], START + i + 1)
                    link_(dve.tensor_tensor(nmax_, absmax, rms, ALU.mult))
                    link_(dve.tensor_scalar(nmax_, nmax_, EPS, None, ALU.max))
                    link_(dve.reciprocal(ninv, nmax_))
                    dve.tensor_scalar(nfac, nmax_, 1.0 / 127.0, wmean, ALU.mult, ALU.mult)
                    link_(dve.tensor_scalar(nscale, ninv, 127.0, None, ALU.mult))
                    for t in range(PREP_T):
                        e = dve.tensor_scalar(q32[:, t, :], xn[:, t, :], rms[:, t:t + 1], nscale[:, t:t + 1], ALU.mult, ALU.mult)
                    link_(e)
                    link_(dve.tensor_scalar(q32, q32, ROUND, ROUND, ALU.add, ALU.subtract))
                    link_(dve.tensor_scalar(xq, q32, 127.0, -128.0, ALU.min, ALU.max))
                    assert at[0] == LINKS
                    dve.memset(credit[:, 7:8], 0.0).then_inc(sm["xq_ok"], 1)
                    for t in range(PREP_T):
                        if t >= 2:
                            dve_out(i, t - 2)
                        dve.wait_ge(sm["y_full"], START + i * PREP_T + (t + 1))
                        dve.scalar_tensor_tensor(out=yb[:, t % 2], in0=(pv_ps, out_ps)[t % 2][:, :], scalar=nfac[:, t:t + 1],
                                                 in1=brow, op0=ALU.mult, op1=ALU.add).then_inc(sm["y_free"], 1)
                    dve_out(i, 2)
                    dve_out(i, 3)

            def dve_out(i, t):
                dve.wait_ge(sm["gelu_ok"], START + i * PREP_T + (t + 1))
                dve.wait_ge(sm["xz_ok"], START + i * PREP_T + (t + 1))
                dve.tensor_tensor(xtile(i * PREP_T + t), xtile(i * PREP_T + t), gl[:, t % 2], ALU.add).then_inc(sm["xo_ok"], 1)

            for kind, t0, c in plan:
                if kind == "prep":
                    prep(t0)
                elif kind == "ffn1":
                    ffn1(t0)
                else:
                    {"cross": cross, "self": self_, "ffn0": ffn0}[kind](t0, c)

        @block.tensor
        def _(pe):
            pe.wait_ge(sm["ident_ok"], 3)
            pe.wait_ge(sm["bias_in"], 32)
            pe.wait_ge(sm["const_ok"], 1)

            def product(ps, stat, mov, first, last):
                for n, (s, m) in enumerate(PASSES):
                    mm = pe.matmul(ps, stat(s), mov(m), start=first and n == 0, stop=last and n == 2,
                                   skip_group_check=True)
                return mm

            def pe_start(t0):
                pe.wait_ge(sm["o_free"], 1 + t0["o_free"])
                pe.wait_ge(sm["pv_free"], 1 + t0["pv_free"])
                pe.wait_ge(sm["t_free"], 1 + t0["t_free"])
                pe.wait_ge(sm["sh_ok"], t0["sh_ok"])

            def prep(t0):
                with pe.Fori(0, NT // PREP_T) as i:
                    for t in range(PREP_T):
                        f = i * PREP_T + t
                        pe.wait_ge(sm["ln_xn"], t0["ln_xn"] + f + 1)
                        pe.wait_ge(sm["proj_free"], t0["proj_full"] + f + 1)
                        for k in range(KC):
                            mm = pe.transpose(bank[t % 2][:, k * P:(k + 1) * P], xn[:, t, k * P:(k + 1) * P], identf[:, :])
                        mm.then_inc(sm["proj_full"], 1)

            def cross(t0, c):
                hd = c.hd

                def w(t, part, k, m0, m1):
                    return t[:, part, 0:KC * (t is wq and c.nh * hd or hd)].rearrange("p (k m) -> p k m", k=KC)[:, k, m0:m1]

                def head(h):
                    pe.wait_ge(sm["w_free"], 2 + t0["w_hi"] + h * len(c.chunks) + len(c.chunks))

                def step(what, n, U, par):
                    J = U * GB + n + t0["exp_ok"]
                    if what == "fill":
                        kind, m = c.fills[n]
                        ps = proj_ps[n % 2]
                        pe.wait_ge(sm["proj_free"], t0["proj_full"] + U * c.nf + (n + 1))
                        if n == 0:
                            pe.wait_ge(xg_in[par], 16 * t0["xg"] * GT // 2 + xg_count(U, par))
                        if kind == "kc":
                            pe.wait_ge(sm["ctx_ok"], t0["ctx_ok"] + U + 1)
                        if kind == "q":
                            for j in range(2):
                                hh = 2 * m + j
                                for k in range(KC):
                                    mm = product(ps[0:hd, j * GB * L:(j + 1) * GB * L],
                                                 lambda s: w(wq, s, k, hh * hd, (hh + 1) * hd),
                                                 lambda s: xg[:, par, :, s, k, :], k == 0, k == KC - 1)
                        elif kind == "kc":
                            for k in range(KC):
                                mm = product(ps[0:hd, :], lambda s: w(wk, s, k, 0, hd), lambda s: cT[:, par, s, k, :],
                                             k == 0, k == KC - 1)
                        elif kind == "kl":
                            for k in range(KC):
                                mm = product(ps[0:hd, 0:GB * L], lambda s: w(wk, s, k, 0, hd),
                                             lambda s: xg[:, par, :, s, k, :], k == 0, k == KC - 1)
                        elif kind == "vc":
                            for b in range(GB):
                                for k in range(KC):
                                    mm = product(ps[:, b * hd:(b + 1) * hd], lambda s: cT[:, par, s, k, b * S:(b + 1) * S],
                                                 lambda s: w(wv, s, k, 0, hd), k == 0, k == KC - 1)
                        else:
                            for t in range(GT):
                                for k in range(KC):
                                    mm = product(ps[:, t * hd:(t + 1) * hd], lambda s: xg[:, par, t, s, k, :],
                                                 lambda s: w(wv, s, k, 0, hd), k == 0, k == KC - 1)
                        mm.then_inc(sm["proj_full"], 1)
                    elif what == "scores":
                        if n == 0:
                            pe.wait_ge(sm["proj_free"], 2 + t0["proj_full"] + U * c.nf + c.nf)
                        pe.wait_ge(sm["exp_ok"], J)
                        for j in range(c.pairs):
                            mm = product(score_ps[j // 2][:, (j % 2) * KEYS:(j % 2 + 1) * KEYS],
                                         lambda s: q_view(c, par, s)[:, n, 2 * j:2 * j + 2, :].rearrange("p h t -> p (h t)"),
                                         lambda s: kT[0:hd, par, s, n, :], True, True)
                            if j % 2 == 1:
                                mm.then_inc(sm["s_full"], 1)
                    elif what == "turn":
                        pe.wait_ge(sm["p_ok"], J + 1)
                        pe.wait_ge(sm["t_free"], J + 1)
                        c0 = S if n % 2 == 0 else L
                        w_ = L if n % 2 == 0 else P
                        for j in range(c.pairs):
                            pe.transpose(turn_ps[0][:, j * P:(j + 1) * P], probs[:, j, 0:S], identf[:, :])
                            mm = pe.transpose(turn_ps[1][0:w_, j * P:(j + 1) * P], probs[:, j, c0:c0 + w_], identf[:, :])
                        mm.then_inc(sm["t_full"], 1)
                    elif what == "pv":
                        pe.wait_ge(sm["t_free"], J + 2)
                        pe.wait_ge(sm["pv_free"], t0["pv_free"] + U * GB + (n + 1))
                        m = c.nh * L
                        product(pv_ps[0:hd, 0:m], lambda s: v_view(c, par, s)[:, n, :], lambda s: pT1[:, s, 0:m], True, False)
                        product(pv_ps[0:hd, 0:m], lambda s: v_view(c, par, s)[:, GB + n // 2, :],
                                lambda s: pT2[:, n % 2, s, 0:m], False, True).then_inc(sm["pv_full"], 1)
                    elif what == "out":
                        pe.wait_ge(sm["pv_free"], U * GB + t0["pv_free"] + (2 * n + 3))
                        pe.wait_ge(sm["o_free"], t0["o_free"] + U * GT + (n + 1))
                        for h in range(c.nh):
                            mm = product(out_ps[:, :], lambda s: att[0:hd, s, h * P:(h + 1) * P],
                                         lambda s: wo[0:hd, s, h * D:(h + 1) * D], h == 0, h == c.nh - 1)
                        mm.then_inc(sm["o_full"], 1)

                def xg_count(U, par):
                    return xg_expr[0]

                xg_expr = [0]

                pe_start(t0)
                with pe.Fori(0, KV) as kvh:
                    head(kvh)
                    xg_expr[0] = kvh * (16 * GT * NG // 2) + 16 * GT
                    for n in range(c.nf):
                        step("fill", n, kvh * NG, 0)
                    with pe.Fori(0, NG // 2 - 1) as i:
                        for par in (0, 1):
                            xg_expr[0] = kvh * (16 * GT * NG // 2) + i * (16 * GT) + 16 * GT * (1 if par == 0 else 2)
                            for what, n in slots(c, False):
                                if what == "fill":
                                    step(what, n, kvh * NG + i * 2 + (par + 1), 1 - par)
                                else:
                                    step(what, n, kvh * NG + i * 2 + par, par)
                    for par in (0, 1):
                        xg_expr[0] = kvh * (16 * GT * NG // 2) + 16 * GT * (NG // 2)
                        for what, n in slots(c, par == 1):
                            if what == "fill":
                                step(what, n, kvh * NG + (NG - 2 + par + 1), 1 - par)
                            else:
                                step(what, n, kvh * NG + (NG - 2 + par), par)

            def xg_wait(t0, U, par, i_off):
                pe.wait_ge(xg_in[par], 16 * t0["xg"] * GT // 2 + i_off)

            def self_(t0, c):
                pe_start(t0)
                pe.wait_ge(sm["w_free"], 2 + t0["w_hi"] + len(c.chunks))
                kw = c.kvc * P

                def step(what, n, U, par):
                    if what == "fill":
                        kind, m = c.fills[n]
                        ps = proj_ps[n % 2]
                        pe.wait_ge(sm["proj_free"], t0["proj_free"] + U * c.nf + (n + 1))
                        if n == 0:
                            pe.wait_ge(xg_in[par], 8 * GT * t0["xg"] + (U - par) * (8 * GT) + 16 * GT)
                        if kind in "qk":
                            w = sw["wq" if kind == "q" else "wk"]
                            for j in range(1 if kind == "k" and c.rope else 2):
                                ch = 2 * m + j
                                for k in range(KC):
                                    mm = product(ps[:, j * GT * P:(j + 1) * GT * P], lambda s: w[:, s, k, ch * P:(ch + 1) * P],
                                                 lambda s: xg[:, par, :, s, k, :], k == 0, k == KC - 1)
                        elif kind == "r":
                            wd = GT * P * (1 if m == 2 else 2)
                            pe.wait_ge(sm["proj_hi"], t0["proj_hi"] + U * c.nf + n)
                            mm = pe.matmul(ps[:, 0:wd], perm, raw32[:, 0:wd], start=True, stop=True)
                        else:
                            for k in range(KC):
                                mm = product(ps[:, 0:kw], lambda s: xg[:, par, m, s, k, :], lambda s: sw["wv"][:, s, k, 0:kw],
                                             k == 0, k == KC - 1 and c.rope)
                            if not c.rope:
                                for s in (HI, LO):
                                    mm = pe.matmul(ps[:, :], row0[:, :], sw["bv"][:, s, 0, :], start=False, stop=s == LO,
                                                   skip_group_check=True)
                        mm.then_inc(sm["proj_full"], 1)
                    elif what == "scores":
                        _, tile, bt, c0 = unit(n)
                        pe.wait_ge(sm["nmax"], t0["nmax"] + U * UNITS + n - 1)
                        if n % 4 == 0:
                            pe.wait_ge(sm["qm_ok"], t0["qm_ok"] + U * GT + (tile + 1))
                            pe.wait_ge(sm["proj_free"], 2 + t0["proj_free"] + U * c.nf + c.nf)
                            if c.rope:
                                pe.wait_ge(sm["rope_lo"], t0["rope_lo"] + U * c.nrope + c.nrope)
                        tok = (tile * 2 + bt) * L
                        for ci in range(2):
                            for t in range(2):
                                for j in range(2):
                                    at = ((ci * 2 + t) * 2 + j) * L
                                    kc = 0 if c.rope else c0 + ci
                                    mm = product(score_ps[n % 2][:, at:at + L],
                                                 lambda s: qm[:, tile, s, c0 + ci, bt, 4 * j + 2 * t:4 * j + 2 * t + 2, :].rearrange("p h t -> p (h t)"),
                                                 lambda s: sk[:, par, s, kc, tok:tok + L], True, True)
                        mm.then_inc(sm["s_full"], 1)
                    elif what == "turn":
                        pe.wait_ge(sm["p_ok"], t0["p_ok"] + U * UNITS + (n + 1))
                        pe.wait_ge(sm["t_free"], t0["t_free"] + U * UNITS + n)
                        for g in range(4):
                            mm = pe.transpose(turn_ps[n % 2][:, g * P:(g + 1) * P],
                                              sc[:, n % 2, 2 * g:2 * g + 2, :].rearrange("p g k -> p (g k)"), identf[:, :])
                        mm.then_inc(sm["t_full"], 1)
                    elif what == "pv":
                        _, tile, bt, c0 = unit(n)
                        pe.wait_ge(sm["t_free"], 2 + t0["t_free"] + U * UNITS + n)
                        if n % 4 == 0:
                            pe.wait_ge(sm["vx_ok"], t0["vx_ok"] + U * GT + (tile + 1))
                            pe.wait_ge(sm["pv_free"], t0["pv_free"] + U * GT + (tile + 1))
                        for ci in range(2):
                            at = (c0 + ci) * P + bt * L
                            for th in range(4):
                                kc = 0 if c.rope else c0 + ci
                                col = (ci * 4 + th) * L
                                mm = product(pv_ps[:, at:at + L], lambda s: vx[:, tile, s, bt, kc, th, :],
                                             lambda s: spT[:, n % 2, s, col:col + L], th == 0, th == 3)
                        if n % 4 == 3:
                            mm.then_inc(sm["pv_full"], 1)
                    elif what == "out":
                        pe.wait_ge(sm["pv_free"], 1 + t0["pv_free"] + U * GT + (n + 1))
                        pe.wait_ge(sm["o_free"], t0["o_free"] + U * GT + (n + 1))
                        for k in range(KC):
                            mm = product(out_ps[:, :], lambda s: satt[:, s, k, :], lambda s: sw["wo"][:, s, k, :],
                                         k == 0, k == KC - 1 and c.rope)
                        if not c.rope:
                            for s in (HI, LO):
                                mm = pe.matmul(out_ps[:, :], row0[:, :], sw["bo"][:, s, 0, :], start=False, stop=s == LO,
                                               skip_group_check=True)
                        mm.then_inc(sm["o_full"], 1)
                walk(pe, self_first(c), self_order, c, step)

            def ffn0(t0, c):
                pe_start(t0)
                pe.wait_ge(sm["w_free"], 2 + t0["w_hi"] + len(c.chunks))

                def step(what, n, U, par):
                    if what == "fill":
                        kind, m = c.fills[n]
                        ps = proj_ps[n % 2]
                        pe.wait_ge(sm["proj_free"], t0["proj_free"] + U * c.nf + (n + 1))
                        if n == 0:
                            pe.wait_ge(xg_in[par], 8 * GT * t0["xg"] + (U - par) * (8 * GT) + 16 * GT)
                        if kind in "uf":
                            w = fw["up" if kind == "u" else "fc1"]
                            for j in range(2):
                                ch = 2 * m + j
                                for k in range(KC):
                                    mm = product(ps[:, j * GT * P:(j + 1) * GT * P], lambda s: w[:, s, k, ch * P:(ch + 1) * P],
                                                 lambda s: xg[:, par, :, s, k, :], k == 0, k == KC - 1)
                        elif kind == "e":
                            pe.wait_ge(sm["proj_free"], 2 + t0["proj_free"] + U * c.nf + 1)
                            for j in range(2):
                                for k in range(2):
                                    mm = product(ps[:, j * GT * P:(j + 1) * GT * P],
                                                 lambda s: fw["expert"][:, s, k, j * P:(j + 1) * P],
                                                 lambda s: fT[:, s, k, :], k == 0, k == 1)
                        else:
                            for k in range(KC):
                                mm = product(ps[:, 0:8], lambda s: xg[:, par, m, s, k, :], lambda s: fw["gate"][:, s, k, :],
                                             k == 0, k == KC - 1)
                        mm.then_inc(sm["proj_full"], 1)
                    elif what == "down":
                        N = U * GT + n
                        pe.wait_ge(sm["h_ok"], t0["h_ok"] + U * 4 + 4)
                        pe.wait_ge(sm["proj_free"], 2 + t0["proj_free"] + U * c.nf + 6)
                        pe.wait_ge(sm["sh_ok"], t0["sh_ok"] + N)
                        for k in range(8):
                            mm = product(out_ps[:, :], lambda s: hT[:, par, s, k, n * P:(n + 1) * P],
                                         lambda s: fw["down"][:, s, k, :], k == 0, k == 7)
                        mm.then_inc(sm["o_full"], 1)
                        pe.wait_ge(sm["pv_free"], t0["pv_free"] + N + 1)
                        for k in range(2):
                            mm = product(pv_ps[:, :], lambda s: eT[:, par, s, k, n * P:(n + 1) * P],
                                         lambda s: fw["fc2"][:, s, k, :], k == 0, k == 1)
                        mm.then_inc(sm["pv_full"], 1)
                walk(pe, ffn_first(c), ffn_order, c, step)

            def ffn1(t0):
                pe_start(t0)
                pe.wait_ge(sm["proj_free"], 2 + t0["proj_free"])
                pe.wait_ge(sm["wsum"], 1)
                pe.wait_ge(sm["zero_ok"], t0["zero_ok"] + 1)
                pe.matmul(out_ps[:, 0:1], ones, wabs, start=True, stop=True).then_inc(sm["wsum_ps"], 1)
                pe.wait_ge(sm["wt_ok"], 1)

                def turn(i, t):
                    if t < 2:
                        pe.wait_ge(sm["q_evac"], START + i * PREP_T)
                    else:
                        pe.wait_ge(sm["q_evac"], START + i * PREP_T + (t - 1))
                    for k in range(KC):
                        mm = pe.transpose(bank[t % 2][:, k * P // 2:(k + 1) * P // 2].bitcast(BF16), xq[:, t, k * P:(k + 1) * P], identb[:, :])
                    mm.then_inc(sm["q_turn"], 1)

                with pe.Fori(0, NT // PREP_T) as i:
                    pe.wait_ge(sm["xq_ok"], START + i + 1)
                    turn(i, 0)
                    for t in range(PREP_T):
                        if t + 1 < PREP_T:
                            turn(i, t + 1)
                        pe.wait_ge(sm["q_evac"], START + i * PREP_T + (t + 1))
                        pe.wait_ge(sm["y_free"], START + i * PREP_T + max(t - 1, 0))
                        for k in range(KC):
                            mm = pe.matmul((pv_ps, out_ps)[t % 2][:, :], xqT[:, t % 2, k, :], tw[:, k, :], start=k == 0, stop=k == KC - 1)
                        mm.then_inc(sm["y_full"], 1)

            for kind, t0, c in plan:
                if kind == "prep":
                    prep(t0)
                elif kind == "ffn1":
                    ffn1(t0)
                else:
                    {"cross": cross, "self": self_, "ffn0": ffn0}[kind](t0, c)


def _consts():
    p = np.arange(P)
    hmask = (p[:, None] // HD == np.arange(HPC)[None, :]).astype(np.float32)
    cmask = np.where(np.arange(L)[None, :] <= (p[:, None] % L), 0.0, -1e30).astype(np.float32)
    swap = (p // HD) * HD + (p % HD + HD // 2) % HD
    perm = np.zeros((P, P), np.float32)
    perm[swap, p] = 1.0
    f32 = np.float32
    theta, factor, hi_f, lo_f, l0 = 500000.0, 32.0, 4.0, 1.0, 1024
    idx = np.arange(0, HD, 2, dtype=f32) / f32(HD)
    freq = (f32(1.0 / (2.0 * np.pi)) * np.power(f32(theta), -idx)).astype(f32)
    low, high = lo_f / l0, hi_f / l0
    scaled = np.where(freq < low, freq / f32(factor), freq)
    smooth = np.clip((l0 * freq - lo_f) / (hi_f - lo_f), 0.0, 1.0).astype(f32)
    mixed = (1 - smooth) * (freq / f32(factor)) + smooth * freq
    freq = np.where((freq >= low) & (freq <= high), mixed, scaled).astype(f32)
    phase = (f32(2.0 * np.pi) * np.arange(L, dtype=f32)[None, :] * freq[p % (HD // 2)][:, None]).astype(f32)
    sign = np.where(p % HD < HD // 2, -1.0, 1.0)[:, None]
    return np.concatenate([hmask, cmask, perm, np.cos(phase), np.sin(phase) * sign], axis=1).astype(f32)


def _layout(inputs):
    def f(n):
        return np.asarray(inputs[n])
    arr = {
        "x": f("x").reshape(B * L, D),
        "ctxT": f("ctx_4096").reshape(B * S, D).T,
        "L0_xattn_Wq": f("L0_xattn_Wq").T, "L0_xattn_Wk": f("L0_xattn_Wk").T,
        "L0_xattn_Wv": f("L0_xattn_Wv").T, "L0_xattn_Wo": f("L0_xattn_Wo").T,
        "L1_xattn_Wq": f("L1_xattn_Wq"), "L1_xattn_Wk": f("L1_xattn_Wk"),
        "L1_xattn_Wv": f("L1_xattn_Wv"), "L1_xattn_Wo": f("L1_xattn_Wo"),
        "L1_ffn_W": f("L1_ffn_W").T, "L1_ffn_b": f("L1_ffn_b"), "consts": _consts(),
    }
    for n in ("Wq", "Wk", "Wv", "Wo"):
        arr["L0_attn_" + n] = f("L0_attn_" + n).T
    for n in ("bv", "bo"):
        arr["L0_attn_" + n] = f("L0_attn_" + n)
    arr["L0_attn_bqk"] = np.stack([f("L0_attn_bq").reshape(KC, P).T, f("L0_attn_bk").reshape(KC, P).T], axis=1)
    for n in ("gate_w", "up_w", "down_w", "fc1_w", "fc2_w", "expert_w", "ln_gamma", "ln_beta"):
        arr["L0_ffn_" + n] = f("L0_ffn_" + n)
    arr["L1_attn_Wq"] = f("L1_attn_Wq").reshape(D, 8, 4, HD).transpose(0, 2, 1, 3).reshape(D, D)
    arr["L1_attn_Wo"] = f("L1_attn_Wo").reshape(8, 4, HD, D).transpose(1, 0, 2, 3).reshape(D, D)
    arr["L1_attn_Wk"], arr["L1_attn_Wv"] = f("L1_attn_Wk"), f("L1_attn_Wv")
    return {k: np.ascontiguousarray(v) for k, v in arr.items()}


def kernel(**inputs):
    import concourse.bacc as _bacc
    from concourse.bass_utils import run_bass_kernel_spmd as _run

    nc = _bacc.Bacc("TRN2", target_bir_lowering=False, num_devices=1)
    arr = _layout(inputs)
    aps = {k: nc.dram_tensor(f"in_{k}", v.shape, mybir.dt.from_np(v.dtype), kind="ExternalInput").ap()
           for k, v in arr.items()}
    out = nc.dram_tensor("out_x", (B * L, D), F32, kind="ExternalOutput").ap()
    build(nc, aps, out)
    r = _run(nc, [{f"in_{k}": v for k, v in arr.items()}], core_ids=[0])
    return r.results[0]["out_x"].reshape(B, L, D)
```

```python
from contextlib import ExitStack

import numpy as np

import concourse.bass as bass
from concourse import mybir

F32 = mybir.dt.float32
BF16 = mybir.dt.bfloat16
ALU = mybir.AluOpType
ACT = mybir.ActivationFunctionType
AX = mybir.AxisListType

P = 128
B, L, D = 32, 64, 512
S = 128
KC = D // P
NT = B * L // P
GB = 4
GT = GB * L // P
NG = B // GB
KV = 4
KEYS = S + L
EPS = 1e-5
HI, LO = 0, 1
PASSES = ((HI, HI), (HI, LO), (LO, HI))
PREP_T = 4


class Cross:

    def __init__(self, name, heads, hd):
        self.name, self.hd = name, hd
        self.nh = heads // KV
        self.pairs = self.nh // 2
        self.sbanks = self.pairs // 2
        self.scale = float(hd) ** -0.5
        self.fills = [("q", n) for n in range(self.nh // 2)] + [("kc", 0), ("kl", 0), ("vc", 0), ("vl", 0)]
        self.nf = len(self.fills)
        self.nqk = self.nf - 2
        if self.nh * hd * KC > 2048:
            self.chunks = [("wq", 0, 2), ("wq", 2, 2), ("wk", 0, KC), ("wv", 0, KC),
                           ("wo", 0, self.nh // 2), ("wo", self.nh // 2, self.nh // 2)]
        else:
            self.chunks = [("wq", 0, KC), ("wk", 0, KC), ("wv", 0, KC), ("wo", 0, self.nh)]
        self.nw = len(self.chunks)
        self.proj_w = [n for n in range(self.nw) if self.chunks[n][0] != "wo"]
        self.out_w = [n for n in range(self.nw) if self.chunks[n][0] == "wo"]


class Self:

    def __init__(self, name, rope):
        self.name, self.rope = name, rope
        self.kvc = 1 if rope else KC
        if rope:
            self.fills = [("q", 0), ("r", 0), ("q", 1), ("r", 1), ("k", 0), ("r", 2), ("v", 0), ("v", 1)]
            self.chunks = [("wq", 0, KC), ("wk", 0, KC), ("wv", 0, KC), ("wo", 0, KC)]
        else:
            self.fills = [("q", 0), ("q", 1), ("k", 0), ("k", 1), ("v", 0), ("v", 1)]
            self.chunks = [("wq", 0, KC), ("wk", 0, KC), ("wv", 0, KC), ("wo", 0, KC), ("bv", 0, 1), ("bo", 0, 1)]
        self.nf = len(self.fills)
        self.nrope = 3 if rope else 0


class Ffn:
    hidden, lat, experts = 1024, 256, 8
    fills = [("f", 0), ("u", 0), ("u", 1), ("u", 2), ("u", 3), ("e", 0), ("g", 0), ("g", 1)]
    nf = len(fills)
    chunks = [("up", 0, 2), ("up", 2, 2), ("fc1", 0, KC), ("gate", 0, KC), ("expert", 0, 2),
              ("fc2", 0, 2), ("down", 0, 4), ("down", 4, 4)]


A0 = Self("L0_attn", False)
A1 = Self("L1_attn", True)
F0 = Ffn()
HPC = 8
HD = 16
UNITS = 2 * GB
QX = 4
SCB = 4
ROUND = 1.5 * 2.0 ** 23
X0 = Cross("L0_xattn", 16, 96)
X1 = Cross("L1_xattn", 32, 128)


def build(nc, a, out, layers=6):
    ctx = ExitStack()
    with ctx:
        def sb(name, shape, dt):
            return ctx.enter_context(nc.sbuf_tensor(name, shape, dt))

        def sem(name):
            return ctx.enter_context(nc.semaphore(name))

        bank = [ctx.enter_context(nc.psum_tensor(f"bank{i}", [P, 512], F32)) for i in range(8)]
        proj_ps, score_ps, turn_ps, pv_ps, out_ps = bank[0:2], bank[2:4], bank[4:6], bank[6], bank[7]

        scratch = nc.dram_tensor("xn_scratch", (NT, P, 2, KC, P), BF16).ap()

        X = sb("X", [P, NT, D], F32)
        identf = sb("identf", [P, P], F32)
        neghalf = sb("neghalf", [P, PREP_T], F32)
        credit = sb("credit", [P, 8], F32)
        carrier = sb("carrier", [P, 8], F32)
        scales = sb("scales", [P, 4], F32)
        stats = sb("stats", [P, PREP_T, 6], F32)
        meanvar = sb("meanvar", [P, PREP_T, 2], F32)
        vareps = sb("vareps", [P, PREP_T], F32)
        rstd = sb("rstd", [P, PREP_T], F32)
        xn = sb("xn", [P, PREP_T, D], F32)
        xt = sb("xt", [P, 2, 2, KC, P], BF16)
        wstage = sb("wstage", [P, 2, 2048], F32)
        xg = sb("xg", [P, 2, GT, 2, KC, P], BF16)
        consts = sb("consts", [P, 8 + 64 + 128 + 64 + 64], F32)
        hmask, cmask, perm = consts[:, 0:8], consts[:, 8:72], consts[:, 72:200]
        cos, sin = consts[:, 200:264], consts[:, 264:328]
        row0 = sb("row0", [P, P], BF16)
        identb = sb("identb", [P, P], BF16)
        maskb = sb("maskb", [P, L], BF16)
        bqk = sb("bqk", [P, 2, KC], F32)

        ARENA = 70144
        arena = sb("arena", [P, ARENA], BF16)

        class Carve:
            def __init__(self):
                self.at = 0

            def __call__(self, shape, dt):
                n = int(np.prod(shape)) * (2 if dt == F32 else 1)
                ap = arena[:, self.at:self.at + n]
                self.at += n
                assert self.at <= ARENA, self.at
                if dt == F32:
                    ap = ap.bitcast(F32)
                if len(shape) > 1:
                    names = "abcdefg"[:len(shape)]
                    ap = ap.rearrange("p (" + " ".join(names) + ") -> p " + " ".join(names),
                                      **{k: v for k, v in zip(names[1:], shape[1:])})
                return ap

        cv = Carve()
        wq = cv([2, KC * 1024], BF16)
        wk = cv([2, KC * P], BF16)
        wv = cv([2, KC * P], BF16)
        wo = cv([2, 8 * D], BF16)
        cstage = cv([2, KC, GB * S], F32)
        cT = cv([2, 2, KC, GB * S], BF16)
        q = cv([2, 2, GB * 8 * L], BF16)
        kT = cv([2, 2, GB, KEYS], BF16)
        v = cv([2, 2, (GB + GT) * P], BF16)
        negmax, nbias, rowsum, rinv = cv([2, 4], F32), cv([2, 4], F32), cv([2, 4], F32), cv([2, 4], F32)
        probs = cv([2, 4, KEYS], F32)
        pT1 = cv([2, 512], BF16)
        pT2 = cv([2, 2, 512], BF16)
        att = cv([2, 8 * P], BF16)

        cv = Carve()
        sw = {n: cv([2, KC, D], BF16) for n in ("wq", "wk", "wv", "wo")}
        shared_at = cv.at
        sw.update({n: cv([2, 1, D], BF16) for n in ("bv", "bo")})
        cv.at = shared_at
        raw32, rt1, rt2 = cv([512], F32), cv([512], F32), cv([512], F32)
        vx_at = cv.at
        vx = cv([2, 2, 2, KC, 4, P], BF16)
        qm = cv([2, 2, KC, 2, HPC, L], BF16)
        sq = cv([2, 2, KC, GT * P], BF16)
        sk = cv([2, 2, KC, GT * P], BF16)
        sv = cv([2, GT, D], BF16)
        sc = cv([SCB, HPC, L], F32)
        spT = cv([2, 2, 512], BF16)
        satt = cv([2, KC, P], BF16)
        smax, ssum, sinv = cv([SCB, 8], F32), cv([SCB, 8], F32), cv([SCB, 8], F32)
        cv = Carve()
        fw = {"up": cv([2, KC, Ffn.hidden], BF16), "fc1": cv([2, KC, Ffn.lat], BF16),
              "gate": cv([2, KC, Ffn.experts], BF16), "expert": cv([2, 2, Ffn.lat], BF16),
              "fc2": cv([2, 2, D], BF16), "down": cv([2, Ffn.hidden // P, D], BF16)}
        hT = cv([2, 2, 8, GT * P], BF16)
        fT = cv([2, 2, GT * P], BF16)
        eT = cv([2, 2, 2, GT * P], BF16)
        relu32, sq32 = cv([512], F32), cv([512], F32)
        logits, top8 = cv([2, 8], F32), cv([2, 8], F32)
        gsum = cv([2, GT], F32)
        shared, y32, yn = cv([D], F32), cv([D], F32), cv([D], F32)
        ystats, ymv, yvar, yrstd = cv([6], F32), cv([2], F32), cv([1], F32), cv([1], F32)
        gamma, beta = cv([D], F32), cv([D], F32)
        cv = Carve()
        tw = cv([KC, D], BF16)
        tw32 = cv([KC * D], F32)
        ones = cv([P], F32)
        wabs, wmean, winv = cv([1], F32), cv([1], F32), cv([1], F32)
        brow = cv([D], F32)
        junk = cv([PREP_T, D], F32)
        sumsq, absmax, rms_in, rms = cv([PREP_T], F32), cv([PREP_T], F32), cv([PREP_T], F32), cv([PREP_T], F32)
        nmax_, ninv, nscale, nfac = cv([PREP_T], F32), cv([PREP_T], F32), cv([PREP_T], F32), cv([PREP_T], F32)
        q32 = cv([PREP_T, D], F32)
        xq = cv([PREP_T, D], BF16)
        xqT = cv([2, KC, P], BF16)
        yb, gl = cv([2, D], F32), cv([2, D], F32)

        names = ("x_in ident_set ident_ok const_ok x_out credits scratch_in "
                 "ln_stat ln_mv ln_var ln_rstd ln_xn "
                 "w_hi w_free ctx_hi ctx_ok "
                 "proj_full proj_hi proj_free s_full s_free nmax nbias_ok exp_ok rinv_ok p_ok "
                 "t_full t_hi t_free pv_full pv_hi pv_free o_full o_free "
                 "bias_in shifted summed qm_ok qlo_ok vx_ok rope_ok rope_lo zero_ok rot_ok "
                 "h_hi h_ok gate_max gate_ok sh_ok y_stat y_mv y_var y_rstd y_n y_g y_b x_ok gb_in "
                 "wt_in wsum wsum_ps wm wround wt_ok sumsq_ok rms_in rms_ok d1 v1 v2 xq_ok "
                 "q_turn q_evac y_full y_free gelu_ok xz_ok xo_ok").split()
        sm = {n: sem(n) for n in names}
        w_in = [sem("w_in0"), sem("w_in1")]
        xg_in = [sem("xg_in0"), sem("xg_in1")]
        ctx_in = [sem("ctx_in0"), sem("ctx_in1")]
        xt_out = [sem("xt_out0"), sem("xt_out1")]

        START = 1
        once = "x_in ident_set ident_ok const_ok x_out bias_in wt_in gb_in wsum wsum_ps wm wt_ok".split()
        done = {n: 0 if n in once else START for n in sm}
        done["xg"] = done["ctx"] = 0
        plan = []

        def block_of(kind, c, **raised):
            plan.append((kind, dict(done), c))
            for n, k in raised.items():
                done[n] += k

        for n in range(layers):
            if n < 5:
                block_of("prep", None, ln_stat=NT // PREP_T, ln_mv=NT // PREP_T, ln_var=NT // PREP_T,
                         ln_rstd=NT // PREP_T, ln_xn=NT, proj_full=NT, proj_hi=NT, proj_free=NT)
            if n in (0, 3):
                c = X0 if n == 0 else X1
                f, j, t = KV * NG * c.nf, KV * B, KV * NT
                block_of("cross", c, proj_full=f, proj_hi=f, proj_free=f, s_full=j * c.sbanks, nmax=j,
                         nbias_ok=j, exp_ok=j, rinv_ok=j, p_ok=j, t_full=j, t_hi=j, t_free=j,
                         pv_full=j, pv_hi=j, pv_free=j, o_full=t, o_free=t, w_hi=KV * len(c.chunks),
                         w_free=KV * len(c.chunks), ctx_hi=KV * NG * KC, ctx_ok=KV * NG * KC, ctx=KV * NG, xg=KV * NG, zero_ok=2)
            if n in (1, 4):
                c = A0 if n == 1 else A1
                f, j = NG * c.nf, NG * UNITS
                block_of("self", c, proj_full=f, proj_hi=f, proj_free=f, s_full=j, nmax=j, summed=j, shifted=j,
                         qlo_ok=NT * QX, exp_ok=j, rinv_ok=j, p_ok=j, t_full=j, t_hi=j, t_free=j,
                         pv_full=NT, pv_hi=NT, pv_free=NT, o_full=NT, o_free=NT, w_hi=len(c.chunks),
                         w_free=len(c.chunks), xg=NG, qm_ok=NT * QX, vx_ok=NT * 2,
                         rope_ok=NG * c.nrope, rot_ok=NG * c.nrope, rope_lo=NG * c.nrope, zero_ok=1)
            if n == 2:
                c = F0
                f = NG * c.nf
                block_of("ffn0", c, proj_full=f, proj_hi=f, proj_free=f, h_hi=NG * 4, h_ok=NG * 4, gate_ok=NT,
                         o_full=NT, pv_full=NT, pv_free=NT, sh_ok=NT, y_stat=NT, y_mv=NT, y_var=NT,
                         y_rstd=NT, y_n=NT, y_g=NT, y_b=NT, x_ok=NT, w_hi=len(c.chunks), w_free=len(c.chunks), xg=NG)
            if n == 5:
                block_of("ffn1", None)

        def wchunk(c, part, name, i, n):
            hd = c.hd
            if name == "wq":
                w = wq[:, part, 0:KC * c.nh * hd].rearrange("p (k m) -> p k m", k=KC)
                return w[:, i:i + n, :], P, c.nh * hd
            if name in ("wk", "wv"):
                w = (wk if name == "wk" else wv)[:, part, 0:KC * hd].rearrange("p (k m) -> p k m", k=KC)
                return w[:, i:i + n, :], P, hd
            w = wo[0:hd, part, 0:c.nh * D].rearrange("p (h m) -> p h m", h=c.nh)
            return w[:, i:i + n, :], hd, D

        def stage_of(slot, rows, n, m):
            return wstage[0:rows, slot, 0:n * m].rearrange("p (k m) -> p k m", k=n)

        def q_view(c, par, part):
            return q[0:c.hd, par, part, 0:GB * c.nh * L].rearrange("p (b h t) -> p b h t", b=GB, h=c.nh)

        def v_view(c, par, part):
            return v[:, par, part, 0:(GB + GT) * c.hd].rearrange("p (n m) -> p n m", m=c.hd)

        def fill_io(c, fill, par, part):
            def views(ps):
                kind, n = fill
                hd = c.hd
                if kind == "q":
                    return (ps[0:hd, :].rearrange("p (h b t) -> p h b t", h=2, b=GB),
                            q_view(c, par, part)[:, :, 2 * n:2 * n + 2, :].rearrange("p b h t -> p h b t"))
                if kind == "kc":
                    return ps[0:hd, :].rearrange("p (b t) -> p b t", b=GB), kT[0:hd, par, part, :, 0:S]
                if kind == "kl":
                    return (ps[0:hd, 0:GB * L].rearrange("p (b t) -> p b t", b=GB),
                            kT[0:hd, par, part, :, S:KEYS])
                if kind == "vc":
                    return (ps[:, 0:GB * hd].rearrange("p (b t) -> p b t", b=GB), v_view(c, par, part)[:, 0:GB, :])
                return (ps[:, 0:GT * hd].rearrange("p (b t) -> p b t", b=GT),
                        v_view(c, par, part)[:, GB:GB + GT, :])
            return views

        def cross_order(c, fill, ctx, seam):
            order, fills = [], iter(range(c.nf) if fill else ())

            def take(k):
                for n in (n for _, n in zip(range(k), fills)):
                    order.append(("fill", n, 1))
            if c.nf == 8:
                before, after = ([1, 1, 1, 1], [1, 1, 0, 1]) if not seam else ([0, 0, 1, 3], [0, 1, 1, 1])
            else:
                before, after = ([1, 0, 0, 1], [1, 1, 0, 1]) if not seam else ([0, 0, 1, 1], [0, 1, 1, 1])
            weights = iter(c.proj_w if seam else ())
            for b in range(GB):
                if ctx:
                    order.append(("ctx", b, 2))
                if seam and b < 2:
                    order += [("w", n, 1) for _, n in zip(range((len(c.proj_w) + 1 - b) // 2), weights)]
                take(before[b])
                if b < GB - 1:
                    order.append(("scores", b + 1, 0))
                elif fill:
                    order.append(("scores", 0, 1))
                order.append(("turn", b, 0))
                if b < GB - 1:
                    order.append(("exp", b + 1, 0))
                elif fill:
                    order.append(("exp", 0, 1))
                if b == 2:
                    order.append(("out", 0, 0))
                take(after[b])
                if b < GB - 1:
                    order.append(("norm", b + 1, 0))
                elif fill:
                    order.append(("norm", 0, 1))
                order.append(("pv", b, 0))
            take(c.nf)
            order.append(("out", 1, 0))
            if seam:
                order += [("w", n, 1) for n in c.out_w]
            return order

        def cross_walk(c, eng, step):
            def run(what, n, ahead, U, par, h, g, seam=False):
                if what == "w":
                    step(what, n, None, None, h + 1, None)
                elif ahead and seam:
                    step(what, n, U + ahead, (par + ahead) % 2, h + 1, 0)
                else:
                    step(what, n, U + ahead, (par + ahead) % 2, h, g)

            for n in range(c.nw):
                step("w", n, None, None, 0, None)
            for U in (0, 1):
                for k in range(KC):
                    step("ctx", k, U, U, 0, U)
            for n in range(c.nf):
                step("fill", n, 0, 0, 0, 0)
            for what in ("scores", "exp", "norm"):
                step(what, 0, 0, 0, 0, 0)

            def head(h, last):
                with eng.Fori(0, NG // 2 - 1) as i:
                    for par in (0, 1):
                        for what, n, ahead in cross_order(c, True, True, False):
                            run(what, n, ahead, h * NG + i * 2 + par, par, h, i * 2 + par)
                for par in (0, 1):
                    for what, n, ahead in cross_order(c, par == 0 or not last, not last, par == 1 and not last):
                        run(what, n, ahead, h * NG + (NG - 2 + par), par, h, NG - 2 + par, par == 1)
            with eng.Fori(0, KV - 1) as h:
                head(h, False)
            head(KV - 1, True)

        def swdst(c, part, name, i, n):
            m = D if name in ("wq", "wo", "bv", "bo") else c.kvc * P
            return sw[name][:, part, i:i + n, 0:m], P, m

        def fwdst(c, part, name, i, n):
            return fw[name][:, part, i:i + n, :], P, fw[name].shape[-1]

        def self_order(c, last):
            order = []
            at = {0: [0, 1], 1: [2, 3], 2: [4], 3: [5], 4: [6, 7]} if c.nf == 8 else {n: [n] for n in range(5)} | {4: [4, 5]}

            def ahead(what, n):
                if n < UNITS:
                    order.append((what, n, 0))
                elif not last:
                    order.append((what, n - UNITS, 1))
            for u in range(UNITS):
                if u:
                    ahead("scores", u + 2)
                if not last:
                    order += [("fill", f, 1) for f in at.get(u, [])]
                if u < 2:
                    order.append(("qx", QX + 2 + u, 0))
                elif not last:
                    order.append(("qx", u - 2, 1))
                ahead("sum", u + 1)
                if u:
                    order.append(("pv", u - 1, 0))
                if u == UNITS // 2:
                    order += [("pve", 0, 0), ("out", 0, 0)]
                if u in (1, 2):
                    order.append(("vx", 2 + (u - 1), 0))
                elif u >= UNITS - 2 and not last:
                    order.append(("vx", u - (UNITS - 2), 1))
                order.append(("turn", u, 0))
            ahead("scores", UNITS + 2)
            return order + [("pv", UNITS - 1, 0), ("pve", 1, 0), ("out", 1, 0)]

        def ffn_order(c, last):
            order = [("fill", n, 1) for n in range(4) if not last] + [("down", 0, 0)]
            return order + [("fill", n, 1) for n in range(4, 8) if not last] + [("down", 1, 0)]

        def walk(eng, first, order, c, step):
            for what, n in first:
                step(what, n, 0, 0)
            with eng.Fori(0, NG // 2 - 1) as i:
                for par in (0, 1):
                    for what, n, ahead in order(c, False):
                        step(what, n, i * 2 + (par + ahead), (par + ahead) % 2)
            for par in (0, 1):
                for what, n, ahead in order(c, par == 1):
                    step(what, n, NG - 2 + par + ahead, (par + ahead) % 2)

        def self_first(c):
            return [("fill", n) for n in range(c.nf)] + [("qx", n) for n in range(QX)] + [("vx", 0), ("vx", 1)] + \
                [("scores", n) for n in range(2)] + [("qx", QX), ("qx", QX + 1), ("scores", 2), ("sum", 0)]

        def ffn_first(c):
            return [("fill", n) for n in range(c.nf)]

        def rope_dst(m, par, part):
            return sk[:, par, part, 0:1, :] if m == 2 else sq[:, par, part, 2 * m:2 * m + 2, :]

        def spread(eng, t0, c, n, U, par, part):
            tile, piece = divmod(n, QX)
            nq = 4 if c.rope else 2
            eng.wait_ge(sm["proj_free"], 2 + t0["proj_full"] + U * c.nf + nq)
            if c.rope:
                eng.wait_ge(sm["rope_lo"], t0["rope_lo"] + U * c.nrope + 2)
            if tile == 1:
                eng.wait_ge(sm["s_full"], t0["s_full"] + U * UNITS)
            elif not (isinstance(U, int) and U == 0):
                eng.wait_ge(sm["s_full"], t0["s_full"] + U * UNITS - UNITS // 2)
            for h in range(piece * HPC // QX, (piece + 1) * HPC // QX):
                e = eng.tensor_tensor(qm[:, tile, part, :, :, h, :],
                                      sq[:, par, part, :, tile * P:(tile + 1) * P].rearrange("p c (b t) -> p c b t", b=2),
                                      hmask[:, h:h + 1].unsqueeze(2).unsqueeze(3).to_broadcast([P, KC, 2, L]), ALU.mult)
            return e

        def unit(u):
            b, half = divmod(u, 2)
            return b, b // 2, b % 2, 2 * half

        def xtile(t):
            return X[:, bass.ds(t, 1), :].rearrange("p o d -> p (o d)")

        def carry(eng, col):
            if eng is nc.gpsimd:
                eng.tensor_tensor(carrier[:, col:col + 1], neghalf[:, 0:1], neghalf[:, 0:1], ALU.mult)
            else:
                eng.memset(carrier[:, col:col + 1], 0.0)

        block = ctx.enter_context(nc.Block())

        @block.sync
        def _(sp):
            for n in sm:
                if n not in once:
                    sp.sem_inc(sm[n], START)
            for slot in (0, 1):
                sp.sem_inc(xt_out[slot], 16)
            sp.dma_start(X[:, :, :], a["x"].rearrange("(t p) d -> p t d", p=P)).then_inc(sm["x_in"], 16)
            sp.dma_start(consts[:, :], a["consts"]).then_inc(sm["bias_in"], 16)
            sp.dma_start(bqk[:, :, :], a["L0_attn_bqk"]).then_inc(sm["bias_in"], 16)

            def prep(t0):
                with sp.Fori(0, NT // PREP_T) as i:
                    for t in range(PREP_T):
                        slot = t % 2
                        sp.wait_ge(sm["proj_free"], 2 + t0["proj_full"] + i * PREP_T + (t + 1))
                        sp.dma_start(scratch[bass.ds(i * PREP_T + t, 1), :, :, :, :].rearrange("o p s k t -> p (o s k t)"),
                                     xt[:, slot].rearrange("p s k t -> p (s k t)")).then_inc(xt_out[slot], 16)

            def scratch_whole(t0):
                for slot in (0, 1):
                    sp.wait_ge(xt_out[slot], 16 + 16 * (t0["ln_var"] - START) * PREP_T // 2)

            def cross(t0, c):
                nm = c.name
                qw, ow = c.nh * c.hd, c.nh * c.hd
                src = {
                    "wq": lambda h, i, n: a[nm + "_Wq"].rearrange("(k p) m -> p k m", p=P)[:, i:i + n, bass.ds(h * qw, qw)],
                    "wk": lambda h, i, n: a[nm + "_Wk"].rearrange("(k p) m -> p k m", p=P)[:, i:i + n, bass.ds(h * c.hd, c.hd)],
                    "wv": lambda h, i, n: a[nm + "_Wv"].rearrange("(k p) m -> p k m", p=P)[:, i:i + n, bass.ds(h * c.hd, c.hd)],
                    "wo": lambda h, i, n: a[nm + "_Wo"].rearrange("(v h p) m -> v p h m", p=c.hd, h=c.nh)[bass.ds(h, 1), :, i:i + n, :].rearrange("o p h m -> (o p) h m"),
                }

                def ctx_load(U, par, gi):
                    sp.dma_start(cstage[:, par, :, :], a["ctxT"].rearrange("(k p) t -> p k t", p=P)[:, :, bass.ds(gi * (GB * S), GB * S)]
                                 ).then_inc(ctx_in[par], 16)

                def xn_load(U, par, gi):
                    for t in range(GT):
                        sp.dma_start(xg[:, par, t].rearrange("p s k t -> p (s k t)"),
                                     scratch[bass.ds(gi * GT + t, 1), :, :, :, :].rearrange("o p s k t -> p (o s k t)")
                                     ).then_inc(xg_in[par], 16)

                def group_in(U, par, gi):
                    sp.wait_ge(sm["ctx_ok"], t0["ctx_ok"] + (U - 1) * KC)
                    ctx_load(U, par, gi)
                    sp.wait_ge(sm["proj_full"], t0["proj_full"] + (U - 1) * c.nf)
                    xn_load(U, par, gi)

                def weights_in(h, chunks):
                    for n in chunks:
                        name, i, k = c.chunks[n]
                        _, rows, m = wchunk(c, HI, name, i, k)
                        sp.wait_ge(sm["w_free"], t0["w_hi"] + h * c.nw + (n + 1))
                        sp.dma_start(stage_of(n % 2, rows, k, m), src[name](h, i, k)).then_inc(w_in[n % 2], 16)

                weights_in(0, range(2))
                sp.wait_ge(sm["o_full"], t0["o_full"])
                sp.wait_ge(sm["x_ok"], t0["x_ok"])
                for U in (0, 1):
                    ctx_load(U, U, U)
                scratch_whole(t0)
                for U in (0, 1):
                    xn_load(U, U, U)
                weights_in(0, range(2, c.nw))

                def middle(h):
                    with sp.Fori(0, NG // 2 - 1) as i:
                        for par in (0, 1):
                            group_in(h * NG + i * 2 + (par + 2), par, i * 2 + (par + 2))
                with sp.Fori(0, KV - 1) as h:
                    middle(h)
                    weights_in(h + 1, range(2))
                    for g in (0, 1):
                        group_in(h * NG + (NG + g), g, g)
                    weights_in(h + 1, range(2, c.nw))
                middle(KV - 1)

            def simple(t0, c, src, dst):
                for n, (name, i, k) in enumerate(c.chunks):
                    _, rows, m = dst(c, HI, name, i, k)
                    sp.wait_ge(sm["w_free"], t0["w_hi"] + (n + 1))
                    sp.dma_start(stage_of(n % 2, rows, k, m), src(name, i, k)).then_inc(w_in[n % 2], 16)
                scratch_whole(t0)
                with sp.Fori(0, NG // 2) as i:
                    for par in (0, 1):
                        sp.wait_ge(sm["proj_full"], t0["proj_full"] - c.nf + (i * 2 + par) * c.nf)
                        for t in range(GT):
                            sp.dma_start(xg[:, par, t].rearrange("p s k t -> p (s k t)"),
                                         scratch[bass.ds((i * 2 + par) * GT + t, 1), :, :, :, :].rearrange("o p s k t -> p (o s k t)")
                                         ).then_inc(xg_in[par], 16)

            def rows_of(name):
                return lambda n, i, k: a[name(n)].rearrange("(k p) m -> p k m", p=P)[:, i:i + k, :]

            def self_(t0, c):
                def src(n, i, k):
                    if n in ("bv", "bo"):
                        return a[c.name + "_" + n].rearrange("(o k m) -> o k m", o=1, k=1).to_broadcast([P, 1, D])
                    return a[c.name + "_W" + n[1]].rearrange("(k p) m -> p k m", p=P)[:, i:i + k, :]
                simple(t0, c, src, swdst)

            def ffn0(t0, c):
                sp.wait_ge(sm["o_full"], t0["o_full"])
                for n, t in (("gamma", gamma), ("beta", beta)):
                    sp.dma_start(t, a["L0_ffn_ln_" + n].rearrange("(o m) -> o m", o=1).to_broadcast([P, D])).then_inc(sm["gb_in"], 16)
                simple(t0, c, lambda n, i, k: a["L0_ffn_" + n + "_w"].rearrange("(k p) m -> p k m", p=P)[:, i:i + k, :], fwdst)

            def ffn1(t0):
                sp.wait_ge(sm["w_free"], 2 + t0["w_hi"])
                sp.dma_start(wstage[:, :, :].rearrange("p (k s) m -> p k (s m)", k=1)[:, 0, 0:KC * D].rearrange("p (k m) -> p k m", k=KC),
                             a["L1_ffn_W"].rearrange("(k p) m -> p k m", p=P)).then_inc(sm["wt_in"], 16)
                sp.wait_ge(sm["o_full"], t0["o_full"])
                sp.dma_start(brow, a["L1_ffn_b"].rearrange("(o m) -> o m", o=1).to_broadcast([P, D])).then_inc(sm["wt_in"], 16)
                with sp.Fori(0, NT // PREP_T) as i:
                    for t in range(PREP_T):
                        sp.wait_ge(sm["xo_ok"], START + i * PREP_T + (t + 1))
                        sp.dma_start(out.rearrange("(t p) d -> t p d", p=P)[bass.ds(i * PREP_T + t, 1), :, :].rearrange("o p d -> p (o d)"),
                                     xtile(i * PREP_T + t)).then_inc(sm["x_out"], 16)
                sp.wait_ge(sm["x_out"], 16 * NT)

            for kind, t0, c in plan:
                if kind == "prep":
                    prep(t0)
                elif kind == "ffn1":
                    ffn1(t0)
                else:
                    {"cross": cross, "self": self_, "ffn0": ffn0}[kind](t0, c)
            if layers < 6:
                sp.wait_ge(sm["o_free"], 1 + done["o_free"])
                sp.wait_ge(sm["x_ok"], done["x_ok"])
                sp.dma_start(out.rearrange("(t p) d -> p t d", p=P), X[:, :, :]).then_inc(sm["x_out"], 16)
                sp.wait_ge(sm["x_out"], 16)

        @block.gpsimd
        def _(pool):
            pool.memset(neghalf[:, :], -0.5).then_inc(sm["ident_set"], 1)
            pool.memset(identf[:, :], 0.0).then_inc(sm["ident_set"], 1)
            pool.wait_ge(sm["ident_set"], 2)
            pool.affine_select(out=identf[:, :], in_=identf[:, :], compare_op=ALU.not_equal, fill=1.0,
                               base=0, pattern=[[-1, P]], channel_multiplier=1).then_inc(sm["ident_ok"], 1)
            pool.memset(row0[:, :], 0.0).then_inc(sm["ident_set"], 1)
            pool.wait_ge(sm["ident_set"], 3)
            pool.memset(row0[0:1, :], 1.0).then_inc(sm["ident_ok"], 1)
            pool.wait_ge(sm["ident_ok"], 1)
            pool.tensor_copy(identb[:, :], identf[:, :]).then_inc(sm["ident_ok"], 1)
            pool.wait_ge(sm["bias_in"], 32)
            pool.tensor_copy(maskb[:, :], cmask).then_inc(sm["ident_ok"], 1)

            def prep(t0):
                with pool.Fori(0, NT // PREP_T) as i:
                    pool.wait_ge(sm["ln_var"], t0["ln_var"] + i + 1)
                    pool.tensor_tensor(rstd[:, :], vareps[:, :], neghalf[:, :], ALU.pow).then_inc(sm["ln_rstd"], 1)

            def cross(t0, c):
                def step(what, n, U, par, h, g):
                    if what == "ctx":
                        N = U * KC + n + 1
                        pool.wait_ge(sm["ctx_hi"], t0["ctx_hi"] + N)
                        pool.tensor_tensor(cT[:, par, LO, n, :], cstage[:, par, n, :], cT[:, par, HI, n, :], ALU.subtract).then_inc(sm["ctx_ok"], 1)
                    elif what == "scores":
                        pool.wait_ge(sm["nmax"], t0["nmax"] + U * GB + (n + 1))
                        pool.tensor_tensor(nbias[:, n % 2, 0:c.pairs], negmax[:, n % 2, 0:c.pairs], scales[:, 0:c.pairs], ALU.mult).then_inc(sm["nbias_ok"], 1)
                    elif what == "norm":
                        pool.wait_ge(sm["rinv_ok"], t0["rinv_ok"] + U * GB + (n + 1))
                        pool.tensor_tensor(probs[:, n % 2, 0:c.pairs, :], probs[:, n % 2, 0:c.pairs, :],
                                           rinv[:, n % 2, 0:c.pairs].unsqueeze(2).to_broadcast([P, c.pairs, KEYS]), ALU.mult).then_inc(sm["p_ok"], 1)

                pool.wait_ge(sm["o_full"], t0["o_full"])
                pool.wait_ge(sm["x_ok"], t0["x_ok"])
                pool.memset(pT2.bitcast(F32), 0.0).then_inc(sm["zero_ok"], 1)
                pool.memset(scales[:, :], c.scale).then_inc(sm["zero_ok"], 1)
                pool.wait_ge(sm["zero_ok"], t0["zero_ok"] + 2)
                cross_walk(c, pool, step)

            def self_(t0, c):
                pool.wait_ge(sm["o_full"], t0["o_full"])
                pool.memset(vx.bitcast(F32), 0.0).then_inc(sm["zero_ok"], 1)
                pool.wait_ge(sm["bias_in"], 32)

                def step(what, n, U, par):
                    if what == "fill" and c.fills[n][0] == "r":
                        m = c.fills[n][1]
                        N = t0["rope_ok"] + U * c.nrope + m
                        w = GT * P * (1 if m == 2 else 2)
                        pool.wait_ge(sm["rot_ok"], N + 1)
                        pool.tensor_tensor(rt1[:, 0:w], rt1[:, 0:w], rt2[:, 0:w], ALU.add).then_inc(sm["rope_ok"], 1)
                        pool.wait_ge(sm["proj_hi"], t0["proj_full"] + U * c.nf + (n + 1))
                        hi, lo = (rope_dst(m, par, x) for x in (HI, LO))
                        pool.tensor_tensor(lo, rt1[:, 0:w].rearrange("p (c t) -> p c t", t=GT * P), hi, ALU.subtract).then_inc(sm["rope_lo"], 1)
                    if what == "qx":
                        spread(pool, t0, c, n, U, par, LO).then_inc(sm["qlo_ok"], 1)
                    if what == "sum":
                        Q, s = t0["exp_ok"] + U * UNITS + n, n % SCB
                        pool.wait_ge(sm["rinv_ok"], Q + 1)
                        pool.tensor_tensor(sc[:, s], sc[:, s], sinv[:, s].unsqueeze(2).to_broadcast([P, HPC, L]), ALU.mult).then_inc(sm["p_ok"], 1)
                walk(pool, self_first(c), self_order, c, step)

            def ffn0(t0, c):
                pool.wait_ge(sm["gb_in"], 32)

                def step(what, n, U, par):
                    if what == "fill" and c.fills[n][0] == "u":
                        m = c.fills[n][1]
                        pool.wait_ge(sm["h_hi"], t0["h_hi"] + U * 4 + (m + 1))
                        pool.tensor_tensor(hT[:, par, LO, 2 * m:2 * m + 2, :], sq32.rearrange("p (c t) -> p c t", c=2),
                                           hT[:, par, HI, 2 * m:2 * m + 2, :], ALU.subtract).then_inc(sm["h_ok"], 1)
                    if what == "down":
                        N = t0["x_ok"] + U * GT + n
                        pool.wait_ge(sm["y_var"], N + 1)
                        pool.tensor_tensor(yrstd, yvar, neghalf[:, 0:1], ALU.pow).then_inc(sm["y_rstd"], 1)
                        pool.wait_ge(sm["y_n"], N + 1)
                        pool.tensor_tensor(yn, yn, gamma, ALU.mult).then_inc(sm["y_g"], 1)
                        pool.wait_ge(sm["y_g"], N + 1)
                        pool.tensor_tensor(yn, yn, beta, ALU.add).then_inc(sm["y_b"], 1)
                        pool.wait_ge(sm["y_b"], N + 1)
                        pool.tensor_tensor(xtile(U * GT + n), xtile(U * GT + n), yn, ALU.add).then_inc(sm["x_ok"], 1)
                walk(pool, ffn_first(c), ffn_order, c, step)

            def ffn1(t0):
                pool.wait_ge(sm["o_full"], t0["o_full"])
                pool.memset(ones, 1.0).then_inc(sm["zero_ok"], 1)
                with pool.Fori(0, NT // PREP_T) as i:
                    pool.wait_ge(sm["ln_var"], t0["ln_var"] + i + 1)
                    pool.tensor_tensor(rstd[:, :], vareps[:, :], neghalf[:, :], ALU.pow).then_inc(sm["ln_rstd"], 1)
                    pool.wait_ge(sm["rms_in"], START + i + 1)
                    pool.tensor_tensor(rms, rms_in, neghalf[:, :], ALU.pow).then_inc(sm["rms_ok"], 1)
                    for t in range(PREP_T):
                        pool.tensor_tensor(xtile(i * PREP_T + t), xtile(i * PREP_T + t), xn[:, t, :], ALU.add).then_inc(sm["xz_ok"], 1)

            for kind, t0, c in plan:
                if kind == "prep":
                    prep(t0)
                elif kind == "ffn1":
                    ffn1(t0)
                else:
                    {"cross": cross, "self": self_, "ffn0": ffn0}[kind](t0, c)

        @block.scalar
        def _(act):
            def prep(t0):
                with act.Fori(0, NT // PREP_T) as i:
                    for t in range(PREP_T):
                        f = i * PREP_T + t
                        slot = t % 2
                        act.wait_ge(sm["proj_full"], t0["proj_full"] + f + 1)
                        if t >= 2:
                            act.wait_ge(xt_out[slot], 16 + 8 * PREP_T * (t0["ln_var"] - START) + i * (8 * PREP_T) + 16 * ((t - 2) // 2 + 1))
                        else:
                            act.wait_ge(xt_out[slot], 16 + 8 * PREP_T * (t0["ln_var"] - START) + i * (8 * PREP_T))
                        act.activation(xt[:, slot, HI], bank[t % 2][:, :].rearrange("p (k t) -> p k t", k=KC), ACT.Copy).then_inc(sm["proj_hi"], 1)

            def cross(t0, c):
                def step(what, n, U, par, h, g):
                    if what == "w":
                        name, i, k = c.chunks[n]
                        dst, rows, m = wchunk(c, HI, name, i, k)
                        if name == "wo":
                            act.wait_ge(sm["o_full"], t0["o_full"] + h * NT)
                        act.wait_ge(w_in[n % 2], 8 * (t0["w_hi"] - START) + h * (8 * c.nw) + 16 * (n // 2 + 1))
                        act.activation(dst, stage_of(n % 2, rows, k, m), ACT.Copy).then_inc(sm["w_hi"], 1)
                        return
                    if what == "ctx":
                        act.wait_ge(ctx_in[par], 8 * t0["ctx"] + (U - par) * 8 + 16)
                        act.activation(cT[:, par, HI, n, :], cstage[:, par, n, :], ACT.Copy).then_inc(sm["ctx_hi"], 1)
                        return
                    J = U * GB + n + t0["exp_ok"]
                    if what == "fill":
                        src, dst = fill_io(c, c.fills[n], par, HI)(proj_ps[n % 2])
                        act.wait_ge(sm["proj_full"], t0["proj_full"] + U * c.nf + (n + 1))
                        act.activation(dst, src, ACT.Copy).then_inc(sm["proj_hi"], 1)
                    elif what == "exp":
                        act.wait_ge(sm["nbias_ok"], J - t0["exp_ok"] + t0["nbias_ok"] + 1)
                        for j in range(c.pairs):
                            e = act.activation(probs[:, n % 2, j, :], score_ps[j // 2][:, (j % 2) * KEYS:(j % 2 + 1) * KEYS],
                                               ACT.Exp, bias=nbias[:, n % 2, j:j + 1], scale=c.scale,
                                               accum_out=rowsum[:, n % 2, j:j + 1])
                        e.then_inc(sm["exp_ok"], 1)
                    elif what == "turn":
                        w = c.pairs * P
                        lo = 64 * (n % 2)
                        act.wait_ge(sm["t_full"], J + 1)
                        act.activation(pT1[:, HI, 0:w], turn_ps[0][:, 0:w], ACT.Copy)
                        act.activation(pT2[lo:lo + 64, n % 2, HI, 0:w], turn_ps[1][lo:lo + 64, 0:w], ACT.Copy).then_inc(sm["t_hi"], 1)
                    elif what == "pv":
                        act.wait_ge(sm["pv_full"], t0["pv_full"] + U * GB + (n + 1))
                        dst = att[0:c.hd, HI, 0:c.nh * P].rearrange("p (h t) -> p h t", h=c.nh)[:, :, 64 * (n % 2):64 * (n % 2) + 64]
                        act.activation(dst, pv_ps[0:c.hd, 0:c.nh * L].rearrange("p (h t) -> p h t", h=c.nh), ACT.Copy).then_inc(sm["pv_hi"], 1)

                act.wait_ge(sm["zero_ok"], t0["zero_ok"] + 2)
                cross_walk(c, act, step)

            def weights(t0, c, dst):
                act.wait_ge(sm["o_full"], t0["o_full"])
                act.wait_ge(sm["x_ok"], t0["x_ok"])
                for n, (name, i, k) in enumerate(c.chunks):
                    d, rows, m = dst(c, HI, name, i, k)
                    act.wait_ge(w_in[n % 2], 8 * (t0["w_hi"] - START) + 16 * (n // 2 + 1))
                    act.activation(d, stage_of(n % 2, rows, k, m), ACT.Copy).then_inc(sm["w_hi"], 1)

            def self_(t0, c):
                weights(t0, c, swdst)
                act.wait_ge(sm["zero_ok"], t0["zero_ok"] + 1)
                act.wait_ge(sm["bias_in"], 32)

                def step(what, n, U, par):
                    if what == "fill":
                        kind, m = c.fills[n]
                        ps = proj_ps[n % 2]
                        F = t0["proj_full"] + U * c.nf + (n + 1)
                        if kind in "qk" and not c.rope:
                            act.wait_ge(sm["proj_full"], F)
                            for j in range(2):
                                ch = 2 * m + j
                                e = act.activation((sq if kind == "q" else sk)[:, par, HI, ch, :], ps[:, j * GT * P:(j + 1) * GT * P],
                                                   ACT.Identity, bias=bqk[:, 0 if kind == "q" else 1, ch:ch + 1])
                            e.then_inc(sm["proj_hi"], 1)
                        elif kind in "qk":
                            w = GT * P * (2 if kind == "q" else 1)
                            act.wait_ge(sm["proj_full"], F)
                            act.activation(raw32[:, 0:w], ps[:, 0:w], ACT.Copy).then_inc(sm["proj_hi"], 1)
                        elif kind == "r":
                            w = GT * P * (1 if m == 2 else 2)
                            act.wait_ge(sm["rope_ok"], t0["rope_ok"] + U * c.nrope + (m + 1))
                            act.activation(rope_dst(m, par, HI), rt1[:, 0:w].rearrange("p (c t) -> p c t", t=GT * P),
                                           ACT.Copy).then_inc(sm["proj_hi"], 1)
                        else:
                            act.wait_ge(sm["proj_full"], F)
                            act.activation(sv[:, HI, m, 0:c.kvc * P], ps[:, 0:c.kvc * P], ACT.Copy).then_inc(sm["proj_hi"], 1)
                    elif what == "vx":
                        act.wait_ge(sm["proj_free"], 2 + t0["proj_full"] + U * c.nf + c.nf)
                        tile, b = divmod(n, 2)
                        if tile == 1:
                            act.wait_ge(sm["pv_full"], t0["pv_full"] + U * GT)
                        elif not (isinstance(U, int) and U == 0):
                            act.wait_ge(sm["pv_full"], t0["pv_full"] + U * GT - 1)
                        for j in range(2):
                            for part in (HI, LO):
                                at = vx_at + ((tile * 2 + part) * 2 + b) * KC * 4 * P + 64 * j
                                dst = bass.AP(tensor=arena[:, :].tensor, offset=arena[64 * j:64 * j + 64, at:at + 1].offset,
                                              ap=[[ARENA, 64], [4 * P, c.kvc], [P + HD, 4], [1, HD]])
                                src = sv[64 * b:64 * b + 64, part, tile, 0:c.kvc * P].rearrange("p (c j t d) -> p c j t d", j=2, t=4, d=HD)[:, :, j]
                                e = act.activation(dst, src, ACT.Copy)
                        e.then_inc(sm["vx_ok"], 1)
                    elif what == "scores":
                        act.wait_ge(sm["shifted"], t0["shifted"] + U * UNITS + (n + 1))
                        act.activation(sc[:, n % SCB], sc[:, n % SCB], ACT.Exp, scale=HD ** -0.5).then_inc(sm["exp_ok"], 1)
                    elif what == "turn":
                        act.wait_ge(sm["t_full"], t0["t_full"] + U * UNITS + (n + 1))
                        act.activation(spT[:, n % 2, HI], turn_ps[n % 2][:, :], ACT.Copy).then_inc(sm["t_hi"], 1)
                    elif what == "pve":
                        act.wait_ge(sm["pv_full"], t0["pv_full"] + U * GT + (n + 1))
                        act.activation(satt[:, HI], pv_ps[:, :].rearrange("p (c t) -> p c t", c=KC), ACT.Copy).then_inc(sm["pv_hi"], 1)
                walk(act, self_first(c), self_order, c, step)

            def ffn0(t0, c):
                weights(t0, c, fwdst)

                def step(what, n, U, par):
                    if what == "fill":
                        kind, m = c.fills[n]
                        ps = proj_ps[n % 2]
                        F = t0["proj_full"] + U * c.nf + (n + 1)
                        act.wait_ge(sm["proj_full"], F)
                        two = ps[:, :].rearrange("p (c t) -> p c t", c=2)
                        if kind == "u":
                            act.activation(relu32, ps[:, :], ACT.Relu).then_inc(sm["proj_hi"], 1)
                            act.wait_ge(sm["proj_free"], 2 + F)
                            act.activation(hT[:, par, HI, 2 * m:2 * m + 2, :], sq32.rearrange("p (c t) -> p c t", c=2),
                                           ACT.Copy).then_inc(sm["h_hi"], 1)
                        elif kind == "f":
                            act.activation(fT[:, HI], two, ACT.Copy).then_inc(sm["proj_hi"], 1)
                        elif kind == "e":
                            act.activation(eT[:, par, HI], two, ACT.Copy).then_inc(sm["proj_hi"], 1)
                        else:
                            act.activation(logits[:, m], ps[:, 0:8], ACT.Copy).then_inc(sm["proj_hi"], 1)
                    elif what == "down":
                        N = U * GT + n
                        act.wait_ge(sm["o_full"], t0["o_full"] + N + 1)
                        act.wait_ge(sm["pv_free"], 1 + t0["pv_full"] + N)
                        act.activation(shared, out_ps[:, :], ACT.Copy).then_inc(sm["sh_ok"], 1)
                walk(act, ffn_first(c), ffn_order, c, step)

            def ffn1(t0):
                act.wait_ge(sm["o_full"], t0["o_full"])
                with act.Fori(0, NT // PREP_T) as i:
                    for t in range(PREP_T):
                        act.wait_ge(sm["ln_xn"], t0["ln_xn"] + i * PREP_T + (t + 1))
                        e = act.activation(junk[:, t], xn[:, t, :], ACT.Square, accum_out=sumsq[:, t:t + 1])
                    e.then_inc(sm["sumsq_ok"], 1)
                    for t in range(PREP_T):
                        act.wait_ge(sm["q_turn"], START + i * PREP_T + (t + 1))
                        act.activation(xqT[:, t % 2], bank[t % 2][:, 0:KC * P // 2].bitcast(BF16).rearrange("p (k t) -> p k t", k=KC),
                                       ACT.Copy).then_inc(sm["q_evac"], 1)
                        if t:
                            gelu(act, i, t - 1)
                    gelu(act, i, PREP_T - 1)

            def gelu(act, i, t):
                act.wait_ge(sm["y_free"], START + i * PREP_T + (t + 1))
                act.activation(gl[:, t % 2], yb[:, t % 2], ACT.Gelu).then_inc(sm["gelu_ok"], 1)

            for kind, t0, c in plan:
                if kind == "prep":
                    prep(t0)
                elif kind == "ffn1":
                    ffn1(t0)
                else:
                    {"cross": cross, "self": self_, "ffn0": ffn0}[kind](t0, c)

        @block.vector
        def _(dve):
            dve.memset(credit[:, 0:1], 0.0).then_inc(sm["proj_free"], 2)
            dve.memset(credit[:, 1:2], 0.0).then_inc(sm["w_free"], 2)
            dve.memset(credit[:, 3:4], 0.0).then_inc(sm["t_free"], 1)
            dve.memset(credit[:, 4:5], 0.0).then_inc(sm["pv_free"], 1)
            dve.memset(credit[:, 5:6], 0.0).then_inc(sm["o_free"], 1)
            dve.memset(credit[:, 6:7], 0.0).then_inc(sm["const_ok"], 1)
            dve.wait_ge(sm["x_in"], 16)
            dve.wait_ge(sm["const_ok"], 1)

            def x_final(t0):
                dve.wait_ge(sm["o_free"], 1 + t0["o_free"])
                dve.wait_ge(sm["x_ok"], t0["x_ok"])

            def prep(t0):
                x_final(t0)
                with dve.Fori(0, NT // PREP_T) as i:
                    N = t0["ln_var"] + i
                    for t in range(PREP_T):
                        s = dve.bn_stats(stats[:, t, :], X[:, bass.ds(i * PREP_T + t, 1), :].rearrange("p o d -> p (o d)"))
                    s.then_inc(sm["ln_stat"], 1)
                    dve.wait_ge(sm["ln_stat"], N + 1)
                    carry(dve, 1)
                    for t in range(PREP_T):
                        s = dve.bn_aggr(meanvar[:, t, :], stats[:, t, :])
                    s.then_inc(sm["ln_mv"], 1)
                    dve.wait_ge(sm["ln_mv"], N + 1)
                    dve.tensor_scalar(vareps[:, :], meanvar[:, :, 1], EPS, None, ALU.add).then_inc(sm["ln_var"], 1)
                    dve.wait_ge(sm["ln_rstd"], N + 1)
                    for t in range(PREP_T):
                        dve.tensor_scalar(xn[:, t, :], X[:, bass.ds(i * PREP_T + t, 1), :].rearrange("p o d -> p (o d)"),
                                          meanvar[:, t, 0:1], rstd[:, t:t + 1], ALU.subtract, ALU.mult).then_inc(sm["ln_xn"], 1)
                    for t in range(PREP_T):
                        f = i * PREP_T + t
                        dve.wait_ge(sm["proj_hi"], t0["proj_full"] + f + 1)
                        dve.tensor_tensor(xt[:, t % 2, LO], bank[t % 2][:, :].rearrange("p (k t) -> p k t", k=KC),
                                          xt[:, t % 2, HI], ALU.subtract).then_inc(sm["proj_free"], 1)

            def cross(t0, c):
                def step(what, n, U, par, h, g):
                    if what == "w":
                        name, i, k = c.chunks[n]
                        hi, rows, m = wchunk(c, HI, name, i, k)
                        lo, _, _ = wchunk(c, LO, name, i, k)
                        dve.wait_ge(sm["w_hi"], t0["w_hi"] + h * c.nw + (n + 1))
                        dve.tensor_tensor(lo, stage_of(n % 2, rows, k, m), hi, ALU.subtract).then_inc(sm["w_free"], 1)
                        return
                    if what == "ctx":
                        return
                    J = U * GB + n + t0["exp_ok"]
                    if what == "fill":
                        src, lo = fill_io(c, c.fills[n], par, LO)(proj_ps[n % 2])
                        _, hi = fill_io(c, c.fills[n], par, HI)(proj_ps[n % 2])
                        dve.wait_ge(sm["proj_hi"], t0["proj_full"] + U * c.nf + (n + 1))
                        dve.tensor_tensor(lo, src, hi, ALU.subtract).then_inc(sm["proj_free"], 1)
                    elif what == "scores":
                        for s in range(c.sbanks):
                            dve.wait_ge(sm["s_full"], t0["s_full"] + U * (GB * c.sbanks) + (n * c.sbanks + s + 1))
                            r = dve.tensor_reduce(negmax[:, n % 2, 2 * s:2 * s + 2],
                                                  score_ps[s][:, 0:2 * KEYS].rearrange("p (j k) -> p j k", j=2),
                                                  AX.X, ALU.max, negate=True)
                        r.then_inc(sm["nmax"], 1)
                    elif what == "norm":
                        dve.wait_ge(sm["exp_ok"], J + 1)
                        dve.reciprocal(rinv[:, n % 2, 0:c.pairs], rowsum[:, n % 2, 0:c.pairs]).then_inc(sm["rinv_ok"], 1)
                    elif what == "turn":
                        w = c.pairs * P
                        lo = 64 * (n % 2)
                        dve.wait_ge(sm["t_hi"], J + 1)
                        dve.tensor_tensor(pT1[:, LO, 0:w], turn_ps[0][:, 0:w], pT1[:, HI, 0:w], ALU.subtract)
                        dve.tensor_tensor(pT2[lo:lo + 64, n % 2, LO, 0:w], turn_ps[1][lo:lo + 64, 0:w],
                                          pT2[lo:lo + 64, n % 2, HI, 0:w], ALU.subtract).then_inc(sm["t_free"], 1)
                    elif what == "pv":
                        dve.wait_ge(sm["pv_hi"], t0["pv_hi"] + U * GB + (n + 1))
                        at = [att[0:c.hd, part, 0:c.nh * P].rearrange("p (h t) -> p h t", h=c.nh)[:, :, 64 * (n % 2):64 * (n % 2) + 64]
                              for part in (HI, LO)]
                        dve.tensor_tensor(at[LO], pv_ps[0:c.hd, 0:c.nh * L].rearrange("p (h t) -> p h t", h=c.nh),
                                          at[HI], ALU.subtract).then_inc(sm["pv_free"], 1)
                    elif what == "out":
                        dve.wait_ge(sm["o_full"], t0["o_full"] + U * GT + (n + 1))
                        xt_ = X[:, bass.ds(g * GT + n, 1), :].rearrange("p o d -> p (o d)")
                        dve.tensor_tensor(xt_, out_ps[:, :], xt_, ALU.add).then_inc(sm["o_free"], 1)

                cross_walk(c, dve, step)

            def weights(t0, c, dst):
                for n, (name, i, k) in enumerate(c.chunks):
                    hi, rows, m = dst(c, HI, name, i, k)
                    lo, _, _ = dst(c, LO, name, i, k)
                    dve.wait_ge(sm["w_hi"], t0["w_hi"] + (n + 1))
                    dve.tensor_tensor(lo, stage_of(n % 2, rows, k, m), hi, ALU.subtract).then_inc(sm["w_free"], 1)

            def self_(t0, c):
                weights(t0, c, swdst)
                dve.wait_ge(sm["bias_in"], 32)

                def step(what, n, U, par):
                    if what == "fill":
                        kind, m = c.fills[n]
                        ps = proj_ps[n % 2]
                        F = t0["proj_full"] + U * c.nf + (n + 1)
                        if kind in "qk" and not c.rope:
                            dve.wait_ge(sm["proj_hi"], F)
                            t = sq if kind == "q" else sk
                            for j in range(2):
                                ch = 2 * m + j
                                e = dve.scalar_tensor_tensor(out=t[:, par, LO, ch, :], in0=ps[:, j * GT * P:(j + 1) * GT * P],
                                                             scalar=bqk[:, 0 if kind == "q" else 1, ch:ch + 1],
                                                             in1=t[:, par, HI, ch, :], op0=ALU.add, op1=ALU.subtract)
                            e.then_inc(sm["proj_free"], 1)
                        elif kind in "qk":
                            g = GB * (2 if kind == "q" else 1)
                            dve.wait_ge(sm["proj_hi"], F)
                            r = {"q": m, "k": 2}[kind]
                            dve.wait_ge(sm["rope_lo"], t0["rope_lo"] + U * c.nrope + r)
                            dve.tensor_tensor(rt1[:, 0:g * L].rearrange("p (g t) -> p g t", g=g), ps[:, 0:g * L].rearrange("p (g t) -> p g t", g=g),
                                              cos.unsqueeze(1).to_broadcast([P, g, L]), ALU.mult).then_inc(sm["proj_free"], 1)
                        elif kind == "r":
                            g = GB * (1 if m == 2 else 2)
                            dve.wait_ge(sm["proj_full"], F)
                            dve.tensor_tensor(rt2[:, 0:g * L].rearrange("p (g t) -> p g t", g=g), ps[:, 0:g * L].rearrange("p (g t) -> p g t", g=g),
                                              sin.unsqueeze(1).to_broadcast([P, g, L]), ALU.mult).then_inc(sm["proj_free"], 1)
                            dve.wait_ge(sm["proj_free"], 2 + F)
                            dve.memset(credit[:, 7:8], 0.0).then_inc(sm["rot_ok"], 1)
                        else:
                            dve.wait_ge(sm["proj_hi"], F)
                            dve.tensor_tensor(sv[:, LO, m, 0:c.kvc * P], ps[:, 0:c.kvc * P], sv[:, HI, m, 0:c.kvc * P],
                                              ALU.subtract).then_inc(sm["proj_free"], 1)
                    elif what == "qx":
                        spread(dve, t0, c, n, U, par, HI).then_inc(sm["qm_ok"], 1)
                    elif what == "scores":
                        Q, s = t0["exp_ok"] + U * UNITS + n, n % SCB
                        dve.wait_ge(sm["s_full"], t0["s_full"] + U * UNITS + (n + 1))
                        rows = score_ps[n % 2][:, :].rearrange("p (g k) -> p g k", g=HPC)
                        dve.tensor_reduce(smax[:, s], rows, AX.X, ALU.max, negate=True).then_inc(sm["nmax"], 1)
                        dve.wait_ge(sm["nmax"], t0["nmax"] + U * UNITS + (n + 1))
                        dve.tensor_tensor(sc[:, s], rows, smax[:, s].unsqueeze(2).to_broadcast([P, HPC, L]), ALU.add).then_inc(sm["shifted"], 1)
                    elif what == "sum":
                        Q, s = t0["exp_ok"] + U * UNITS + n, n % SCB
                        dve.wait_ge(sm["exp_ok"], Q + 1)
                        dve.tensor_reduce(ssum[:, s], sc[:, s], AX.X, ALU.add).then_inc(sm["summed"], 1)
                        dve.wait_ge(sm["summed"], t0["summed"] + U * UNITS + (n + 1))
                        dve.reciprocal(sinv[:, s], ssum[:, s]).then_inc(sm["rinv_ok"], 1)
                    elif what == "turn":
                        dve.wait_ge(sm["t_hi"], t0["t_hi"] + U * UNITS + (n + 1))
                        dve.tensor_tensor(spT[:, n % 2, LO], turn_ps[n % 2][:, :], spT[:, n % 2, HI], ALU.subtract).then_inc(sm["t_free"], 1)
                    elif what == "pve":
                        dve.wait_ge(sm["pv_hi"], t0["pv_hi"] + U * GT + (n + 1))
                        dve.tensor_tensor(satt[:, LO], pv_ps[:, :].rearrange("p (c t) -> p c t", c=KC), satt[:, HI],
                                          ALU.subtract).then_inc(sm["pv_free"], 1)
                    elif what == "out":
                        dve.wait_ge(sm["o_full"], t0["o_full"] + U * GT + (n + 1))
                        dve.tensor_tensor(xtile(U * GT + n), out_ps[:, :], xtile(U * GT + n), ALU.add).then_inc(sm["o_free"], 1)
                walk(dve, self_first(c), self_order, c, step)

            def ffn0(t0, c):
                weights(t0, c, fwdst)

                def step(what, n, U, par):
                    if what == "fill":
                        kind, m = c.fills[n]
                        ps = proj_ps[n % 2]
                        F = t0["proj_full"] + U * c.nf + (n + 1)
                        dve.wait_ge(sm["proj_hi"], F)
                        two = ps[:, :].rearrange("p (c t) -> p c t", c=2)
                        if kind == "u":
                            dve.wait_ge(sm["h_ok"], t0["h_ok"] + U * 4 + m)
                            dve.scalar_tensor_tensor(out=sq32, in0=ps[:, :], scalar=0.0, in1=relu32,
                                                     op0=ALU.max, op1=ALU.mult).then_inc(sm["proj_free"], 1)
                        elif kind == "f":
                            dve.tensor_tensor(fT[:, LO], two, fT[:, HI], ALU.subtract).then_inc(sm["proj_free"], 1)
                        elif kind == "e":
                            dve.tensor_tensor(eT[:, par, LO], two, eT[:, par, HI], ALU.subtract).then_inc(sm["proj_free"], 1)
                        else:
                            carry(dve, 1)
                            dve.max(top8[:, m], logits[:, m]).then_inc(sm["proj_free"], 1)
                            dve.wait_ge(sm["proj_free"], 2 + F)
                            dve.tensor_tensor(gsum[:, par, m:m + 1], top8[:, m, 0:1], top8[:, m, 1:2], ALU.add).then_inc(sm["gate_ok"], 1)
                    elif what == "down":
                        N = U * GT + n
                        dve.wait_ge(sm["gate_ok"], t0["gate_ok"] + U * GT + GT)
                        dve.wait_ge(sm["sh_ok"], t0["sh_ok"] + N + 1)
                        dve.wait_ge(sm["y_n"], t0["y_n"] + N)
                        dve.wait_ge(sm["pv_full"], t0["pv_full"] + N + 1)
                        dve.scalar_tensor_tensor(out=y32, in0=pv_ps[:, :], scalar=gsum[:, par, n:n + 1], in1=shared,
                                                 op0=ALU.mult, op1=ALU.add).then_inc(sm["pv_free"], 1)
                        dve.wait_ge(sm["pv_free"], 1 + t0["pv_full"] + N + 1)
                        dve.bn_stats(ystats, y32).then_inc(sm["y_stat"], 1)
                        dve.wait_ge(sm["y_stat"], t0["y_stat"] + N + 1)
                        carry(dve, 1)
                        dve.bn_aggr(ymv, ystats).then_inc(sm["y_mv"], 1)
                        dve.wait_ge(sm["y_mv"], t0["y_mv"] + N + 1)
                        dve.tensor_scalar(yvar, ymv[:, 1:2], EPS, None, ALU.add).then_inc(sm["y_var"], 1)
                        dve.wait_ge(sm["y_rstd"], t0["y_rstd"] + N + 1)
                        dve.wait_ge(sm["x_ok"], t0["x_ok"] + N)
                        dve.tensor_scalar(yn, y32, ymv[:, 0:1], yrstd, ALU.subtract, ALU.mult).then_inc(sm["y_n"], 1)
                walk(dve, ffn_first(c), ffn_order, c, step)

            def ffn1(t0):
                x_final(t0)
                W = wstage[:, 0, :]
                link = [0]

                def chain(ins):
                    link[0] += 1
                    ins.then_inc(sm["wm"], 1)
                    dve.wait_ge(sm["wm"], link[0])
                dve.wait_ge(sm["wt_in"], 32)
                dve.tensor_reduce(wabs, W, AX.X, ALU.add, apply_absolute_value=True).then_inc(sm["wsum"], 1)
                dve.wait_ge(sm["wsum_ps"], 1)
                chain(dve.tensor_scalar(wmean, out_ps[:, 0:1], 1.0 / (D * D), EPS, ALU.mult, ALU.max))
                chain(dve.reciprocal(winv, wmean))
                chain(dve.tensor_scalar(tw32, W, winv, ROUND, ALU.mult, ALU.add))
                chain(dve.tensor_scalar(tw32, tw32, ROUND, 1.0, ALU.subtract, ALU.min))
                dve.tensor_scalar(tw.rearrange("p k m -> p (k m)"), tw32, -1.0, None, ALU.max).then_inc(sm["wt_ok"], 1)
                LINKS = 7

                with dve.Fori(0, NT // PREP_T) as i:
                    N = t0["ln_stat"] + i
                    at = [0]

                    def link_(ins):
                        at[0] += 1
                        ins.then_inc(sm["d1"], 1)
                        dve.wait_ge(sm["d1"], START + i * LINKS + at[0])
                    dve.wait_ge(sm["xz_ok"], START + i * PREP_T)
                    for t in range(PREP_T):
                        s = dve.bn_stats(stats[:, t, :], xtile(i * PREP_T + t))
                    s.then_inc(sm["ln_stat"], 1)
                    dve.wait_ge(sm["ln_stat"], N + 1)
                    carry(dve, 1)
                    for t in range(PREP_T):
                        s = dve.bn_aggr(meanvar[:, t, :], stats[:, t, :])
                    s.then_inc(sm["ln_mv"], 1)
                    dve.wait_ge(sm["ln_mv"], t0["ln_mv"] + i + 1)
                    dve.tensor_scalar(vareps[:, :], meanvar[:, :, 1], EPS, None, ALU.add).then_inc(sm["ln_var"], 1)
                    dve.wait_ge(sm["ln_rstd"], t0["ln_rstd"] + i + 1)
                    for t in range(PREP_T):
                        dve.tensor_scalar(xn[:, t, :], xtile(i * PREP_T + t), meanvar[:, t, 0:1], rstd[:, t:t + 1],
                                          ALU.subtract, ALU.mult).then_inc(sm["ln_xn"], 1)
                    dve.wait_ge(sm["ln_xn"], t0["ln_xn"] + i * PREP_T + PREP_T)
                    dve.tensor_reduce(absmax, xn[:, :, :], AX.X, ALU.max, apply_absolute_value=True)
                    dve.wait_ge(sm["sumsq_ok"], START + i + 1)
                    dve.tensor_scalar(rms_in, sumsq, 1.0 / D, EPS, ALU.mult, ALU.add).then_inc(sm["rms_in"], 1)
                    dve.wait_ge(sm["rms_ok"], START + i + 1)
                    link_(dve.tensor_tensor(nmax_, absmax, rms, ALU.mult))
                    link_(dve.tensor_scalar(nmax_, nmax_, EPS, None, ALU.max))
                    link_(dve.reciprocal(ninv, nmax_))
                    dve.tensor_scalar(nfac, nmax_, 1.0 / 127.0, wmean, ALU.mult, ALU.mult)
                    link_(dve.tensor_scalar(nscale, ninv, 127.0, None, ALU.mult))
                    for t in range(PREP_T):
                        e = dve.tensor_scalar(q32[:, t, :], xn[:, t, :], rms[:, t:t + 1], nscale[:, t:t + 1], ALU.mult, ALU.mult)
                    link_(e)
                    link_(dve.tensor_scalar(q32, q32, ROUND, ROUND, ALU.add, ALU.subtract))
                    link_(dve.tensor_scalar(xq, q32, 127.0, -128.0, ALU.min, ALU.max))
                    assert at[0] == LINKS
                    dve.memset(credit[:, 7:8], 0.0).then_inc(sm["xq_ok"], 1)
                    for t in range(PREP_T):
                        if t >= 2:
                            dve_out(i, t - 2)
                        dve.wait_ge(sm["y_full"], START + i * PREP_T + (t + 1))
                        dve.scalar_tensor_tensor(out=yb[:, t % 2], in0=(pv_ps, out_ps)[t % 2][:, :], scalar=nfac[:, t:t + 1],
                                                 in1=brow, op0=ALU.mult, op1=ALU.add).then_inc(sm["y_free"], 1)
                    dve_out(i, 2)
                    dve_out(i, 3)

            def dve_out(i, t):
                dve.wait_ge(sm["gelu_ok"], START + i * PREP_T + (t + 1))
                dve.wait_ge(sm["xz_ok"], START + i * PREP_T + (t + 1))
                dve.tensor_tensor(xtile(i * PREP_T + t), xtile(i * PREP_T + t), gl[:, t % 2], ALU.add).then_inc(sm["xo_ok"], 1)

            for kind, t0, c in plan:
                if kind == "prep":
                    prep(t0)
                elif kind == "ffn1":
                    ffn1(t0)
                else:
                    {"cross": cross, "self": self_, "ffn0": ffn0}[kind](t0, c)

        @block.tensor
        def _(pe):
            pe.wait_ge(sm["ident_ok"], 4)
            pe.wait_ge(sm["bias_in"], 32)
            pe.wait_ge(sm["const_ok"], 1)

            def product(ps, stat, mov, first, last):
                for n, (s, m) in enumerate(PASSES):
                    mm = pe.matmul(ps, stat(s), mov(m), start=first and n == 0, stop=last and n == 2,
                                   skip_group_check=True)
                return mm

            def pe_start(t0):
                pe.wait_ge(sm["o_free"], 1 + t0["o_free"])
                pe.wait_ge(sm["pv_free"], 1 + t0["pv_free"])
                pe.wait_ge(sm["t_free"], 1 + t0["t_free"])
                pe.wait_ge(sm["sh_ok"], t0["sh_ok"])

            def prep(t0):
                with pe.Fori(0, NT // PREP_T) as i:
                    for t in range(PREP_T):
                        f = i * PREP_T + t
                        pe.wait_ge(sm["ln_xn"], t0["ln_xn"] + f + 1)
                        pe.wait_ge(sm["proj_free"], t0["proj_full"] + f + 1)
                        for k in range(KC):
                            mm = pe.transpose(bank[t % 2][:, k * P:(k + 1) * P], xn[:, t, k * P:(k + 1) * P], identf[:, :])
                        mm.then_inc(sm["proj_full"], 1)

            def cross(t0, c):
                hd = c.hd

                def w(t, part, k, m0, m1):
                    return t[:, part, 0:KC * (t is wq and c.nh * hd or hd)].rearrange("p (k m) -> p k m", k=KC)[:, k, m0:m1]

                def step(what, n, U, par, h, g):
                    if what in ("w", "ctx"):
                        return
                    J = U * GB + n + t0["exp_ok"]
                    if what == "fill":
                        kind, m = c.fills[n]
                        ps = proj_ps[n % 2]
                        pe.wait_ge(sm["proj_free"], t0["proj_full"] + U * c.nf + (n + 1))
                        if n == 0:
                            pe.wait_ge(xg_in[par], 8 * GT * t0["xg"] + (U - par) * (8 * GT) + 16 * GT)
                            pe.wait_ge(sm["w_free"], 2 + t0["w_hi"] + h * c.nw + len(c.proj_w))
                        if kind == "kc":
                            pe.wait_ge(sm["ctx_ok"], t0["ctx_ok"] + U * KC + KC)
                        if kind == "q":
                            for j in range(2):
                                hh = 2 * m + j
                                for k in range(KC):
                                    mm = product(ps[0:hd, j * GB * L:(j + 1) * GB * L],
                                                 lambda s: w(wq, s, k, hh * hd, (hh + 1) * hd),
                                                 lambda s: xg[:, par, :, s, k, :], k == 0, k == KC - 1)
                        elif kind == "kc":
                            for k in range(KC):
                                mm = product(ps[0:hd, :], lambda s: w(wk, s, k, 0, hd), lambda s: cT[:, par, s, k, :],
                                             k == 0, k == KC - 1)
                        elif kind == "kl":
                            for k in range(KC):
                                mm = product(ps[0:hd, 0:GB * L], lambda s: w(wk, s, k, 0, hd),
                                             lambda s: xg[:, par, :, s, k, :], k == 0, k == KC - 1)
                        elif kind == "vc":
                            for b in range(GB):
                                for k in range(KC):
                                    mm = product(ps[:, b * hd:(b + 1) * hd], lambda s: cT[:, par, s, k, b * S:(b + 1) * S],
                                                 lambda s: w(wv, s, k, 0, hd), k == 0, k == KC - 1)
                        else:
                            for t in range(GT):
                                for k in range(KC):
                                    mm = product(ps[:, t * hd:(t + 1) * hd], lambda s: xg[:, par, t, s, k, :],
                                                 lambda s: w(wv, s, k, 0, hd), k == 0, k == KC - 1)
                        mm.then_inc(sm["proj_full"], 1)
                    elif what == "scores":
                        if n == 0:
                            pe.wait_ge(sm["proj_free"], 2 + t0["proj_full"] + U * c.nf + c.nqk)
                        pe.wait_ge(sm["exp_ok"], J)
                        for j in range(c.pairs):
                            mm = product(score_ps[j // 2][:, (j % 2) * KEYS:(j % 2 + 1) * KEYS],
                                         lambda s: q_view(c, par, s)[:, n, 2 * j:2 * j + 2, :].rearrange("p h t -> p (h t)"),
                                         lambda s: kT[0:hd, par, s, n, :], True, True)
                            if j % 2 == 1:
                                mm.then_inc(sm["s_full"], 1)
                    elif what == "turn":
                        pe.wait_ge(sm["p_ok"], J + 1)
                        pe.wait_ge(sm["t_free"], J + 1)
                        c0 = S if n % 2 == 0 else L
                        w_ = L if n % 2 == 0 else P
                        for j in range(c.pairs):
                            pe.transpose(turn_ps[0][:, j * P:(j + 1) * P], probs[:, n % 2, j, 0:S], identf[:, :])
                            mm = pe.transpose(turn_ps[1][0:w_, j * P:(j + 1) * P], probs[:, n % 2, j, c0:c0 + w_], identf[:, :])
                        mm.then_inc(sm["t_full"], 1)
                    elif what == "pv":
                        pe.wait_ge(sm["t_free"], J + 2)
                        if n == 0:
                            pe.wait_ge(sm["proj_free"], 2 + t0["proj_full"] + U * c.nf + c.nf)
                        pe.wait_ge(sm["pv_free"], t0["pv_free"] + U * GB + (n + 1))
                        m = c.nh * L
                        product(pv_ps[0:hd, 0:m], lambda s: v_view(c, par, s)[:, n, :], lambda s: pT1[:, s, 0:m], True, False)
                        product(pv_ps[0:hd, 0:m], lambda s: v_view(c, par, s)[:, GB + n // 2, :],
                                lambda s: pT2[:, n % 2, s, 0:m], False, True).then_inc(sm["pv_full"], 1)
                    elif what == "out":
                        pe.wait_ge(sm["pv_free"], U * GB + t0["pv_free"] + (2 * n + 3))
                        pe.wait_ge(sm["o_free"], t0["o_free"] + U * GT + (n + 1))
                        if n == 0:
                            pe.wait_ge(sm["w_free"], 2 + t0["w_hi"] + h * c.nw + c.nw)
                        for q_ in range(c.nh):
                            mm = product(out_ps[:, :], lambda s: att[0:hd, s, q_ * P:(q_ + 1) * P],
                                         lambda s: wo[0:hd, s, q_ * D:(q_ + 1) * D], q_ == 0, q_ == c.nh - 1)
                        mm.then_inc(sm["o_full"], 1)

                pe_start(t0)
                cross_walk(c, pe, step)

            def self_(t0, c):
                pe_start(t0)
                pe.wait_ge(sm["w_free"], 2 + t0["w_hi"] + len(c.chunks))
                kw = c.kvc * P

                def step(what, n, U, par):
                    if what == "fill":
                        kind, m = c.fills[n]
                        ps = proj_ps[n % 2]
                        pe.wait_ge(sm["proj_free"], t0["proj_free"] + U * c.nf + (n + 1))
                        if n == 0:
                            pe.wait_ge(xg_in[par], 8 * GT * t0["xg"] + (U - par) * (8 * GT) + 16 * GT)
                        if kind in "qk":
                            w = sw["wq" if kind == "q" else "wk"]
                            for j in range(1 if kind == "k" and c.rope else 2):
                                ch = 2 * m + j
                                for k in range(KC):
                                    mm = product(ps[:, j * GT * P:(j + 1) * GT * P], lambda s: w[:, s, k, ch * P:(ch + 1) * P],
                                                 lambda s: xg[:, par, :, s, k, :], k == 0, k == KC - 1)
                        elif kind == "r":
                            wd = GT * P * (1 if m == 2 else 2)
                            pe.wait_ge(sm["proj_hi"], t0["proj_hi"] + U * c.nf + n)
                            mm = pe.matmul(ps[:, 0:wd], perm, raw32[:, 0:wd], start=True, stop=True)
                        else:
                            for k in range(KC):
                                mm = product(ps[:, 0:kw], lambda s: xg[:, par, m, s, k, :], lambda s: sw["wv"][:, s, k, 0:kw],
                                             k == 0, k == KC - 1 and c.rope)
                            if not c.rope:
                                for s in (HI, LO):
                                    mm = pe.matmul(ps[:, :], row0[:, :], sw["bv"][:, s, 0, :], start=False, stop=s == LO,
                                                   skip_group_check=True)
                        mm.then_inc(sm["proj_full"], 1)
                    elif what == "scores":
                        _, tile, bt, c0 = unit(n)
                        pe.wait_ge(sm["shifted"], t0["shifted"] + U * UNITS + n - 1)
                        if n % 4 == 0:
                            pe.wait_ge(sm["qm_ok"], t0["qm_ok"] + U * (GT * QX) + (tile + 1) * QX)
                            pe.wait_ge(sm["qlo_ok"], t0["qlo_ok"] + U * (GT * QX) + (tile + 1) * QX)
                            pe.wait_ge(sm["proj_free"], 2 + t0["proj_free"] + U * c.nf + c.nf)
                            if c.rope:
                                pe.wait_ge(sm["rope_lo"], t0["rope_lo"] + U * c.nrope + c.nrope)
                        tok = (tile * 2 + bt) * L
                        pe.matmul(score_ps[n % 2][:, :], identb[:, :], maskb[:, :].unsqueeze(1).to_broadcast([P, HPC, L]), start=True, stop=False, skip_group_check=True)
                        for ci in range(2):
                            for t in range(2):
                                for j in range(2):
                                    at = ((ci * 2 + t) * 2 + j) * L
                                    kc = 0 if c.rope else c0 + ci
                                    mm = product(score_ps[n % 2][:, at:at + L],
                                                 lambda s: qm[:, tile, s, c0 + ci, bt, 4 * j + 2 * t:4 * j + 2 * t + 2, :].rearrange("p h t -> p (h t)"),
                                                 lambda s: sk[:, par, s, kc, tok:tok + L], False, True)
                        mm.then_inc(sm["s_full"], 1)
                    elif what == "turn":
                        pe.wait_ge(sm["p_ok"], t0["p_ok"] + U * UNITS + (n + 1))
                        pe.wait_ge(sm["t_free"], t0["t_free"] + U * UNITS + n)
                        for g in range(4):
                            mm = pe.transpose(turn_ps[n % 2][:, g * P:(g + 1) * P],
                                              sc[:, n % SCB, 2 * g:2 * g + 2, :].rearrange("p g k -> p (g k)"), identf[:, :])
                        mm.then_inc(sm["t_full"], 1)
                    elif what == "pv":
                        _, tile, bt, c0 = unit(n)
                        pe.wait_ge(sm["t_free"], 2 + t0["t_free"] + U * UNITS + n)
                        if n % 4 == 0:
                            pe.wait_ge(sm["vx_ok"], t0["vx_ok"] + U * (GT * 2) + (tile + 1) * 2)
                            pe.wait_ge(sm["pv_free"], t0["pv_free"] + U * GT + (tile + 1))
                        for ci in range(2):
                            at = (c0 + ci) * P + bt * L
                            for th in range(4):
                                kc = 0 if c.rope else c0 + ci
                                col = (ci * 4 + th) * L
                                mm = product(pv_ps[:, at:at + L], lambda s: vx[:, tile, s, bt, kc, th, :],
                                             lambda s: spT[:, n % 2, s, col:col + L], th == 0, th == 3)
                        if n % 4 == 3:
                            mm.then_inc(sm["pv_full"], 1)
                    elif what == "out":
                        pe.wait_ge(sm["pv_free"], 1 + t0["pv_free"] + U * GT + (n + 1))
                        pe.wait_ge(sm["o_free"], t0["o_free"] + U * GT + (n + 1))
                        for k in range(KC):
                            mm = product(out_ps[:, :], lambda s: satt[:, s, k, :], lambda s: sw["wo"][:, s, k, :],
                                         k == 0, k == KC - 1 and c.rope)
                        if not c.rope:
                            for s in (HI, LO):
                                mm = pe.matmul(out_ps[:, :], row0[:, :], sw["bo"][:, s, 0, :], start=False, stop=s == LO,
                                               skip_group_check=True)
                        mm.then_inc(sm["o_full"], 1)
                walk(pe, self_first(c), self_order, c, step)

            def ffn0(t0, c):
                pe_start(t0)
                pe.wait_ge(sm["w_free"], 2 + t0["w_hi"] + len(c.chunks))

                def step(what, n, U, par):
                    if what == "fill":
                        kind, m = c.fills[n]
                        ps = proj_ps[n % 2]
                        pe.wait_ge(sm["proj_free"], t0["proj_free"] + U * c.nf + (n + 1))
                        if n == 0:
                            pe.wait_ge(xg_in[par], 8 * GT * t0["xg"] + (U - par) * (8 * GT) + 16 * GT)
                        if kind in "uf":
                            w = fw["up" if kind == "u" else "fc1"]
                            for j in range(2):
                                ch = 2 * m + j
                                for k in range(KC):
                                    mm = product(ps[:, j * GT * P:(j + 1) * GT * P], lambda s: w[:, s, k, ch * P:(ch + 1) * P],
                                                 lambda s: xg[:, par, :, s, k, :], k == 0, k == KC - 1)
                        elif kind == "e":
                            pe.wait_ge(sm["proj_free"], 2 + t0["proj_free"] + U * c.nf + 1)
                            for j in range(2):
                                for k in range(2):
                                    mm = product(ps[:, j * GT * P:(j + 1) * GT * P],
                                                 lambda s: fw["expert"][:, s, k, j * P:(j + 1) * P],
                                                 lambda s: fT[:, s, k, :], k == 0, k == 1)
                        else:
                            for k in range(KC):
                                mm = product(ps[:, 0:8], lambda s: xg[:, par, m, s, k, :], lambda s: fw["gate"][:, s, k, :],
                                             k == 0, k == KC - 1)
                        mm.then_inc(sm["proj_full"], 1)
                    elif what == "down":
                        N = U * GT + n
                        pe.wait_ge(sm["h_ok"], t0["h_ok"] + U * 4 + 4)
                        pe.wait_ge(sm["proj_free"], 2 + t0["proj_free"] + U * c.nf + 6)
                        pe.wait_ge(sm["sh_ok"], t0["sh_ok"] + N)
                        for k in range(8):
                            mm = product(out_ps[:, :], lambda s: hT[:, par, s, k, n * P:(n + 1) * P],
                                         lambda s: fw["down"][:, s, k, :], k == 0, k == 7)
                        mm.then_inc(sm["o_full"], 1)
                        pe.wait_ge(sm["pv_free"], t0["pv_free"] + N + 1)
                        for k in range(2):
                            mm = product(pv_ps[:, :], lambda s: eT[:, par, s, k, n * P:(n + 1) * P],
                                         lambda s: fw["fc2"][:, s, k, :], k == 0, k == 1)
                        mm.then_inc(sm["pv_full"], 1)
                walk(pe, ffn_first(c), ffn_order, c, step)

            def ffn1(t0):
                pe_start(t0)
                pe.wait_ge(sm["proj_free"], 2 + t0["proj_free"])
                pe.wait_ge(sm["wsum"], 1)
                pe.wait_ge(sm["zero_ok"], t0["zero_ok"] + 1)
                pe.matmul(out_ps[:, 0:1], ones, wabs, start=True, stop=True).then_inc(sm["wsum_ps"], 1)
                pe.wait_ge(sm["wt_ok"], 1)

                def turn(i, t):
                    if t < 2:
                        pe.wait_ge(sm["q_evac"], START + i * PREP_T)
                    else:
                        pe.wait_ge(sm["q_evac"], START + i * PREP_T + (t - 1))
                    for k in range(KC):
                        mm = pe.transpose(bank[t % 2][:, k * P // 2:(k + 1) * P // 2].bitcast(BF16), xq[:, t, k * P:(k + 1) * P], identb[:, :])
                    mm.then_inc(sm["q_turn"], 1)

                with pe.Fori(0, NT // PREP_T) as i:
                    pe.wait_ge(sm["xq_ok"], START + i + 1)
                    turn(i, 0)
                    for t in range(PREP_T):
                        if t + 1 < PREP_T:
                            turn(i, t + 1)
                        pe.wait_ge(sm["q_evac"], START + i * PREP_T + (t + 1))
                        pe.wait_ge(sm["y_free"], START + i * PREP_T + max(t - 1, 0))
                        for k in range(KC):
                            mm = pe.matmul((pv_ps, out_ps)[t % 2][:, :], xqT[:, t % 2, k, :], tw[:, k, :], start=k == 0, stop=k == KC - 1)
                        mm.then_inc(sm["y_full"], 1)

            for kind, t0, c in plan:
                if kind == "prep":
                    prep(t0)
                elif kind == "ffn1":
                    ffn1(t0)
                else:
                    {"cross": cross, "self": self_, "ffn0": ffn0}[kind](t0, c)


def _consts():
    p = np.arange(P)
    hmask = (p[:, None] // HD == np.arange(HPC)[None, :]).astype(np.float32)
    cmask = np.where(np.arange(L)[None, :] <= (p[:, None] % L), 0.0, -1e30).astype(np.float32)
    swap = (p // HD) * HD + (p % HD + HD // 2) % HD
    perm = np.zeros((P, P), np.float32)
    perm[swap, p] = 1.0
    f32 = np.float32
    theta, factor, hi_f, lo_f, l0 = 500000.0, 32.0, 4.0, 1.0, 1024
    idx = np.arange(0, HD, 2, dtype=f32) / f32(HD)
    freq = (f32(1.0 / (2.0 * np.pi)) * np.power(f32(theta), -idx)).astype(f32)
    low, high = lo_f / l0, hi_f / l0
    scaled = np.where(freq < low, freq / f32(factor), freq)
    smooth = np.clip((l0 * freq - lo_f) / (hi_f - lo_f), 0.0, 1.0).astype(f32)
    mixed = (1 - smooth) * (freq / f32(factor)) + smooth * freq
    freq = np.where((freq >= low) & (freq <= high), mixed, scaled).astype(f32)
    phase = (f32(2.0 * np.pi) * np.arange(L, dtype=f32)[None, :] * freq[p % (HD // 2)][:, None]).astype(f32)
    sign = np.where(p % HD < HD // 2, -1.0, 1.0)[:, None]
    return np.concatenate([hmask, cmask, perm, np.cos(phase), np.sin(phase) * sign], axis=1).astype(f32)


def _layout(inputs):
    def f(n):
        return np.asarray(inputs[n])
    arr = {
        "x": f("x").reshape(B * L, D),
        "ctxT": f("ctx_4096").reshape(B * S, D).T,
        "L0_xattn_Wq": f("L0_xattn_Wq").T, "L0_xattn_Wk": f("L0_xattn_Wk").T,
        "L0_xattn_Wv": f("L0_xattn_Wv").T, "L0_xattn_Wo": f("L0_xattn_Wo").T,
        "L1_xattn_Wq": f("L1_xattn_Wq"), "L1_xattn_Wk": f("L1_xattn_Wk"),
        "L1_xattn_Wv": f("L1_xattn_Wv"), "L1_xattn_Wo": f("L1_xattn_Wo"),
        "L1_ffn_W": f("L1_ffn_W").T, "L1_ffn_b": f("L1_ffn_b"), "consts": _consts(),
    }
    for n in ("Wq", "Wk", "Wv", "Wo"):
        arr["L0_attn_" + n] = f("L0_attn_" + n).T
    for n in ("bv", "bo"):
        arr["L0_attn_" + n] = f("L0_attn_" + n)
    arr["L0_attn_bqk"] = np.stack([f("L0_attn_bq").reshape(KC, P).T, f("L0_attn_bk").reshape(KC, P).T], axis=1)
    for n in ("gate_w", "up_w", "down_w", "fc1_w", "fc2_w", "expert_w", "ln_gamma", "ln_beta"):
        arr["L0_ffn_" + n] = f("L0_ffn_" + n)
    arr["L1_attn_Wq"] = f("L1_attn_Wq").reshape(D, 8, 4, HD).transpose(0, 2, 1, 3).reshape(D, D)
    arr["L1_attn_Wo"] = f("L1_attn_Wo").reshape(8, 4, HD, D).transpose(1, 0, 2, 3).reshape(D, D)
    arr["L1_attn_Wk"], arr["L1_attn_Wv"] = f("L1_attn_Wk"), f("L1_attn_Wv")
    return {k: np.ascontiguousarray(v) for k, v in arr.items()}


def kernel(**inputs):
    import concourse.bacc as _bacc
    from concourse.bass_utils import run_bass_kernel_spmd as _run

    nc = _bacc.Bacc("TRN2", target_bir_lowering=False, num_devices=1)
    arr = _layout(inputs)
    aps = {k: nc.dram_tensor(f"in_{k}", v.shape, mybir.dt.from_np(v.dtype), kind="ExternalInput").ap()
           for k, v in arr.items()}
    out = nc.dram_tensor("out_x", (B * L, D), F32, kind="ExternalOutput").ap()
    build(nc, aps, out)
    r = _run(nc, [{f"in_{k}": v for k, v in arr.items()}], core_ids=[0])
    return r.results[0]["out_x"].reshape(B, L, D)
```

```python
from contextlib import ExitStack

import numpy as np

import concourse.bass as bass
from concourse import mybir

F32 = mybir.dt.float32
BF16 = mybir.dt.bfloat16
ALU = mybir.AluOpType
ACT = mybir.ActivationFunctionType
AX = mybir.AxisListType

P = 128
B, L, D = 32, 64, 512
S = 128
KC = D // P
NT = B * L // P
GB = 4
GT = GB * L // P
NG = B // GB
KV = 4
KEYS = S + L
EPS = 1e-5
HI, LO = 0, 1
PASSES = ((HI, HI), (HI, LO), (LO, HI))
PREP_T = 4
QUADS = NT // PREP_T
XT = 4


class Cross:

    def __init__(self, name, heads, hd):
        self.name, self.hd = name, hd
        self.nh = heads // KV
        self.pairs = self.nh // 2
        self.sbanks = self.pairs // 2
        self.scale = float(hd) ** -0.5
        self.fills = [("q", n) for n in range(self.nh // 2)] + [("kc", 0), ("kl", 0), ("vc", 0), ("vl", 0)]
        self.nf = len(self.fills)
        self.nqk = self.nf - 2
        if self.nh * hd * KC > 2048:
            self.chunks = [("wq", 0, 2), ("wq", 2, 2), ("wk", 0, KC), ("wv", 0, KC),
                           ("wo", 0, self.nh // 2), ("wo", self.nh // 2, self.nh // 2)]
        else:
            self.chunks = [("wq", 0, KC), ("wk", 0, KC), ("wv", 0, KC), ("wo", 0, self.nh)]
        self.nw = len(self.chunks)
        self.proj_w = [n for n in range(self.nw) if self.chunks[n][0] != "wo"]
        self.out_w = [n for n in range(self.nw) if self.chunks[n][0] == "wo"]


class Self:

    def __init__(self, name, rope):
        self.name, self.rope = name, rope
        self.kvc = 1 if rope else KC
        if rope:
            self.fills = [("q", 0), ("r", 0), ("q", 1), ("r", 1), ("k", 0), ("r", 2), ("v", 0), ("v", 1)]
            self.chunks = [("wq", 0, KC), ("wk", 0, KC), ("wv", 0, KC), ("wo", 0, KC)]
        else:
            self.fills = [("q", 0), ("q", 1), ("k", 0), ("k", 1), ("v", 0), ("v", 1)]
            self.chunks = [("wq", 0, KC), ("wk", 0, KC), ("wv", 0, KC), ("wo", 0, KC), ("bv", 0, 1), ("bo", 0, 1)]
        self.nf = len(self.fills)
        self.nrope = 3 if rope else 0


class Ffn:
    name = "L0_ffn"
    hidden, lat, experts = 1024, 256, 8
    fills = [("f", 0), ("u", 0), ("u", 1), ("u", 2), ("u", 3), ("e", 0), ("g", 0), ("g", 1)]
    nf = len(fills)
    chunks = [("up", 0, 2), ("up", 2, 2), ("fc1", 0, KC), ("gate", 0, KC), ("expert", 0, 2),
              ("fc2", 0, 2), ("down", 0, 4), ("down", 4, 4)]


A0 = Self("L0_attn", False)
A1 = Self("L1_attn", True)
F0 = Ffn()
HPC = 8
HD = 16
UNITS = 2 * GB
QX = 4
SCB = 4
ROUND = 1.5 * 2.0 ** 23
X0 = Cross("L0_xattn", 16, 96)
X1 = Cross("L1_xattn", 32, 128)


def build(nc, a, out, layers=6):
    ctx = ExitStack()
    with ctx:
        def sb(name, shape, dt):
            return ctx.enter_context(nc.sbuf_tensor(name, shape, dt))

        def sem(name):
            return ctx.enter_context(nc.semaphore(name))

        bank = [ctx.enter_context(nc.psum_tensor(f"bank{i}", [P, 512], F32)) for i in range(8)]
        proj_ps, score_ps, turn_ps, pv_ps, out_ps = bank[0:2], bank[2:4], bank[4:6], bank[6], bank[7]

        scratch = nc.dram_tensor("xn_scratch", (NT, P, 2, KC, P), BF16).ap()

        X = sb("X", [P, NT, D], F32)
        identf = sb("identf", [P, P], F32)
        neghalf = sb("neghalf", [P, NT], F32)
        credit = sb("credit", [P, 8], F32)
        carrier = sb("carrier", [P, 8], F32)
        scales = sb("scales", [P, 4], F32)
        stats = sb("stats", [P, NT, 6], F32)
        meanvar = sb("meanvar", [P, NT, 2], F32)
        vareps = sb("vareps", [P, NT], F32)
        rstd = sb("rstd", [P, NT], F32)
        xn = sb("xn", [P, PREP_T, D], F32)
        wstage = sb("wstage", [P, 2, 2048], F32)
        xg = sb("xg", [P, 2, GT, 2, KC, P], BF16)
        consts = sb("consts", [P, 8 + 64 + 128 + 64 + 64], F32)
        hmask, cmask, perm = consts[:, 0:8], consts[:, 8:72], consts[:, 72:200]
        cos, sin = consts[:, 200:264], consts[:, 264:328]
        row0 = sb("row0", [P, P], BF16)
        identb = sb("identb", [P, P], BF16)
        maskb = sb("maskb", [P, L], BF16)
        bqk = sb("bqk", [P, 2, KC], F32)

        ARENA = 71808
        arena = sb("arena", [P, ARENA], BF16)

        class Carve:
            def __init__(self):
                self.at = 0

            def __call__(self, shape, dt):
                n = int(np.prod(shape)) * (2 if dt == F32 else 1)
                ap = arena[:, self.at:self.at + n]
                self.at += n
                assert self.at <= ARENA, self.at
                if dt == F32:
                    ap = ap.bitcast(F32)
                if len(shape) > 1:
                    names = "abcdefg"[:len(shape)]
                    ap = ap.rearrange("p (" + " ".join(names) + ") -> p " + " ".join(names),
                                      **{k: v for k, v in zip(names[1:], shape[1:])})
                return ap

        cv = Carve()
        cv.at = ARENA - XT * 2 * KC * P
        xt = cv([XT, 2, KC, P], BF16)
        cv = Carve()
        wq = cv([2, KC * 1024], BF16)
        wk = cv([2, KC * P], BF16)
        wv = cv([2, KC * P], BF16)
        wo = cv([2, 8 * D], BF16)
        cstage = cv([2, KC, GB * S], F32)
        cT = cv([2, 2, KC, GB * S], BF16)
        q = cv([2, 2, GB * 8 * L], BF16)
        kT = cv([2, 2, GB, KEYS], BF16)
        v = cv([2, 2, (GB + GT) * P], BF16)
        negmax, nbias, rowsum, rinv = cv([2, 4], F32), cv([2, 4], F32), cv([2, 4], F32), cv([2, 4], F32)
        probs = cv([2, 4, KEYS], F32)
        pT1 = cv([2, 512], BF16)
        pT2 = cv([2, 2, 512], BF16)
        att = cv([2, 8 * P], BF16)

        cv = Carve()
        sw = {n: cv([2, KC, D], BF16) for n in ("wq", "wk", "wv", "wo")}
        shared_at = cv.at
        sw.update({n: cv([2, 1, D], BF16) for n in ("bv", "bo")})
        cv.at = shared_at
        raw32, rt1, rt2 = cv([512], F32), cv([512], F32), cv([512], F32)
        vx_at = cv.at
        vx = cv([2, 2, 2, KC, 4, P], BF16)
        qm = cv([2, 2, KC, 2, HPC, L], BF16)
        sq = cv([2, 2, KC, GT * P], BF16)
        sk = cv([2, 2, KC, GT * P], BF16)
        sv = cv([2, GT, D], BF16)
        sc = cv([SCB, HPC, L], F32)
        spT = cv([2, 2, 512], BF16)
        satt = cv([2, KC, P], BF16)
        smax, ssum, sinv = cv([SCB, 8], F32), cv([SCB, 8], F32), cv([SCB, 8], F32)
        cv = Carve()
        fw = {"up": cv([2, KC, Ffn.hidden], BF16), "fc1": cv([2, KC, Ffn.lat], BF16),
              "gate": cv([2, KC, Ffn.experts], BF16), "expert": cv([2, 2, Ffn.lat], BF16),
              "fc2": cv([2, 2, D], BF16), "down": cv([2, Ffn.hidden // P, D], BF16)}
        hT = cv([2, 2, 8, GT * P], BF16)
        fT = cv([2, 2, GT * P], BF16)
        eT = cv([2, 2, 2, GT * P], BF16)
        relu32, sq32 = cv([512], F32), cv([512], F32)
        logits, top8 = cv([2, 8], F32), cv([2, 8], F32)
        gsum = cv([2, GT], F32)
        shared, y32, yn = cv([D], F32), cv([D], F32), cv([D], F32)
        ystats, ymv, yvar, yrstd = cv([6], F32), cv([2], F32), cv([1], F32), cv([1], F32)
        gamma, beta = cv([D], F32), cv([D], F32)
        cv = Carve()
        tw = cv([KC, D], BF16)
        tw32 = cv([KC * D], F32)
        ones = cv([P], F32)
        wabs, wmean, winv = cv([1], F32), cv([1], F32), cv([1], F32)
        brow = cv([D], F32)
        junk = cv([PREP_T, D], F32)
        sumsq, absmax, rms_in, rms = cv([PREP_T], F32), cv([PREP_T], F32), cv([PREP_T], F32), cv([PREP_T], F32)
        nmax_, ninv, nscale, nfac = cv([PREP_T], F32), cv([PREP_T], F32), cv([PREP_T], F32), cv([2, PREP_T], F32)
        q32 = cv([PREP_T, D], F32)
        zn = cv([2, PREP_T, D], F32)
        xq = cv([2, PREP_T, D], BF16)
        xqT = cv([2, KC, P], BF16)
        yb, gl = cv([2, D], F32), cv([2, D], F32)

        names = ("ident_set ident_ok const_ok x_out ln_stat ln_mv ln_var ln_rstd ln_xn w_hi w_free ctx_hi "
                 "ctx_ok proj_full proj_hi proj_free s_full nmax nbias_ok exp_ok rinv_ok p_ok t_full t_hi "
                 "t_free pv_full pv_hi pv_free o_full o_free bias_in shifted summed qm_ok qlo_ok qlo2_ok vx_ok "
                 "rope_ok rope_lo zero_ok rot_ok h_hi h_ok gate_ok sh_ok y_stat y_mv y_var y_rstd y_n y_g y_b "
                 "x_ok gb_in wt_in wsum wsum_ps wm wt_ok sumsq_ok rms_in rms_ok d1 xq_ok q_turn q_evac y_full "
                 "y_free gelu_ok xz_ok xo_ok").split()
        sm = {n: sem(n) for n in names}
        w_in = [sem("w_in0"), sem("w_in1")]
        xg_in = [sem("xg_in0"), sem("xg_in1")]
        ctx_in = [sem("ctx_in0"), sem("ctx_in1")]
        xt_out = [sem(f"xt_out{n}") for n in range(XT)]
        x_in = [sem(f"x_in{n}") for n in range(NT // PREP_T)]

        START = 1
        once = "ident_set ident_ok const_ok x_out bias_in wt_in gb_in wsum wsum_ps wm wt_ok".split()
        done = {n: 0 if n in once else START for n in sm}
        done["xg"] = done["ctx"] = 0
        plan = []
        OWN_STATS = (0, 3)

        def block_of(kind, c, **raised):
            plan.append((kind, dict(done), c))
            for n, k in raised.items():
                done[n] += k

        for n in range(layers):
            if n < 5:
                c = (X0, A0, F0, X1, A1)[n]
                block_of("prep", c, ln_stat=NT if n in OWN_STATS else 0, ln_mv=1, ln_var=1, ln_rstd=1, ln_xn=NT, proj_full=NT, proj_hi=NT,
                         proj_free=NT, w_hi=len(c.chunks), w_free=len(c.chunks))
            if n in (0, 3):
                c = X0 if n == 0 else X1
                f, j, t = KV * NG * c.nf, KV * B, KV * NT
                block_of("cross", c, ln_stat=NT, proj_full=f, proj_hi=f, proj_free=f, s_full=j * c.sbanks, nmax=j,
                         nbias_ok=j, exp_ok=j, rinv_ok=j, p_ok=j, t_full=j, t_hi=j, t_free=j,
                         pv_full=j, pv_hi=j, pv_free=j, o_full=t, o_free=t, w_hi=(KV - 1) * c.nw,
                         w_free=(KV - 1) * c.nw, ctx_hi=KV * NG * KC, ctx_ok=KV * NG * KC, ctx=KV * NG, xg=KV * NG, zero_ok=2)
            if n in (1, 4):
                c = A0 if n == 1 else A1
                f, j = NG * c.nf, NG * UNITS
                block_of("self", c, ln_stat=NT, proj_full=f, proj_hi=f, proj_free=f, s_full=j, nmax=j, summed=j, shifted=j,
                         qlo_ok=NT * QX, qlo2_ok=NT * QX, exp_ok=j, rinv_ok=j, p_ok=j, t_full=j, t_hi=j, t_free=j,
                         pv_full=NT, pv_hi=NT, pv_free=NT, o_full=NT, o_free=NT, xg=NG, qm_ok=NT * QX, vx_ok=NT * 2,
                         rope_ok=NG * c.nrope, rot_ok=NG * c.nrope, rope_lo=NG * c.nrope, zero_ok=1)
            if n == 2:
                c = F0
                f = NG * c.nf
                block_of("ffn0", c, proj_full=f, proj_hi=f, proj_free=f, h_hi=NG * 4, h_ok=NG * 4, gate_ok=NT,
                         o_full=NT, pv_full=NT, pv_free=NT, sh_ok=NT, y_stat=NT, y_mv=NT, y_var=NT,
                         y_rstd=NT, y_n=NT, y_g=NT, y_b=NT, x_ok=NT, xg=NG)
            if n == 5:
                block_of("ffn1", None)

        def wchunk(c, part, name, i, n):
            hd = c.hd
            if name == "wq":
                w = wq[:, part, 0:KC * c.nh * hd].rearrange("p (k m) -> p k m", k=KC)
                return w[:, i:i + n, :], P, c.nh * hd
            if name in ("wk", "wv"):
                w = (wk if name == "wk" else wv)[:, part, 0:KC * hd].rearrange("p (k m) -> p k m", k=KC)
                return w[:, i:i + n, :], P, hd
            w = wo[0:hd, part, 0:c.nh * D].rearrange("p (h m) -> p h m", h=c.nh)
            return w[:, i:i + n, :], hd, D

        def chunk_dst(c, part, n):
            dst = wchunk if isinstance(c, Cross) else fwdst if isinstance(c, Ffn) else swdst
            name, i, k = c.chunks[n]
            d, rows, m = dst(c, part, name, i, k)
            return d, stage_of(n % 2, rows, k, m)

        def prep_order(c):
            order = [("stats", 0), ("w", 0), ("w", 1), ("xn", 0), ("xn", 1)]
            for f in range(NT):
                if f + 2 < NT:
                    order.append(("xn", f + 2))
                order.append(("tile", f))
                if f % 4 == 3 and 2 + f // 4 < len(c.chunks):
                    order.append(("w", 2 + f // 4))
            return order + [("w", n) for n in range(2 + NT // 4, len(c.chunks))]

        def w_split_hi(act, t0w, c, n, h):
            act.wait_ge(w_in[n % 2], 8 * (t0w - START) + h * (8 * len(c.chunks)) + 16 * (n // 2 + 1))
            d, stage = chunk_dst(c, HI, n)
            act.activation(d, stage, ACT.Copy).then_inc(sm["w_hi"], 1)

        def w_split_lo(dve, t0w, c, n, h):
            dve.wait_ge(sm["w_hi"], t0w + h * len(c.chunks) + (n + 1))
            hi, stage = chunk_dst(c, HI, n)
            lo, _ = chunk_dst(c, LO, n)
            dve.tensor_tensor(lo, stage, hi, ALU.subtract).then_inc(sm["w_free"], 1)

        def stage_of(slot, rows, n, m):
            return wstage[0:rows, slot, 0:n * m].rearrange("p (k m) -> p k m", k=n)

        def q_view(c, par, part):
            return q[0:c.hd, par, part, 0:GB * c.nh * L].rearrange("p (b h t) -> p b h t", b=GB, h=c.nh)

        def v_view(c, par, part):
            return v[:, par, part, 0:(GB + GT) * c.hd].rearrange("p (n m) -> p n m", m=c.hd)

        def fill_io(c, fill, par, part):
            def views(ps):
                kind, n = fill
                hd = c.hd
                if kind == "q":
                    return (ps[0:hd, :].rearrange("p (h b t) -> p h b t", h=2, b=GB),
                            q_view(c, par, part)[:, :, 2 * n:2 * n + 2, :].rearrange("p b h t -> p h b t"))
                if kind == "kc":
                    return ps[0:hd, :].rearrange("p (b t) -> p b t", b=GB), kT[0:hd, par, part, :, 0:S]
                if kind == "kl":
                    return (ps[0:hd, 0:GB * L].rearrange("p (b t) -> p b t", b=GB),
                            kT[0:hd, par, part, :, S:KEYS])
                if kind == "vc":
                    return (ps[:, 0:GB * hd].rearrange("p (b t) -> p b t", b=GB), v_view(c, par, part)[:, 0:GB, :])
                return (ps[:, 0:GT * hd].rearrange("p (b t) -> p b t", b=GT),
                        v_view(c, par, part)[:, GB:GB + GT, :])
            return views

        def cross_order(c, fill, ctx, seam):
            order, fills = [], iter(range(c.nf) if fill else ())

            def take(k):
                for n in (n for _, n in zip(range(k), fills)):
                    order.append(("fill", n, 1))
            if c.nf == 8:
                before, after = ([1, 1, 2, 0], [1, 1, 0, 1]) if not seam else ([0, 0, 1, 3], [0, 1, 1, 1])
            else:
                before, after = ([1, 0, 1, 0], [1, 1, 0, 1]) if not seam else ([0, 0, 1, 1], [0, 1, 1, 1])
            weights = iter(c.proj_w if seam else ())
            for b in range(GB):
                if ctx:
                    order.append(("ctx", b, 2))
                if seam and b < 2:
                    order += [("w", n, 1) for _, n in zip(range((len(c.proj_w) + 1 - b) // 2), weights)]
                take(before[b])
                if b < GB - 1:
                    order.append(("scores", b + 1, 0))
                elif fill:
                    order.append(("scores", 0, 1))
                order.append(("turn", b, 0))
                if b < GB - 1:
                    order += [("exp", b + 1, 0), ("norm", b + 1, 0)]
                elif fill:
                    order += [("exp", 0, 1), ("norm", 0, 1)]
                if b == 2:
                    order.append(("out", 0, 0))
                take(after[b])
                order.append(("pv", b, 0))
            take(c.nf)
            order.append(("out", 1, 0))
            if seam:
                order += [("w", n, 1) for n in c.out_w]
            return order

        def cross_walk(c, eng, step):
            def run(what, n, ahead, U, par, h, g, seam=False):
                if what == "w":
                    step(what, n, None, None, h + 1, None)
                elif ahead and seam:
                    step(what, n, U + ahead, (par + ahead) % 2, h + 1, 0)
                else:
                    step(what, n, U + ahead, (par + ahead) % 2, h, g)

            for k in range(KC):
                step("ctx", k, 0, 0, 0, 0)
            for n in range(c.nf):
                step("fill", n, 0, 0, 0, 0)
            for k in range(KC):
                step("ctx", k, 1, 1, 0, 1)
            for what in ("scores", "exp", "norm"):
                step(what, 0, 0, 0, 0, 0)

            def head(h, last):
                with eng.Fori(0, NG // 2 - 1) as i:
                    for par in (0, 1):
                        for what, n, ahead in cross_order(c, True, True, False):
                            run(what, n, ahead, h * NG + i * 2 + par, par, h, i * 2 + par)
                for par in (0, 1):
                    for what, n, ahead in cross_order(c, par == 0 or not last, not last, par == 1 and not last):
                        run(what, n, ahead, h * NG + (NG - 2 + par), par, h, NG - 2 + par, par == 1)
            with eng.Fori(0, KV - 1) as h:
                head(h, False)
            head(KV - 1, True)

        def swdst(c, part, name, i, n):
            m = D if name in ("wq", "wo", "bv", "bo") else c.kvc * P
            return sw[name][:, part, i:i + n, 0:m], P, m

        def fwdst(c, part, name, i, n):
            return fw[name][:, part, i:i + n, :], P, fw[name].shape[-1]

        def self_order(c, left):
            order = []
            if c.rope:
                fills = {6: [(0, 2)], 7: [(1, 2)], 0: [(2, 1)], 1: [(3, 1)], 2: [(4, 1)], 3: [(5, 1)], 4: [(6, 1), (7, 1)]}
            else:
                fills = {n: [(n, 1)] for n in range(c.nf)}
            spreads = {0: [(QX + 3, 0)], 2: [(0, 1), (1, 1)], 3: [(2, 1)], 4: [(3, 1)],
                       5: [(QX, 1)], 6: [(QX + 1, 1)], 7: [(QX + 2, 1)]}
            values = {1: (2, 0), 2: (3, 0), 6: (0, 1), 7: (1, 1)}

            def put(what, n, ahead=0):
                ahead, n = (ahead, n) if what in ("fill", "qx", "vx") else divmod(n, UNITS)
                if ahead <= left:
                    order.append((what, n, ahead))
            for u in range(UNITS + 1):
                queries = [("qx", n, ahead) for n, ahead in spreads.get(u, [])]
                projections = [("fill", n, ahead) for n, ahead in fills.get(u, [])]
                sums = [("sum", u + 2, 0)] if u else []
                if u:
                    put("pv", u - 1)
                if u in (UNITS // 2, UNITS):
                    put("pve", 2 * u // UNITS - 1)
                for item in projections + queries + sums if c.rope else sums + queries + projections:
                    put(*item)
                if u:
                    put("turn", u + 1)
                if u in values:
                    put("vx", *values[u])
                if u:
                    put("scores", u + 3)
                if u in (UNITS // 2, UNITS):
                    put("out", 2 * u // UNITS - 1)
            return order

        def ffn_order(c, left):
            last = left == 0
            order = [("fill", n, 1) for n in range(4) if not last] + [("down", 0, 0)]
            return order + [("fill", n, 1) for n in range(4, 8) if not last] + [("down", 1, 0)]

        def walk(eng, first, order, c, step):
            for what, n, U in first:
                step(what, n, U, U)
            with eng.Fori(0, NG // 2 - 1) as i:
                for par in (0, 1):
                    for what, n, ahead in order(c, 2):
                        step(what, n, i * 2 + (par + ahead), (par + ahead) % 2)
            for par in (0, 1):
                for what, n, ahead in order(c, 1 - par):
                    step(what, n, NG - 2 + par + ahead, (par + ahead) % 2)

        def self_first(c):
            own = [("fill", n) for n in range(c.nf)] + [("qx", n) for n in range(QX)] + [("vx", 0), ("vx", 1)]
            own += [("scores", 0), ("scores", 1), ("sum", 0), ("qx", QX), ("qx", QX + 1), ("qx", QX + 2)]
            own += [("sum", 1), ("turn", 0), ("scores", 2), ("sum", 2), ("turn", 1), ("scores", 3)]
            return [(what, n, 0) for what, n in own] + ([("fill", 0, 1), ("fill", 1, 1)] if c.rope else [])

        def ffn_first(c):
            return [("fill", n, 0) for n in range(c.nf)]

        def rope_dst(m, par, part):
            return sk[:, par, part, 0:1, :] if m == 2 else sq[:, par, part, 2 * m:2 * m + 2, :]

        def spread(eng, t0, c, n, U, par, part):
            tile, piece = divmod(n, QX)
            nq = 4 if c.rope else 2
            eng.wait_ge(sm["proj_free"], 2 + t0["proj_full"] + U * c.nf + nq)
            if c.rope:
                eng.wait_ge(sm["rope_lo"], t0["rope_lo"] + U * c.nrope + 2)
            if tile == 1:
                eng.wait_ge(sm["s_full"], t0["s_full"] + U * UNITS)
            elif not (isinstance(U, int) and U == 0):
                eng.wait_ge(sm["s_full"], t0["s_full"] + U * UNITS - UNITS // 2)
            for h in range(piece * HPC // QX, (piece + 1) * HPC // QX):
                if part == LO and (h % 2 == 0) != (eng is nc.scalar):
                    continue
                src = sq[:, par, part, :, tile * P:(tile + 1) * P].rearrange("p c (b t) -> p c b t", b=2)
                if part == HI:
                    e = eng.tensor_scalar(qm[:, tile, part, :, :, h, :], src, hmask[:, h:h + 1], None, ALU.mult)
                elif eng is nc.gpsimd:
                    e = eng.tensor_tensor(qm[:, tile, part, :, :, h, :], src,
                                          hmask[:, h:h + 1].unsqueeze(2).unsqueeze(3).to_broadcast([P, KC, 2, L]), ALU.mult)
                else:
                    e = eng.activation(qm[:, tile, part, :, :, h, :], src, ACT.Copy, scale=hmask[:, h:h + 1])
            return e

        def unit(u):
            b, half = divmod(u, 2)
            return b, b // 2, b % 2, 2 * half

        def xtile(t):
            return X[:, bass.ds(t, 1), :].rearrange("p o d -> p (o d)")

        def carry(eng, col):
            if eng is nc.gpsimd:
                eng.tensor_tensor(carrier[:, col:col + 1], neghalf[:, 0:1], neghalf[:, 0:1], ALU.mult)
            else:
                eng.memset(carrier[:, col:col + 1], 0.0)

        block = ctx.enter_context(nc.Block())

        @block.sync
        def _(sp):
            for n in sm:
                if n not in once:
                    sp.sem_inc(sm[n], START)
            for slot in range(XT):
                sp.sem_inc(xt_out[slot], 16)
            for n in range(NT // PREP_T):
                sp.dma_start(X[:, n * PREP_T:(n + 1) * PREP_T, :],
                             a["x"].rearrange("(t p) d -> p t d", p=P)[:, n * PREP_T:(n + 1) * PREP_T, :]).then_inc(x_in[n], 16)
            sp.dma_start(consts[:, :], a["consts"]).then_inc(sm["bias_in"], 16)
            sp.dma_start(bqk[:, :, :], a["L0_attn_bqk"]).then_inc(sm["bias_in"], 16)

            def chunk_in(t0, c, n, h=0):
                name, i, k = c.chunks[n]
                nm = c.name
                if isinstance(c, Cross):
                    w = c.nh * c.hd if name == "wq" else c.hd
                    if name == "wo":
                        src = a[nm + "_Wo"].rearrange("(v h p) m -> v p h m", p=c.hd, h=c.nh)[bass.ds(h, 1), :, i:i + k, :].rearrange("o p h m -> (o p) h m")
                    else:
                        src = a[nm + "_W" + name[1]].rearrange("(k p) m -> p k m", p=P)[:, i:i + k, bass.ds(h * w, w)]
                elif isinstance(c, Ffn):
                    src = a[nm + "_" + name + "_w"].rearrange("(k p) m -> p k m", p=P)[:, i:i + k, :]
                elif name in ("bv", "bo"):
                    src = a[nm + "_" + name].rearrange("(o k m) -> o k m", o=1, k=1).to_broadcast([P, 1, D])
                else:
                    src = a[nm + "_W" + name[1]].rearrange("(k p) m -> p k m", p=P)[:, i:i + k, :]
                sp.wait_ge(sm["w_free"], t0["w_hi"] + h * len(c.chunks) + (n + 1))
                _, stage = chunk_dst(c, HI, n)
                sp.dma_start(stage, src).then_inc(w_in[n % 2], 16)

            def prep(t0, c):
                nw, sent = len(c.chunks), 2
                for n in (0, 1):
                    chunk_in(t0, c, n)
                split = 0
                for what, f in prep_order(c):
                    if what == "w":
                        split += 1
                    elif what == "tile":
                        while sent < min(split + 2, nw):
                            chunk_in(t0, c, sent)
                            sent += 1
                        sp.wait_ge(sm["proj_free"], 2 + t0["proj_full"] + f + 1)
                        sp.dma_start(scratch[f].rearrange("p s k t -> p (s k t)"),
                                     xt[:, f % XT].rearrange("p s k t -> p (s k t)")).then_inc(xt_out[f % XT], 16)
                for n in range(sent, nw):
                    chunk_in(t0, c, n)

            def scratch_whole(t0):
                for slot in range(XT):
                    sp.wait_ge(xt_out[slot], 16 + 16 * (t0["ln_var"] - START) * NT // XT)

            def cross(t0, c):
                def ctx_load(U, par, gi):
                    sp.dma_start(cstage[:, par, :, :], a["ctxT"].rearrange("(k p) t -> p k t", p=P)[:, :, bass.ds(gi * (GB * S), GB * S)]
                                 ).then_inc(ctx_in[par], 16)

                def xn_load(U, par, gi):
                    for t in range(GT):
                        sp.dma_start(xg[:, par, t].rearrange("p s k t -> p (s k t)"),
                                     scratch[bass.ds(gi * GT + t, 1), :, :, :, :].rearrange("o p s k t -> p (o s k t)")
                                     ).then_inc(xg_in[par], 16)

                def group_in(U, par, gi):
                    sp.wait_ge(sm["ctx_ok"], t0["ctx_ok"] + (U - 1) * KC)
                    ctx_load(U, par, gi)
                    sp.wait_ge(sm["proj_full"], t0["proj_full"] + (U - 1) * c.nf)
                    xn_load(U, par, gi)

                def weights_in(h, chunks):
                    for n in chunks:
                        chunk_in({"w_hi": t0["w_hi"] - c.nw}, c, n, h)

                sp.wait_ge(sm["o_full"], t0["o_full"])
                sp.wait_ge(sm["x_ok"], t0["x_ok"])
                for U in (0, 1):
                    ctx_load(U, U, U)
                scratch_whole(t0)
                for U in (0, 1):
                    xn_load(U, U, U)

                def middle(h):
                    with sp.Fori(0, NG // 2 - 1) as i:
                        for par in (0, 1):
                            group_in(h * NG + i * 2 + (par + 2), par, i * 2 + (par + 2))
                with sp.Fori(0, KV - 1) as h:
                    middle(h)
                    weights_in(h + 1, range(2))
                    for g in (0, 1):
                        group_in(h * NG + (NG + g), g, g)
                    weights_in(h + 1, range(2, c.nw))
                middle(KV - 1)

            def groups_in(t0, c):
                scratch_whole(t0)
                with sp.Fori(0, NG // 2) as i:
                    for par in (0, 1):
                        sp.wait_ge(sm["proj_full"], t0["proj_full"] - c.nf + (i * 2 + par) * c.nf)
                        for t in range(GT):
                            sp.dma_start(xg[:, par, t].rearrange("p s k t -> p (s k t)"),
                                         scratch[bass.ds((i * 2 + par) * GT + t, 1), :, :, :, :].rearrange("o p s k t -> p (o s k t)")
                                         ).then_inc(xg_in[par], 16)

            def self_(t0, c):
                groups_in(t0, c)

            def ffn0(t0, c):
                sp.wait_ge(sm["o_full"], t0["o_full"])
                for n, t in (("gamma", gamma), ("beta", beta)):
                    sp.dma_start(t, a["L0_ffn_ln_" + n].rearrange("(o m) -> o m", o=1).to_broadcast([P, D])).then_inc(sm["gb_in"], 16)
                groups_in(t0, c)

            def ffn1(t0):
                sp.wait_ge(sm["w_free"], 2 + t0["w_hi"])
                sp.dma_start(wstage[:, :, :].rearrange("p (k s) m -> p k (s m)", k=1)[:, 0, 0:KC * D].rearrange("p (k m) -> p k m", k=KC),
                             a["L1_ffn_W"].rearrange("(k p) m -> p k m", p=P)).then_inc(sm["wt_in"], 16)
                sp.wait_ge(sm["o_full"], t0["o_full"])
                sp.dma_start(brow, a["L1_ffn_b"].rearrange("(o m) -> o m", o=1).to_broadcast([P, D])).then_inc(sm["wt_in"], 16)
                with sp.Fori(0, NT // PREP_T) as i:
                    for t in range(PREP_T):
                        sp.wait_ge(sm["xo_ok"], START + i * PREP_T + (t + 1))
                        sp.dma_start(out.rearrange("(t p) d -> t p d", p=P)[bass.ds(i * PREP_T + t, 1), :, :].rearrange("o p d -> p (o d)"),
                                     xtile(i * PREP_T + t)).then_inc(sm["x_out"], 16)
                sp.wait_ge(sm["x_out"], 16 * NT)

            for kind, t0, c in plan:
                if kind == "prep":
                    prep(t0, c)
                elif kind == "ffn1":
                    ffn1(t0)
                else:
                    {"cross": cross, "self": self_, "ffn0": ffn0}[kind](t0, c)
            if layers < 6:
                sp.wait_ge(sm["o_free"], 1 + done["o_free"])
                sp.wait_ge(sm["x_ok"], done["x_ok"])
                sp.dma_start(out.rearrange("(t p) d -> p t d", p=P), X[:, :, :]).then_inc(sm["x_out"], 16)
                sp.wait_ge(sm["x_out"], 16)

        @block.gpsimd
        def _(pool):
            pool.memset(neghalf[:, :], -0.5).then_inc(sm["ident_set"], 1)
            pool.memset(identf[:, :], 0.0).then_inc(sm["ident_set"], 1)
            pool.wait_ge(sm["ident_set"], 2)
            pool.affine_select(out=identf[:, :], in_=identf[:, :], compare_op=ALU.not_equal, fill=1.0,
                               base=0, pattern=[[-1, P]], channel_multiplier=1).then_inc(sm["ident_ok"], 1)
            pool.memset(row0[:, :], 0.0).then_inc(sm["ident_set"], 1)
            pool.wait_ge(sm["ident_set"], 3)
            pool.memset(row0[0:1, :], 1.0).then_inc(sm["ident_ok"], 1)
            pool.wait_ge(sm["ident_ok"], 1)
            pool.tensor_copy(identb[:, :], identf[:, :]).then_inc(sm["ident_ok"], 1)
            pool.wait_ge(sm["bias_in"], 32)
            pool.tensor_copy(maskb[:, :], cmask).then_inc(sm["ident_ok"], 1)

            def prep(t0, c):
                pool.wait_ge(sm["ln_var"], t0["ln_var"] + 1)
                pool.tensor_tensor(rstd[:, :], vareps[:, :], neghalf[:, :], ALU.pow).then_inc(sm["ln_rstd"], 1)

            def cross(t0, c):
                def step(what, n, U, par, h, g):
                    if what == "ctx":
                        N = U * KC + n + 1
                        pool.wait_ge(sm["ctx_hi"], t0["ctx_hi"] + N)
                        pool.tensor_tensor(cT[:, par, LO, n, :], cstage[:, par, n, :], cT[:, par, HI, n, :], ALU.subtract).then_inc(sm["ctx_ok"], 1)
                    elif what == "scores":
                        pool.wait_ge(sm["nmax"], t0["nmax"] + U * GB + (n + 1))
                        pool.tensor_tensor(nbias[:, n % 2, 0:c.pairs], negmax[:, n % 2, 0:c.pairs], scales[:, 0:c.pairs], ALU.mult).then_inc(sm["nbias_ok"], 1)
                    elif what == "norm":
                        pool.wait_ge(sm["rinv_ok"], t0["rinv_ok"] + U * GB + (n + 1))
                        pool.tensor_tensor(probs[:, n % 2, 0:c.pairs, :], probs[:, n % 2, 0:c.pairs, :],
                                           rinv[:, n % 2, 0:c.pairs].unsqueeze(2).to_broadcast([P, c.pairs, KEYS]), ALU.mult).then_inc(sm["p_ok"], 1)

                pool.wait_ge(sm["o_full"], t0["o_full"])
                pool.wait_ge(sm["x_ok"], t0["x_ok"])
                pool.memset(pT2.bitcast(F32), 0.0).then_inc(sm["zero_ok"], 1)
                pool.memset(scales[:, :], c.scale).then_inc(sm["zero_ok"], 1)
                pool.wait_ge(sm["zero_ok"], t0["zero_ok"] + 2)
                cross_walk(c, pool, step)

            def self_(t0, c):
                pool.wait_ge(sm["o_full"], t0["o_full"])
                pool.memset(vx.bitcast(F32), 0.0).then_inc(sm["zero_ok"], 1)
                pool.wait_ge(sm["bias_in"], 32)

                def step(what, n, U, par):
                    if what == "fill" and c.fills[n][0] == "r":
                        m = c.fills[n][1]
                        N = t0["rope_ok"] + U * c.nrope + m
                        w = GT * P * (1 if m == 2 else 2)
                        pool.wait_ge(sm["rot_ok"], N + 1)
                        pool.tensor_tensor(rt1[:, 0:w], rt1[:, 0:w], rt2[:, 0:w], ALU.add).then_inc(sm["rope_ok"], 1)
                        pool.wait_ge(sm["proj_hi"], t0["proj_full"] + U * c.nf + (n + 1))
                        hi, lo = (rope_dst(m, par, x) for x in (HI, LO))
                        pool.tensor_tensor(lo, rt1[:, 0:w].rearrange("p (c t) -> p c t", t=GT * P), hi, ALU.subtract).then_inc(sm["rope_lo"], 1)
                    if what == "qx":
                        spread(pool, t0, c, n, U, par, LO).then_inc(sm["qlo2_ok"], 1)
                    if what == "sum":
                        Q, s = t0["exp_ok"] + U * UNITS + n, n % SCB
                        pool.wait_ge(sm["rinv_ok"], Q + 1)
                        pool.tensor_tensor(sc[:, s], sc[:, s], sinv[:, s].unsqueeze(2).to_broadcast([P, HPC, L]), ALU.mult).then_inc(sm["p_ok"], 1)
                walk(pool, self_first(c), self_order, c, step)

            def ffn0(t0, c):
                pool.wait_ge(sm["gb_in"], 32)

                def step(what, n, U, par):
                    if what == "fill" and c.fills[n][0] == "u":
                        m = c.fills[n][1]
                        pool.wait_ge(sm["h_hi"], t0["h_hi"] + U * 4 + (m + 1))
                        pool.tensor_tensor(hT[:, par, LO, 2 * m:2 * m + 2, :], sq32.rearrange("p (c t) -> p c t", c=2),
                                           hT[:, par, HI, 2 * m:2 * m + 2, :], ALU.subtract).then_inc(sm["h_ok"], 1)
                    if what == "down":
                        N = t0["x_ok"] + U * GT + n
                        pool.wait_ge(sm["y_var"], N + 1)
                        pool.tensor_tensor(yrstd, yvar, neghalf[:, 0:1], ALU.pow).then_inc(sm["y_rstd"], 1)
                        pool.wait_ge(sm["y_n"], N + 1)
                        pool.tensor_tensor(yn, yn, gamma, ALU.mult).then_inc(sm["y_g"], 1)
                        pool.wait_ge(sm["y_g"], N + 1)
                        pool.tensor_tensor(yn, yn, beta, ALU.add).then_inc(sm["y_b"], 1)
                        pool.wait_ge(sm["y_b"], N + 1)
                        pool.tensor_tensor(xtile(U * GT + n), xtile(U * GT + n), yn, ALU.add).then_inc(sm["x_ok"], 1)
                walk(pool, ffn_first(c), ffn_order, c, step)

            def ffn1(t0):
                pool.wait_ge(sm["o_full"], t0["o_full"])
                pool.memset(ones, 1.0).then_inc(sm["zero_ok"], 1)
                pool.wait_ge(sm["ln_var"], t0["ln_var"] + 1)
                pool.tensor_tensor(rstd[:, :], vareps[:, :], neghalf[:, :], ALU.pow).then_inc(sm["ln_rstd"], 1)
                for i in range(QUADS):
                    pool.wait_ge(sm["rms_in"], START + i + 1)
                    pool.tensor_tensor(rms, rms_in, neghalf[:, 0:PREP_T], ALU.pow).then_inc(sm["rms_ok"], 1)
                    for t in range(PREP_T):
                        pool.tensor_tensor(X[:, i * PREP_T + t, :], X[:, i * PREP_T + t, :], zn[:, i % 2, t, :], ALU.add).then_inc(sm["xz_ok"], 1)

            for kind, t0, c in plan:
                if kind == "prep":
                    prep(t0, c)
                elif kind == "ffn1":
                    ffn1(t0)
                else:
                    {"cross": cross, "self": self_, "ffn0": ffn0}[kind](t0, c)

        @block.scalar
        def _(act):
            def prep(t0, c):
                act.wait_ge(sm["o_full"], t0["o_full"])
                act.wait_ge(sm["x_ok"], t0["x_ok"])
                for what, f in prep_order(c):
                    if what == "w":
                        w_split_hi(act, t0["w_hi"], c, f, 0)
                    elif what == "tile":
                        act.wait_ge(sm["proj_full"], t0["proj_full"] + f + 1)
                        act.wait_ge(xt_out[f % XT], 16 + 16 * (t0["ln_var"] - START) * NT // XT + 16 * (f // XT))
                        act.activation(xt[:, f % XT, HI], bank[f % 2][:, :].rearrange("p (k t) -> p k t", k=KC), ACT.Copy).then_inc(sm["proj_hi"], 1)

            def cross(t0, c):
                def step(what, n, U, par, h, g):
                    if what == "w":
                        if n in c.out_w:
                            act.wait_ge(sm["o_full"], t0["o_full"] + h * NT)
                        w_split_hi(act, t0["w_hi"] - c.nw, c, n, h)
                        return
                    if what == "ctx":
                        act.wait_ge(ctx_in[par], 8 * t0["ctx"] + (U - par) * 8 + 16)
                        act.activation(cT[:, par, HI, n, :], cstage[:, par, n, :], ACT.Copy).then_inc(sm["ctx_hi"], 1)
                        return
                    J = U * GB + n + t0["exp_ok"]
                    if what == "fill":
                        src, dst = fill_io(c, c.fills[n], par, HI)(proj_ps[n % 2])
                        act.wait_ge(sm["proj_full"], t0["proj_full"] + U * c.nf + (n + 1))
                        act.activation(dst, src, ACT.Copy).then_inc(sm["proj_hi"], 1)
                    elif what == "exp":
                        act.wait_ge(sm["nbias_ok"], t0["nbias_ok"] + U * GB + (n + 1))
                        for j in range(c.pairs):
                            e = act.activation(probs[:, n % 2, j, :], score_ps[j // 2][:, (j % 2) * KEYS:(j % 2 + 1) * KEYS],
                                               ACT.Exp, bias=nbias[:, n % 2, j:j + 1], scale=c.scale,
                                               accum_out=rowsum[:, n % 2, j:j + 1])
                        e.then_inc(sm["exp_ok"], 1)
                    elif what == "turn":
                        w = c.pairs * P
                        lo = 64 * (n % 2)
                        act.wait_ge(sm["t_full"], J + 1)
                        act.activation(pT1[:, HI, 0:w], turn_ps[0][:, 0:w], ACT.Copy)
                        act.activation(pT2[lo:lo + 64, n % 2, HI, 0:w], turn_ps[1][lo:lo + 64, 0:w], ACT.Copy).then_inc(sm["t_hi"], 1)
                    elif what == "pv":
                        act.wait_ge(sm["pv_full"], t0["pv_full"] + U * GB + (n + 1))
                        dst = att[0:c.hd, HI, 0:c.nh * P].rearrange("p (h t) -> p h t", h=c.nh)[:, :, 64 * (n % 2):64 * (n % 2) + 64]
                        act.activation(dst, pv_ps[0:c.hd, 0:c.nh * L].rearrange("p (h t) -> p h t", h=c.nh), ACT.Copy).then_inc(sm["pv_hi"], 1)

                act.wait_ge(sm["zero_ok"], t0["zero_ok"] + 2)
                cross_walk(c, act, step)

            def self_(t0, c):
                act.wait_ge(sm["zero_ok"], t0["zero_ok"] + 1)
                act.wait_ge(sm["bias_in"], 32)

                def step(what, n, U, par):
                    if what == "fill":
                        kind, m = c.fills[n]
                        ps = proj_ps[n % 2]
                        F = t0["proj_full"] + U * c.nf + (n + 1)
                        if kind in "qk" and not c.rope:
                            act.wait_ge(sm["proj_full"], F)
                            for j in range(2):
                                ch = 2 * m + j
                                e = act.activation((sq if kind == "q" else sk)[:, par, HI, ch, :], ps[:, j * GT * P:(j + 1) * GT * P],
                                                   ACT.Identity, bias=bqk[:, 0 if kind == "q" else 1, ch:ch + 1])
                            e.then_inc(sm["proj_hi"], 1)
                        elif kind in "qk":
                            w = GT * P * (2 if kind == "q" else 1)
                            act.wait_ge(sm["proj_full"], F)
                            act.activation(raw32[:, 0:w], ps[:, 0:w], ACT.Copy).then_inc(sm["proj_hi"], 1)
                        elif kind == "r":
                            w = GT * P * (1 if m == 2 else 2)
                            act.wait_ge(sm["rope_ok"], t0["rope_ok"] + U * c.nrope + (m + 1))
                            act.activation(rope_dst(m, par, HI), rt1[:, 0:w].rearrange("p (c t) -> p c t", t=GT * P),
                                           ACT.Copy).then_inc(sm["proj_hi"], 1)
                        else:
                            act.wait_ge(sm["proj_full"], F)
                            act.activation(sv[:, HI, m, 0:c.kvc * P], ps[:, 0:c.kvc * P], ACT.Copy).then_inc(sm["proj_hi"], 1)
                    elif what == "qx":
                        spread(act, t0, c, n, U, par, LO).then_inc(sm["qlo_ok"], 1)
                    elif what == "vx":
                        act.wait_ge(sm["proj_free"], 2 + t0["proj_full"] + U * c.nf + c.nf)
                        tile, b = divmod(n, 2)
                        if tile == 1:
                            act.wait_ge(sm["pv_full"], t0["pv_full"] + U * GT)
                        elif not (isinstance(U, int) and U == 0):
                            act.wait_ge(sm["pv_full"], t0["pv_full"] + U * GT - 1)
                        for j in range(2):
                            for part in (HI, LO):
                                at = vx_at + ((tile * 2 + part) * 2 + b) * KC * 4 * P + 64 * j
                                dst = bass.AP(tensor=arena[:, :].tensor, offset=arena[64 * j:64 * j + 64, at:at + 1].offset,
                                              ap=[[ARENA, 64], [4 * P, c.kvc], [P + HD, 4], [1, HD]])
                                src = sv[64 * b:64 * b + 64, part, tile, 0:c.kvc * P].rearrange("p (c j t d) -> p c j t d", j=2, t=4, d=HD)[:, :, j]
                                e = act.activation(dst, src, ACT.Copy)
                        e.then_inc(sm["vx_ok"], 1)
                    elif what == "scores":
                        act.wait_ge(sm["shifted"], t0["shifted"] + U * UNITS + (n + 1))
                        act.activation(sc[:, n % SCB], sc[:, n % SCB], ACT.Exp, scale=HD ** -0.5).then_inc(sm["exp_ok"], 1)
                    elif what == "turn":
                        act.wait_ge(sm["t_full"], t0["t_full"] + U * UNITS + (n + 1))
                        act.activation(spT[:, n % 2, HI], turn_ps[n % 2][:, :], ACT.Copy).then_inc(sm["t_hi"], 1)
                    elif what == "pve":
                        act.wait_ge(sm["pv_full"], t0["pv_full"] + U * GT + (n + 1))
                        act.activation(satt[:, HI], pv_ps[:, :].rearrange("p (c t) -> p c t", c=KC), ACT.Copy).then_inc(sm["pv_hi"], 1)
                walk(act, self_first(c), self_order, c, step)

            def ffn0(t0, c):

                def step(what, n, U, par):
                    if what == "fill":
                        kind, m = c.fills[n]
                        ps = proj_ps[n % 2]
                        F = t0["proj_full"] + U * c.nf + (n + 1)
                        act.wait_ge(sm["proj_full"], F)
                        two = ps[:, :].rearrange("p (c t) -> p c t", c=2)
                        if kind == "u":
                            act.activation(relu32, ps[:, :], ACT.Relu).then_inc(sm["proj_hi"], 1)
                            act.wait_ge(sm["proj_free"], 2 + F)
                            act.activation(hT[:, par, HI, 2 * m:2 * m + 2, :], sq32.rearrange("p (c t) -> p c t", c=2),
                                           ACT.Copy).then_inc(sm["h_hi"], 1)
                        elif kind == "f":
                            act.activation(fT[:, HI], two, ACT.Copy).then_inc(sm["proj_hi"], 1)
                        elif kind == "e":
                            act.activation(eT[:, par, HI], two, ACT.Copy).then_inc(sm["proj_hi"], 1)
                        else:
                            act.activation(logits[:, m], ps[:, 0:8], ACT.Copy).then_inc(sm["proj_hi"], 1)
                    elif what == "down":
                        N = U * GT + n
                        act.wait_ge(sm["o_full"], t0["o_full"] + N + 1)
                        act.wait_ge(sm["pv_free"], 1 + t0["pv_full"] + N)
                        act.activation(shared, out_ps[:, :], ACT.Copy).then_inc(sm["sh_ok"], 1)
                walk(act, ffn_first(c), ffn_order, c, step)

            def ffn1(t0):
                act.wait_ge(sm["o_full"], t0["o_full"])
                def squares(i):
                    for t in range(PREP_T):
                        act.wait_ge(sm["ln_xn"], t0["ln_xn"] + i * PREP_T + (t + 1))
                        e = act.activation(junk[:, t], zn[:, i % 2, t, :], ACT.Square, accum_out=sumsq[:, t:t + 1])
                    e.then_inc(sm["sumsq_ok"], 1)

                def gelu(i, t):
                    act.wait_ge(sm["y_free"], START + i * PREP_T + (t + 1))
                    act.activation(gl[:, t % 2], yb[:, t % 2], ACT.Gelu).then_inc(sm["gelu_ok"], 1)

                squares(0)
                for i in range(QUADS):
                    if i + 1 < QUADS:
                        squares(i + 1)
                    for t in range(PREP_T):
                        act.wait_ge(sm["q_turn"], START + i * PREP_T + (t + 1))
                        act.activation(xqT[:, t % 2], bank[t % 2][:, 0:KC * P // 2].bitcast(BF16).rearrange("p (k t) -> p k t", k=KC),
                                       ACT.Copy).then_inc(sm["q_evac"], 1)
                        if t:
                            gelu(i, t - 1)
                    gelu(i, PREP_T - 1)

            for kind, t0, c in plan:
                if kind == "prep":
                    prep(t0, c)
                elif kind == "ffn1":
                    ffn1(t0)
                else:
                    {"cross": cross, "self": self_, "ffn0": ffn0}[kind](t0, c)

        @block.vector
        def _(dve):
            dve.memset(credit[:, 0:1], 0.0).then_inc(sm["proj_free"], 2)
            dve.memset(credit[:, 1:2], 0.0).then_inc(sm["w_free"], 2)
            dve.memset(credit[:, 3:4], 0.0).then_inc(sm["t_free"], 1)
            dve.memset(credit[:, 4:5], 0.0).then_inc(sm["pv_free"], 1)
            dve.memset(credit[:, 5:6], 0.0).then_inc(sm["o_free"], 1)
            dve.memset(credit[:, 6:7], 0.0).then_inc(sm["const_ok"], 1)
            dve.wait_ge(sm["const_ok"], 1)

            def x_final(t0):
                dve.wait_ge(sm["o_free"], 1 + t0["o_free"])
                dve.wait_ge(sm["x_ok"], t0["x_ok"])

            def tile_stats(t0, outs, tile):
                dve.wait_ge(sm["o_free"], 1 + t0["o_free"] + (outs + 1))
                dve.bn_stats(stats[:, bass.ds(tile, 1), :].rearrange("p o s -> p (o s)"), xtile(tile)).then_inc(sm["ln_stat"], 1)

            def prep(t0, c):
                x_final(t0)
                for what, f in prep_order(c):
                    if what == "stats":
                        own = c in (X0, X1)
                        for t in range(NT if own else 0):
                            if c is X0 and t % PREP_T == 0:
                                dve.wait_ge(x_in[t // PREP_T], 16)
                            dve.bn_stats(stats[:, t, :], X[:, t, :]).then_inc(sm["ln_stat"], 1)
                        dve.wait_ge(sm["ln_stat"], t0["ln_stat"] + (NT if own else 0))
                        for t in range(NT):
                            s = dve.bn_aggr(meanvar[:, t, :], stats[:, t, :])
                        s.then_inc(sm["ln_mv"], 1)
                        dve.wait_ge(sm["ln_mv"], t0["ln_mv"] + 1)
                        dve.tensor_scalar(vareps[:, :], meanvar[:, :, 1], EPS, None, ALU.add).then_inc(sm["ln_var"], 1)
                    elif what == "w":
                        w_split_lo(dve, t0["w_hi"], c, f, 0)
                    elif what == "xn":
                        if f == 0:
                            dve.wait_ge(sm["ln_rstd"], t0["ln_rstd"] + 1)
                        dve.tensor_scalar(xn[:, f % PREP_T, :], X[:, f, :], meanvar[:, f, 0:1], rstd[:, f:f + 1],
                                          ALU.subtract, ALU.mult).then_inc(sm["ln_xn"], 1)
                    else:
                        dve.wait_ge(sm["proj_hi"], t0["proj_full"] + f + 1)
                        dve.tensor_tensor(xt[:, f % XT, LO], bank[f % 2][:, :].rearrange("p (k t) -> p k t", k=KC),
                                          xt[:, f % XT, HI], ALU.subtract).then_inc(sm["proj_free"], 1)

            def cross(t0, c):
                def step(what, n, U, par, h, g):
                    if what == "w":
                        w_split_lo(dve, t0["w_hi"] - c.nw, c, n, h)
                        return
                    if what == "ctx":
                        return
                    J = U * GB + n + t0["exp_ok"]
                    if what == "fill":
                        src, lo = fill_io(c, c.fills[n], par, LO)(proj_ps[n % 2])
                        _, hi = fill_io(c, c.fills[n], par, HI)(proj_ps[n % 2])
                        dve.wait_ge(sm["proj_hi"], t0["proj_full"] + U * c.nf + (n + 1))
                        dve.tensor_tensor(lo, src, hi, ALU.subtract).then_inc(sm["proj_free"], 1)
                    elif what == "scores":
                        for s in range(c.sbanks):
                            dve.wait_ge(sm["s_full"], t0["s_full"] + U * (GB * c.sbanks) + (n * c.sbanks + s + 1))
                            r = dve.tensor_reduce(negmax[:, n % 2, 2 * s:2 * s + 2],
                                                  score_ps[s][:, 0:2 * KEYS].rearrange("p (j k) -> p j k", j=2),
                                                  AX.X, ALU.max, negate=True)
                        r.then_inc(sm["nmax"], 1)
                    elif what == "norm":
                        dve.wait_ge(sm["exp_ok"], J + 1)
                        dve.reciprocal(rinv[:, n % 2, 0:c.pairs], rowsum[:, n % 2, 0:c.pairs]).then_inc(sm["rinv_ok"], 1)
                    elif what == "turn":
                        w = c.pairs * P
                        lo = 64 * (n % 2)
                        dve.wait_ge(sm["t_hi"], J + 1)
                        dve.tensor_tensor(pT1[:, LO, 0:w], turn_ps[0][:, 0:w], pT1[:, HI, 0:w], ALU.subtract)
                        dve.tensor_tensor(pT2[lo:lo + 64, n % 2, LO, 0:w], turn_ps[1][lo:lo + 64, 0:w],
                                          pT2[lo:lo + 64, n % 2, HI, 0:w], ALU.subtract).then_inc(sm["t_free"], 1)
                    elif what == "pv":
                        dve.wait_ge(sm["pv_hi"], t0["pv_hi"] + U * GB + (n + 1))
                        at = [att[0:c.hd, part, 0:c.nh * P].rearrange("p (h t) -> p h t", h=c.nh)[:, :, 64 * (n % 2):64 * (n % 2) + 64]
                              for part in (HI, LO)]
                        dve.tensor_tensor(at[LO], pv_ps[0:c.hd, 0:c.nh * L].rearrange("p (h t) -> p h t", h=c.nh),
                                          at[HI], ALU.subtract).then_inc(sm["pv_free"], 1)
                    elif what == "out":
                        dve.wait_ge(sm["o_full"], t0["o_full"] + U * GT + (n + 1))
                        xt_ = X[:, bass.ds(g * GT + n, 1), :].rearrange("p o d -> p (o d)")
                        dve.tensor_tensor(xt_, out_ps[:, :], xt_, ALU.add).then_inc(sm["o_free"], 1)
                        if isinstance(h, int) and h == KV - 1:
                            tile_stats(t0, U * GT + n, g * GT + n)

                cross_walk(c, dve, step)

            def self_(t0, c):
                dve.wait_ge(sm["bias_in"], 32)

                def step(what, n, U, par):
                    if what == "fill":
                        kind, m = c.fills[n]
                        ps = proj_ps[n % 2]
                        F = t0["proj_full"] + U * c.nf + (n + 1)
                        if kind in "qk" and not c.rope:
                            dve.wait_ge(sm["proj_hi"], F)
                            t = sq if kind == "q" else sk
                            for j in range(2):
                                ch = 2 * m + j
                                e = dve.scalar_tensor_tensor(out=t[:, par, LO, ch, :], in0=ps[:, j * GT * P:(j + 1) * GT * P],
                                                             scalar=bqk[:, 0 if kind == "q" else 1, ch:ch + 1],
                                                             in1=t[:, par, HI, ch, :], op0=ALU.add, op1=ALU.subtract)
                            e.then_inc(sm["proj_free"], 1)
                        elif kind in "qk":
                            g = GB * (2 if kind == "q" else 1)
                            dve.wait_ge(sm["proj_hi"], F)
                            r = {"q": m, "k": 2}[kind]
                            dve.wait_ge(sm["rope_lo"], t0["rope_lo"] + U * c.nrope + r)
                            dve.tensor_tensor(rt1[:, 0:g * L].rearrange("p (g t) -> p g t", g=g), ps[:, 0:g * L].rearrange("p (g t) -> p g t", g=g),
                                              cos.unsqueeze(1).to_broadcast([P, g, L]), ALU.mult).then_inc(sm["proj_free"], 1)
                        elif kind == "r":
                            g = GB * (1 if m == 2 else 2)
                            dve.wait_ge(sm["proj_full"], F)
                            dve.tensor_tensor(rt2[:, 0:g * L].rearrange("p (g t) -> p g t", g=g), ps[:, 0:g * L].rearrange("p (g t) -> p g t", g=g),
                                              sin.unsqueeze(1).to_broadcast([P, g, L]), ALU.mult).then_inc(sm["proj_free"], 1)
                            dve.wait_ge(sm["proj_free"], 2 + F)
                            dve.memset(credit[:, 7:8], 0.0).then_inc(sm["rot_ok"], 1)
                        else:
                            dve.wait_ge(sm["proj_hi"], F)
                            dve.tensor_tensor(sv[:, LO, m, 0:c.kvc * P], ps[:, 0:c.kvc * P], sv[:, HI, m, 0:c.kvc * P],
                                              ALU.subtract).then_inc(sm["proj_free"], 1)
                    elif what == "qx":
                        spread(dve, t0, c, n, U, par, HI).then_inc(sm["qm_ok"], 1)
                    elif what == "scores":
                        Q, s = t0["exp_ok"] + U * UNITS + n, n % SCB
                        dve.wait_ge(sm["s_full"], t0["s_full"] + U * UNITS + (n + 1))
                        rows = score_ps[n % 2][:, :].rearrange("p (g k) -> p g k", g=HPC)
                        dve.tensor_reduce(smax[:, s], rows, AX.X, ALU.max, negate=True).then_inc(sm["nmax"], 1)
                        dve.wait_ge(sm["nmax"], t0["nmax"] + U * UNITS + (n + 1))
                        dve.tensor_tensor(sc[:, s], rows, smax[:, s].unsqueeze(2).to_broadcast([P, HPC, L]), ALU.add).then_inc(sm["shifted"], 1)
                    elif what == "sum":
                        Q, s = t0["exp_ok"] + U * UNITS + n, n % SCB
                        dve.wait_ge(sm["exp_ok"], Q + 1)
                        dve.tensor_reduce(ssum[:, s], sc[:, s], AX.X, ALU.add).then_inc(sm["summed"], 1)
                        dve.wait_ge(sm["summed"], t0["summed"] + U * UNITS + (n + 1))
                        dve.reciprocal(sinv[:, s], ssum[:, s]).then_inc(sm["rinv_ok"], 1)
                    elif what == "turn":
                        dve.wait_ge(sm["t_hi"], t0["t_hi"] + U * UNITS + (n + 1))
                        dve.tensor_tensor(spT[:, n % 2, LO], turn_ps[n % 2][:, :], spT[:, n % 2, HI], ALU.subtract).then_inc(sm["t_free"], 1)
                    elif what == "pve":
                        dve.wait_ge(sm["pv_hi"], t0["pv_hi"] + U * GT + (n + 1))
                        dve.tensor_tensor(satt[:, LO], pv_ps[:, :].rearrange("p (c t) -> p c t", c=KC), satt[:, HI],
                                          ALU.subtract).then_inc(sm["pv_free"], 1)
                    elif what == "out":
                        dve.wait_ge(sm["o_full"], t0["o_full"] + U * GT + (n + 1))
                        dve.tensor_tensor(xtile(U * GT + n), out_ps[:, :], xtile(U * GT + n), ALU.add).then_inc(sm["o_free"], 1)
                        tile_stats(t0, U * GT + n, U * GT + n)
                walk(dve, self_first(c), self_order, c, step)

            def ffn0(t0, c):

                def step(what, n, U, par):
                    if what == "fill":
                        kind, m = c.fills[n]
                        ps = proj_ps[n % 2]
                        F = t0["proj_full"] + U * c.nf + (n + 1)
                        dve.wait_ge(sm["proj_hi"], F)
                        two = ps[:, :].rearrange("p (c t) -> p c t", c=2)
                        if kind == "u":
                            dve.wait_ge(sm["h_ok"], t0["h_ok"] + U * 4 + m)
                            dve.scalar_tensor_tensor(out=sq32, in0=ps[:, :], scalar=0.0, in1=relu32,
                                                     op0=ALU.max, op1=ALU.mult).then_inc(sm["proj_free"], 1)
                        elif kind == "f":
                            dve.tensor_tensor(fT[:, LO], two, fT[:, HI], ALU.subtract).then_inc(sm["proj_free"], 1)
                        elif kind == "e":
                            dve.tensor_tensor(eT[:, par, LO], two, eT[:, par, HI], ALU.subtract).then_inc(sm["proj_free"], 1)
                        else:
                            carry(dve, 1)
                            dve.max(top8[:, m], logits[:, m]).then_inc(sm["proj_free"], 1)
                            dve.wait_ge(sm["proj_free"], 2 + F)
                            dve.tensor_tensor(gsum[:, par, m:m + 1], top8[:, m, 0:1], top8[:, m, 1:2], ALU.add).then_inc(sm["gate_ok"], 1)
                    elif what == "down":
                        N = U * GT + n
                        dve.wait_ge(sm["gate_ok"], t0["gate_ok"] + U * GT + GT)
                        dve.wait_ge(sm["sh_ok"], t0["sh_ok"] + N + 1)
                        dve.wait_ge(sm["y_n"], t0["y_n"] + N)
                        dve.wait_ge(sm["pv_full"], t0["pv_full"] + N + 1)
                        dve.scalar_tensor_tensor(out=y32, in0=pv_ps[:, :], scalar=gsum[:, par, n:n + 1], in1=shared,
                                                 op0=ALU.mult, op1=ALU.add).then_inc(sm["pv_free"], 1)
                        dve.wait_ge(sm["pv_free"], 1 + t0["pv_full"] + N + 1)
                        dve.bn_stats(ystats, y32).then_inc(sm["y_stat"], 1)
                        dve.wait_ge(sm["y_stat"], t0["y_stat"] + N + 1)
                        carry(dve, 1)
                        dve.bn_aggr(ymv, ystats).then_inc(sm["y_mv"], 1)
                        dve.wait_ge(sm["y_mv"], t0["y_mv"] + N + 1)
                        dve.tensor_scalar(yvar, ymv[:, 1:2], EPS, None, ALU.add).then_inc(sm["y_var"], 1)
                        dve.wait_ge(sm["y_rstd"], t0["y_rstd"] + N + 1)
                        dve.wait_ge(sm["x_ok"], t0["x_ok"] + N)
                        dve.tensor_scalar(yn, y32, ymv[:, 0:1], yrstd, ALU.subtract, ALU.mult).then_inc(sm["y_n"], 1)
                walk(dve, ffn_first(c), ffn_order, c, step)

            def ffn1(t0):
                x_final(t0)
                dve.wait_ge(sm["ln_stat"], t0["ln_stat"])
                for t in range(NT):
                    e = dve.bn_aggr(meanvar[:, t, :], stats[:, t, :])
                e.then_inc(sm["ln_mv"], 1)
                dve.wait_ge(sm["ln_mv"], t0["ln_mv"] + 1)
                dve.tensor_scalar(vareps[:, :], meanvar[:, :, 1], EPS, None, ALU.add).then_inc(sm["ln_var"], 1)
                W = wstage[:, 0, :]
                link = [0]

                def chain(ins):
                    link[0] += 1
                    ins.then_inc(sm["wm"], 1)
                    dve.wait_ge(sm["wm"], link[0])
                dve.wait_ge(sm["wt_in"], 32)
                dve.tensor_reduce(wabs, W, AX.X, ALU.add, apply_absolute_value=True).then_inc(sm["wsum"], 1)
                dve.wait_ge(sm["wsum_ps"], 1)
                chain(dve.tensor_scalar(wmean, out_ps[:, 0:1], 1.0 / (D * D), EPS, ALU.mult, ALU.max))
                chain(dve.reciprocal(winv, wmean))
                chain(dve.tensor_scalar(tw32, W, winv, ROUND, ALU.mult, ALU.add))
                chain(dve.tensor_scalar(tw32, tw32, ROUND, 1.0, ALU.subtract, ALU.min))
                dve.tensor_scalar(tw.rearrange("p k m -> p (k m)"), tw32, -1.0, None, ALU.max).then_inc(sm["wt_ok"], 1)
                LINKS = 7

                def front(i):
                    z, at = zn[:, i % 2], [0]

                    def link_(ins):
                        at[0] += 1
                        ins.then_inc(sm["d1"], 1)
                        dve.wait_ge(sm["d1"], START + i * LINKS + at[0])
                    if i >= 2:
                        dve.wait_ge(sm["xz_ok"], START + (i - 1) * PREP_T)
                    for t in range(PREP_T):
                        T = i * PREP_T + t
                        dve.tensor_scalar(z[:, t, :], X[:, T, :], meanvar[:, T, 0:1], rstd[:, T:T + 1],
                                          ALU.subtract, ALU.mult).then_inc(sm["ln_xn"], 1)
                    dve.wait_ge(sm["ln_xn"], t0["ln_xn"] + (i + 1) * PREP_T)
                    dve.tensor_reduce(absmax, z, AX.X, ALU.max, apply_absolute_value=True)
                    dve.wait_ge(sm["sumsq_ok"], START + i + 1)
                    dve.tensor_scalar(rms_in, sumsq, 1.0 / D, EPS, ALU.mult, ALU.add).then_inc(sm["rms_in"], 1)
                    dve.wait_ge(sm["rms_ok"], START + i + 1)
                    link_(dve.tensor_tensor(nmax_, absmax, rms, ALU.mult))
                    link_(dve.tensor_scalar(nmax_, nmax_, EPS, None, ALU.max))
                    link_(dve.reciprocal(ninv, nmax_))
                    dve.tensor_scalar(nfac[:, i % 2], nmax_, 1.0 / 127.0, wmean, ALU.mult, ALU.mult)
                    link_(dve.tensor_scalar(nscale, ninv, 127.0, None, ALU.mult))
                    for t in range(PREP_T):
                        e = dve.tensor_scalar(q32[:, t, :], z[:, t, :], rms[:, t:t + 1], nscale[:, t:t + 1], ALU.mult, ALU.mult)
                    link_(e)
                    link_(dve.tensor_scalar(q32, q32, ROUND, ROUND, ALU.add, ALU.subtract))
                    link_(dve.tensor_scalar(xq[:, i % 2], q32, 127.0, -128.0, ALU.min, ALU.max))
                    assert at[0] == LINKS
                    dve.memset(credit[:, 7:8], 0.0).then_inc(sm["xq_ok"], 1)

                def take_up(i, t):
                    dve.wait_ge(sm["gelu_ok"], START + i * PREP_T + (t + 1))
                    dve.wait_ge(sm["xz_ok"], START + i * PREP_T + (t + 1))
                    dve.tensor_tensor(X[:, i * PREP_T + t, :], X[:, i * PREP_T + t, :], gl[:, t % 2], ALU.add).then_inc(sm["xo_ok"], 1)

                dve.wait_ge(sm["ln_rstd"], t0["ln_rstd"] + 1)
                front(0)
                for i in range(QUADS):
                    if i + 1 < QUADS:
                        front(i + 1)
                    for t in range(PREP_T):
                        if t >= 2:
                            take_up(i, t - 2)
                        dve.wait_ge(sm["y_full"], START + i * PREP_T + (t + 1))
                        dve.scalar_tensor_tensor(out=yb[:, t % 2], in0=(pv_ps, out_ps)[t % 2][:, :], scalar=nfac[:, i % 2, t:t + 1],
                                                 in1=brow, op0=ALU.mult, op1=ALU.add).then_inc(sm["y_free"], 1)
                    take_up(i, 2)
                    take_up(i, 3)

            for kind, t0, c in plan:
                if kind == "prep":
                    prep(t0, c)
                elif kind == "ffn1":
                    ffn1(t0)
                else:
                    {"cross": cross, "self": self_, "ffn0": ffn0}[kind](t0, c)

        @block.tensor
        def _(pe):
            pe.wait_ge(sm["ident_ok"], 4)
            pe.wait_ge(sm["bias_in"], 32)
            pe.wait_ge(sm["const_ok"], 1)

            def product(ps, stat, mov, first, last):
                for n, (s, m) in enumerate(PASSES):
                    mm = pe.matmul(ps, stat(s), mov(m), start=first and n == 0, stop=last and n == 2,
                                   skip_group_check=True)
                return mm

            def pe_start(t0):
                pe.wait_ge(sm["o_free"], 1 + t0["o_free"])
                pe.wait_ge(sm["pv_free"], 1 + t0["pv_free"])
                pe.wait_ge(sm["t_free"], 1 + t0["t_free"])
                pe.wait_ge(sm["sh_ok"], t0["sh_ok"])

            def prep(t0, c):
                for f in range(NT):
                    pe.wait_ge(sm["ln_xn"], t0["ln_xn"] + f + 1)
                    pe.wait_ge(sm["proj_free"], t0["proj_full"] + f + 1)
                    for k in range(KC):
                        mm = pe.transpose(bank[f % 2][:, k * P:(k + 1) * P], xn[:, f % PREP_T, k * P:(k + 1) * P], identf[:, :])
                    mm.then_inc(sm["proj_full"], 1)

            def cross(t0, c):
                hd = c.hd

                def w(t, part, k, m0, m1):
                    return t[:, part, 0:KC * (t is wq and c.nh * hd or hd)].rearrange("p (k m) -> p k m", k=KC)[:, k, m0:m1]

                def step(what, n, U, par, h, g):
                    if what in ("w", "ctx"):
                        return
                    J = U * GB + n + t0["exp_ok"]
                    if what == "fill":
                        kind, m = c.fills[n]
                        ps = proj_ps[n % 2]
                        pe.wait_ge(sm["proj_free"], t0["proj_full"] + U * c.nf + (n + 1))
                        if n == 0:
                            pe.wait_ge(xg_in[par], 8 * GT * t0["xg"] + (U - par) * (8 * GT) + 16 * GT)
                            pe.wait_ge(sm["w_free"], 2 + t0["w_hi"] - c.nw + h * c.nw + len(c.proj_w))
                        if kind == "kc":
                            pe.wait_ge(sm["ctx_ok"], t0["ctx_ok"] + U * KC + KC)
                        if kind == "q":
                            for j in range(2):
                                hh = 2 * m + j
                                for k in range(KC):
                                    mm = product(ps[0:hd, j * GB * L:(j + 1) * GB * L],
                                                 lambda s: w(wq, s, k, hh * hd, (hh + 1) * hd),
                                                 lambda s: xg[:, par, :, s, k, :], k == 0, k == KC - 1)
                        elif kind == "kc":
                            for k in range(KC):
                                mm = product(ps[0:hd, :], lambda s: w(wk, s, k, 0, hd), lambda s: cT[:, par, s, k, :],
                                             k == 0, k == KC - 1)
                        elif kind == "kl":
                            for k in range(KC):
                                mm = product(ps[0:hd, 0:GB * L], lambda s: w(wk, s, k, 0, hd),
                                             lambda s: xg[:, par, :, s, k, :], k == 0, k == KC - 1)
                        elif kind == "vc":
                            for b in range(GB):
                                for k in range(KC):
                                    mm = product(ps[:, b * hd:(b + 1) * hd], lambda s: cT[:, par, s, k, b * S:(b + 1) * S],
                                                 lambda s: w(wv, s, k, 0, hd), k == 0, k == KC - 1)
                        else:
                            for t in range(GT):
                                for k in range(KC):
                                    mm = product(ps[:, t * hd:(t + 1) * hd], lambda s: xg[:, par, t, s, k, :],
                                                 lambda s: w(wv, s, k, 0, hd), k == 0, k == KC - 1)
                        mm.then_inc(sm["proj_full"], 1)
                    elif what == "scores":
                        if n == 0:
                            pe.wait_ge(sm["proj_free"], 2 + t0["proj_full"] + U * c.nf + c.nqk)
                        pe.wait_ge(sm["exp_ok"], J)
                        for j in range(c.pairs):
                            mm = product(score_ps[j // 2][:, (j % 2) * KEYS:(j % 2 + 1) * KEYS],
                                         lambda s: q_view(c, par, s)[:, n, 2 * j:2 * j + 2, :].rearrange("p h t -> p (h t)"),
                                         lambda s: kT[0:hd, par, s, n, :], True, True)
                            if j % 2 == 1:
                                mm.then_inc(sm["s_full"], 1)
                    elif what == "turn":
                        pe.wait_ge(sm["p_ok"], J + 1)
                        pe.wait_ge(sm["t_free"], J + 1)
                        c0 = S if n % 2 == 0 else L
                        w_ = L if n % 2 == 0 else P
                        for j in range(c.pairs):
                            pe.transpose(turn_ps[0][:, j * P:(j + 1) * P], probs[:, n % 2, j, 0:S], identf[:, :])
                            mm = pe.transpose(turn_ps[1][0:w_, j * P:(j + 1) * P], probs[:, n % 2, j, c0:c0 + w_], identf[:, :])
                        mm.then_inc(sm["t_full"], 1)
                    elif what == "pv":
                        pe.wait_ge(sm["t_free"], J + 2)
                        if n == 0:
                            pe.wait_ge(sm["proj_free"], 2 + t0["proj_full"] + U * c.nf + c.nf)
                        pe.wait_ge(sm["pv_free"], t0["pv_free"] + U * GB + (n + 1))
                        m = c.nh * L
                        product(pv_ps[0:hd, 0:m], lambda s: v_view(c, par, s)[:, n, :], lambda s: pT1[:, s, 0:m], True, False)
                        product(pv_ps[0:hd, 0:m], lambda s: v_view(c, par, s)[:, GB + n // 2, :],
                                lambda s: pT2[:, n % 2, s, 0:m], False, True).then_inc(sm["pv_full"], 1)
                    elif what == "out":
                        pe.wait_ge(sm["pv_free"], U * GB + t0["pv_free"] + (2 * n + 3))
                        pe.wait_ge(sm["o_free"], t0["o_free"] + U * GT + (n + 1))
                        if n == 0:
                            pe.wait_ge(sm["w_free"], 2 + t0["w_hi"] + h * c.nw)
                        for q_ in range(c.nh):
                            mm = product(out_ps[:, :], lambda s: att[0:hd, s, q_ * P:(q_ + 1) * P],
                                         lambda s: wo[0:hd, s, q_ * D:(q_ + 1) * D], q_ == 0, q_ == c.nh - 1)
                        mm.then_inc(sm["o_full"], 1)

                pe_start(t0)
                cross_walk(c, pe, step)

            def self_(t0, c):
                pe_start(t0)
                pe.wait_ge(sm["w_free"], 2 + t0["w_hi"])
                kw = c.kvc * P

                def step(what, n, U, par):
                    if what == "fill":
                        kind, m = c.fills[n]
                        ps = proj_ps[n % 2]
                        pe.wait_ge(sm["proj_free"], t0["proj_free"] + U * c.nf + (n + 1))
                        if n == 0:
                            pe.wait_ge(xg_in[par], 8 * GT * t0["xg"] + (U - par) * (8 * GT) + 16 * GT)
                        if kind in "qk":
                            w = sw["wq" if kind == "q" else "wk"]
                            for j in range(1 if kind == "k" and c.rope else 2):
                                ch = 2 * m + j
                                for k in range(KC):
                                    mm = product(ps[:, j * GT * P:(j + 1) * GT * P], lambda s: w[:, s, k, ch * P:(ch + 1) * P],
                                                 lambda s: xg[:, par, :, s, k, :], k == 0, k == KC - 1)
                        elif kind == "r":
                            wd = GT * P * (1 if m == 2 else 2)
                            pe.wait_ge(sm["proj_hi"], t0["proj_hi"] + U * c.nf + n)
                            mm = pe.matmul(ps[:, 0:wd], perm, raw32[:, 0:wd], start=True, stop=True)
                        else:
                            for k in range(KC):
                                mm = product(ps[:, 0:kw], lambda s: xg[:, par, m, s, k, :], lambda s: sw["wv"][:, s, k, 0:kw],
                                             k == 0, k == KC - 1 and c.rope)
                            if not c.rope:
                                for s in (HI, LO):
                                    mm = pe.matmul(ps[:, :], row0[:, :], sw["bv"][:, s, 0, :], start=False, stop=s == LO,
                                                   skip_group_check=True)
                        mm.then_inc(sm["proj_full"], 1)
                    elif what == "scores":
                        _, tile, bt, c0 = unit(n)
                        pe.wait_ge(sm["shifted"], t0["shifted"] + U * UNITS + n - 1)
                        if n % 4 == 0:
                            pe.wait_ge(sm["qm_ok"], t0["qm_ok"] + U * (GT * QX) + (tile + 1) * QX)
                            pe.wait_ge(sm["qlo_ok"], t0["qlo_ok"] + U * (GT * QX) + (tile + 1) * QX)
                            pe.wait_ge(sm["qlo2_ok"], t0["qlo2_ok"] + U * (GT * QX) + (tile + 1) * QX)
                            pe.wait_ge(sm["proj_free"], 2 + t0["proj_free"] + U * c.nf + c.nf)
                            if c.rope:
                                pe.wait_ge(sm["rope_lo"], t0["rope_lo"] + U * c.nrope + c.nrope)
                        tok = (tile * 2 + bt) * L
                        pe.matmul(score_ps[n % 2][:, :], identb[:, :], maskb[:, :].unsqueeze(1).to_broadcast([P, HPC, L]), start=True, stop=False, skip_group_check=True)
                        for ci in range(2):
                            for t in range(2):
                                for j in range(2):
                                    at = ((ci * 2 + t) * 2 + j) * L
                                    kc = 0 if c.rope else c0 + ci
                                    mm = product(score_ps[n % 2][:, at:at + L],
                                                 lambda s: qm[:, tile, s, c0 + ci, bt, 4 * j + 2 * t:4 * j + 2 * t + 2, :].rearrange("p h t -> p (h t)"),
                                                 lambda s: sk[:, par, s, kc, tok:tok + L], False, True)
                        mm.then_inc(sm["s_full"], 1)
                    elif what == "turn":
                        pe.wait_ge(sm["p_ok"], t0["p_ok"] + U * UNITS + (n + 1))
                        pe.wait_ge(sm["t_free"], t0["t_free"] + U * UNITS + n)
                        for g in range(4):
                            mm = pe.transpose(turn_ps[n % 2][:, g * P:(g + 1) * P],
                                              sc[:, n % SCB, 2 * g:2 * g + 2, :].rearrange("p g k -> p (g k)"), identf[:, :])
                        mm.then_inc(sm["t_full"], 1)
                    elif what == "pv":
                        _, tile, bt, c0 = unit(n)
                        pe.wait_ge(sm["t_free"], 2 + t0["t_free"] + U * UNITS + n)
                        if n % 4 == 0:
                            pe.wait_ge(sm["vx_ok"], t0["vx_ok"] + U * (GT * 2) + (tile + 1) * 2)
                            pe.wait_ge(sm["pv_free"], t0["pv_free"] + U * GT + (tile + 1))
                        for ci in range(2):
                            at = (c0 + ci) * P + bt * L
                            for th in range(4):
                                kc = 0 if c.rope else c0 + ci
                                col = (ci * 4 + th) * L
                                mm = product(pv_ps[:, at:at + L], lambda s: vx[:, tile, s, bt, kc, th, :],
                                             lambda s: spT[:, n % 2, s, col:col + L], th == 0, th == 3)
                        if n % 4 == 3:
                            mm.then_inc(sm["pv_full"], 1)
                    elif what == "out":
                        pe.wait_ge(sm["pv_free"], 1 + t0["pv_free"] + U * GT + (n + 1))
                        pe.wait_ge(sm["o_free"], t0["o_free"] + U * GT + (n + 1))
                        for k in range(KC):
                            mm = product(out_ps[:, :], lambda s: satt[:, s, k, :], lambda s: sw["wo"][:, s, k, :],
                                         k == 0, k == KC - 1 and c.rope)
                        if not c.rope:
                            for s in (HI, LO):
                                mm = pe.matmul(out_ps[:, :], row0[:, :], sw["bo"][:, s, 0, :], start=False, stop=s == LO,
                                               skip_group_check=True)
                        mm.then_inc(sm["o_full"], 1)
                walk(pe, self_first(c), self_order, c, step)

            def ffn0(t0, c):
                pe_start(t0)
                pe.wait_ge(sm["w_free"], 2 + t0["w_hi"])

                def step(what, n, U, par):
                    if what == "fill":
                        kind, m = c.fills[n]
                        ps = proj_ps[n % 2]
                        pe.wait_ge(sm["proj_free"], t0["proj_free"] + U * c.nf + (n + 1))
                        if n == 0:
                            pe.wait_ge(xg_in[par], 8 * GT * t0["xg"] + (U - par) * (8 * GT) + 16 * GT)
                        if kind in "uf":
                            w = fw["up" if kind == "u" else "fc1"]
                            for j in range(2):
                                ch = 2 * m + j
                                for k in range(KC):
                                    mm = product(ps[:, j * GT * P:(j + 1) * GT * P], lambda s: w[:, s, k, ch * P:(ch + 1) * P],
                                                 lambda s: xg[:, par, :, s, k, :], k == 0, k == KC - 1)
                        elif kind == "e":
                            pe.wait_ge(sm["proj_free"], 2 + t0["proj_free"] + U * c.nf + 1)
                            for j in range(2):
                                for k in range(2):
                                    mm = product(ps[:, j * GT * P:(j + 1) * GT * P],
                                                 lambda s: fw["expert"][:, s, k, j * P:(j + 1) * P],
                                                 lambda s: fT[:, s, k, :], k == 0, k == 1)
                        else:
                            for k in range(KC):
                                mm = product(ps[:, 0:8], lambda s: xg[:, par, m, s, k, :], lambda s: fw["gate"][:, s, k, :],
                                             k == 0, k == KC - 1)
                        mm.then_inc(sm["proj_full"], 1)
                    elif what == "down":
                        N = U * GT + n
                        pe.wait_ge(sm["h_ok"], t0["h_ok"] + U * 4 + 4)
                        pe.wait_ge(sm["proj_free"], 2 + t0["proj_free"] + U * c.nf + 6)
                        pe.wait_ge(sm["sh_ok"], t0["sh_ok"] + N)
                        for k in range(8):
                            mm = product(out_ps[:, :], lambda s: hT[:, par, s, k, n * P:(n + 1) * P],
                                         lambda s: fw["down"][:, s, k, :], k == 0, k == 7)
                        mm.then_inc(sm["o_full"], 1)
                        pe.wait_ge(sm["pv_free"], t0["pv_free"] + N + 1)
                        for k in range(2):
                            mm = product(pv_ps[:, :], lambda s: eT[:, par, s, k, n * P:(n + 1) * P],
                                         lambda s: fw["fc2"][:, s, k, :], k == 0, k == 1)
                        mm.then_inc(sm["pv_full"], 1)
                walk(pe, ffn_first(c), ffn_order, c, step)

            def ffn1(t0):
                pe_start(t0)
                pe.wait_ge(sm["proj_free"], 2 + t0["proj_free"])
                pe.wait_ge(sm["wsum"], 1)
                pe.wait_ge(sm["zero_ok"], t0["zero_ok"] + 1)
                pe.matmul(out_ps[:, 0:1], ones, wabs, start=True, stop=True).then_inc(sm["wsum_ps"], 1)
                pe.wait_ge(sm["wt_ok"], 1)

                def turn(i, t):
                    if t < 2:
                        pe.wait_ge(sm["q_evac"], START + i * PREP_T)
                    else:
                        pe.wait_ge(sm["q_evac"], START + i * PREP_T + (t - 1))
                    for k in range(KC):
                        mm = pe.transpose(bank[t % 2][:, k * P // 2:(k + 1) * P // 2].bitcast(BF16), xq[:, i % 2, t, k * P:(k + 1) * P], identb[:, :])
                    mm.then_inc(sm["q_turn"], 1)

                for i in range(QUADS):
                    pe.wait_ge(sm["xq_ok"], START + i + 1)
                    turn(i, 0)
                    for t in range(PREP_T):
                        if t + 1 < PREP_T:
                            turn(i, t + 1)
                        pe.wait_ge(sm["q_evac"], START + i * PREP_T + (t + 1))
                        pe.wait_ge(sm["y_free"], START + i * PREP_T + max(t - 1, 0))
                        for k in range(KC):
                            mm = pe.matmul((pv_ps, out_ps)[t % 2][:, :], xqT[:, t % 2, k, :], tw[:, k, :], start=k == 0, stop=k == KC - 1)
                        mm.then_inc(sm["y_full"], 1)

            for kind, t0, c in plan:
                if kind == "prep":
                    prep(t0, c)
                elif kind == "ffn1":
                    ffn1(t0)
                else:
                    {"cross": cross, "self": self_, "ffn0": ffn0}[kind](t0, c)


def _consts():
    p = np.arange(P)
    hmask = (p[:, None] // HD == np.arange(HPC)[None, :]).astype(np.float32)
    cmask = np.where(np.arange(L)[None, :] <= (p[:, None] % L), 0.0, -1e30).astype(np.float32)
    swap = (p // HD) * HD + (p % HD + HD // 2) % HD
    perm = np.zeros((P, P), np.float32)
    perm[swap, p] = 1.0
    f32 = np.float32
    theta, factor, hi_f, lo_f, l0 = 500000.0, 32.0, 4.0, 1.0, 1024
    idx = np.arange(0, HD, 2, dtype=f32) / f32(HD)
    freq = (f32(1.0 / (2.0 * np.pi)) * np.power(f32(theta), -idx)).astype(f32)
    low, high = lo_f / l0, hi_f / l0
    scaled = np.where(freq < low, freq / f32(factor), freq)
    smooth = np.clip((l0 * freq - lo_f) / (hi_f - lo_f), 0.0, 1.0).astype(f32)
    mixed = (1 - smooth) * (freq / f32(factor)) + smooth * freq
    freq = np.where((freq >= low) & (freq <= high), mixed, scaled).astype(f32)
    phase = (f32(2.0 * np.pi) * np.arange(L, dtype=f32)[None, :] * freq[p % (HD // 2)][:, None]).astype(f32)
    sign = np.where(p % HD < HD // 2, -1.0, 1.0)[:, None]
    return np.concatenate([hmask, cmask, perm, np.cos(phase), np.sin(phase) * sign], axis=1).astype(f32)


def _layout(inputs):
    def f(n):
        return np.asarray(inputs[n])
    arr = {
        "x": f("x").reshape(B * L, D),
        "ctxT": f("ctx_4096").reshape(B * S, D).T,
        "L0_xattn_Wq": f("L0_xattn_Wq").T, "L0_xattn_Wk": f("L0_xattn_Wk").T,
        "L0_xattn_Wv": f("L0_xattn_Wv").T, "L0_xattn_Wo": f("L0_xattn_Wo").T,
        "L1_xattn_Wq": f("L1_xattn_Wq"), "L1_xattn_Wk": f("L1_xattn_Wk"),
        "L1_xattn_Wv": f("L1_xattn_Wv"), "L1_xattn_Wo": f("L1_xattn_Wo"),
        "L1_ffn_W": f("L1_ffn_W").T, "L1_ffn_b": f("L1_ffn_b"), "consts": _consts(),
    }
    for n in ("Wq", "Wk", "Wv", "Wo"):
        arr["L0_attn_" + n] = f("L0_attn_" + n).T
    for n in ("bv", "bo"):
        arr["L0_attn_" + n] = f("L0_attn_" + n)
    arr["L0_attn_bqk"] = np.stack([f("L0_attn_bq").reshape(KC, P).T, f("L0_attn_bk").reshape(KC, P).T], axis=1)
    for n in ("gate_w", "up_w", "down_w", "fc1_w", "fc2_w", "expert_w", "ln_gamma", "ln_beta"):
        arr["L0_ffn_" + n] = f("L0_ffn_" + n)
    arr["L1_attn_Wq"] = f("L1_attn_Wq").reshape(D, 8, 4, HD).transpose(0, 2, 1, 3).reshape(D, D)
    arr["L1_attn_Wo"] = f("L1_attn_Wo").reshape(8, 4, HD, D).transpose(1, 0, 2, 3).reshape(D, D)
    arr["L1_attn_Wk"], arr["L1_attn_Wv"] = f("L1_attn_Wk"), f("L1_attn_Wv")
    return {k: np.ascontiguousarray(v) for k, v in arr.items()}


def kernel(**inputs):
    import concourse.bacc as _bacc
    from concourse.bass_utils import run_bass_kernel_spmd as _run

    nc = _bacc.Bacc("TRN2", target_bir_lowering=False, num_devices=1)
    arr = _layout(inputs)
    aps = {k: nc.dram_tensor(f"in_{k}", v.shape, mybir.dt.from_np(v.dtype), kind="ExternalInput").ap()
           for k, v in arr.items()}
    out = nc.dram_tensor("out_x", (B * L, D), F32, kind="ExternalOutput").ap()
    build(nc, aps, out)
    r = _run(nc, [{f"in_{k}": v for k, v in arr.items()}], core_ids=[0])
    return r.results[0]["out_x"].reshape(B, L, D)
```
